# Optimizing a Trainium2 kernel written in Bass

```python
import numpy as np
import jax
import jax.numpy as jnp

def _softmax(x, axis=-1):
    return jax.nn.softmax(x, axis=axis)

def _gelu(x):
    return jax.nn.gelu(x, approximate=True)

def _silu(x):
    return jax.nn.silu(x)

def _sigmoid(x):
    return jax.nn.sigmoid(x)

def _layernorm(x, axis=-1, eps=1e-05):
    m = jnp.mean(x, axis=axis, keepdims=True)
    v = jnp.var(x, axis=axis, keepdims=True)
    return (x - m) / jnp.sqrt(v + eps)

def _scatter_add(tgt, idx, src, axis=0):
    return tgt.at[idx].add(src)

def _segment_sum(src, seg, n):
    return jax.ops.segment_sum(src, seg, n)
kernel_name = 'mk_flamingo_gated_d2_seqx_r4_019133'

def setup_inputs(seed: int=0):
    np.random.seed(seed)
    _w = jnp.asarray

    def _rec_inputs():
        import jax
        import jax.numpy as jnp
        _rk = jax.random.key(seed)
        x = 2.818e-05 + 1 * jax.random.normal(jax.random.fold_in(_rk, 1), (4, 512, 512), jnp.float32)
        _lenS = 512 - jax.random.randint(jax.random.fold_in(_rk, 7), (4,), 0, max(1, 512 // 4) + 1, jnp.int32)
        _lenS2 = 512 - jax.random.randint(jax.random.fold_in(_rk, 8), (4,), 0, max(1, 512 // 4) + 1, jnp.int32)
        _ctx_1024P = jax.random.normal(jax.random.fold_in(_rk, 11), (4, 16, 256), jnp.float32)
        _ctx_1024c = jax.random.dirichlet(jax.random.fold_in(_rk, 511), 0.3 * jnp.ones((16,), jnp.float32), (4, 512))
        _ctx_1024t = jnp.einsum('bsk,bkd->bsd', _ctx_1024c, _ctx_1024P)
        _ctx_1024t = _ctx_1024t * jax.lax.rsqrt(jnp.mean(jnp.square(_ctx_1024t)) + 1e-12) * 0.953939
        ctx_1024 = 7.22013e-05 + 1.00017 * (_ctx_1024t + 0.3 * jax.random.normal(jax.random.fold_in(_rk, 611), (4, 512, 256), jnp.float32))
        _g = jax.random.normal(jax.random.fold_in(_rk, 9001), (2, 2), jnp.float32)
        _g = jnp.sign(_g) * jnp.maximum(jnp.abs(_g), 1.0) + (_g == 0) * 1.0
        g_xattn = _g[0]
        g_ffn = _g[1]
        return (x, ctx_1024, g_xattn, g_ffn)
    x, ctx_1024, g_xattn, g_ffn = _rec_inputs()

    def _L0_xattn_setup():
        import jax, jax.numpy as jnp
        import numpy as np
        B_, L_, D_MODEL = (4, 512, 256)
        D_STATE, D_CONV, EXPAND = (16, 4, 2)
        D_INNER = EXPAND * D_MODEL
        DT_RANK = (D_MODEL + 15) // 16

        def silu(x):
            return x * jax.nn.sigmoid(x)
        key = jax.random.key(seed)
        ks = jax.random.split(key, 10)
        f32 = jnp.float32
        hidden_states = jax.random.normal(ks[0], (B_, L_, D_MODEL), dtype=f32)
        z = jax.random.normal(ks[1], (B_, D_INNER, L_), dtype=f32)
        in_proj_w = jax.random.normal(ks[2], (D_INNER, D_MODEL), dtype=f32) * 0.02
        conv_w = jax.random.normal(ks[3], (D_INNER, 1, D_CONV), dtype=f32) * 0.1
        conv_b = jax.random.normal(ks[4], (D_INNER,), dtype=f32) * 0.02
        x_proj_w = jax.random.normal(ks[5], (DT_RANK + 2 * D_STATE, D_INNER), dtype=f32) * 0.02
        dt_proj_w = jax.random.uniform(ks[6], (D_INNER, DT_RANK), dtype=f32, minval=-DT_RANK ** (-0.5), maxval=DT_RANK ** (-0.5))
        dt = jnp.exp(jax.random.uniform(ks[7], (D_INNER,), dtype=f32, minval=np.log(0.001), maxval=np.log(0.1)))
        dt_proj_b = jnp.log(jnp.expm1(dt))
        A_log = jnp.log(jnp.broadcast_to(jnp.arange(1, D_STATE + 1, dtype=f32), (D_INNER, D_STATE)))
        D = jnp.ones((D_INNER,), f32)
        return {'hidden_states': hidden_states, 'z': z, 'in_proj_w': in_proj_w, 'conv_w': conv_w, 'conv_b': conv_b, 'x_proj_w': x_proj_w, 'dt_proj_w': dt_proj_w, 'dt_proj_b': dt_proj_b, 'A_log': A_log, 'D': D}
    _L0_xattn_all = _L0_xattn_setup()
    _L0_xattn_in = {k: v for k, v in _L0_xattn_all.items() if k in ('in_proj_w', 'conv_w', 'conv_b', 'x_proj_w', 'dt_proj_w', 'dt_proj_b', 'A_log', 'D')}
    del _L0_xattn_all

    def _L0_ffn_setup():
        import jax, jax.numpy as jnp
        import numpy as np
        EPS = 1e-05

        def _bitlinear(x, w):
            rms = jax.lax.rsqrt(jnp.maximum(jnp.mean(w * w), EPS))
            w_quant = jnp.clip(jnp.round(w * rms), -1.0, 1.0) / rms
            w_quant = jax.lax.stop_gradient(w_quant - w) + w
            scale = 127.0 / jnp.maximum(jnp.max(jnp.abs(x), axis=-1, keepdims=True), EPS)
            x_quant = jnp.clip(jnp.round(x * scale), -128.0, 127.0) / scale
            x_quant = jax.lax.stop_gradient(x_quant - x) + x
            return jnp.einsum('bsd,fd->bsf', x_quant, w_quant)
        key = jax.random.key(seed)
        k1, k2, k3 = jax.random.split(key, 3)
        n_embd, d_ff = (512, 2048)
        B, S = (4, 512)
        x = jax.random.normal(k1, (B, S, n_embd), dtype=jnp.float32)
        w1 = jax.random.normal(k2, (d_ff, n_embd), dtype=jnp.float32) * 0.02
        w2 = jax.random.normal(k3, (n_embd, d_ff), dtype=jnp.float32) * 0.02
        return {'x': x, 'w1': w1, 'w2': w2}
    _L0_ffn_all = _L0_ffn_setup()
    _L0_ffn_in = {k: v for k, v in _L0_ffn_all.items() if k in ('w1', 'w2')}
    del _L0_ffn_all

    def _L1_xattn_setup():
        import jax, jax.numpy as jnp
        import numpy as np
        key = jax.random.key(seed)
        ks = jax.random.split(key, 6)
        B, L, N, C, D = (8, 128, 512, 256, 128)
        return {'teacher_logits': jax.random.normal(ks[0], (B, L, N), dtype=jnp.float32), 'teacher_features': jax.random.normal(ks[1], (B, N, C), dtype=jnp.float32), 'Wq': jax.random.normal(ks[2], (D, C), dtype=jnp.float32) * (1.0 / np.sqrt(C)), 'bq': jnp.zeros((D,), dtype=jnp.float32), 'Wk': jax.random.normal(ks[3], (D, C), dtype=jnp.float32) * (1.0 / np.sqrt(C)), 'bk': jnp.zeros((D,), dtype=jnp.float32)}
    _L1_xattn_all = _L1_xattn_setup()
    _L1_xattn_in = {k: v for k, v in _L1_xattn_all.items() if k in ('Wq', 'bq', 'Wk', 'bk')}
    del _L1_xattn_all

    def _L1_ffn_setup():
        import jax, jax.numpy as jnp
        import numpy as np
        L, N, E, H, K = (512, 8, 512, 2048, 8)
        key = jax.random.key(seed)
        ks = jax.random.split(key, 6)
        return {'x': jax.random.normal(ks[0], (L, N, E), dtype=jnp.float32), 'proj1': jax.random.normal(ks[1], (H, E), dtype=jnp.float32) * 0.02, 'proj1_bias': jax.random.normal(ks[2], (H,), dtype=jnp.float32) * 0.02, 'proj2': jax.random.normal(ks[3], (E, H), dtype=jnp.float32) * 0.02, 'proj2_bias': jax.random.normal(ks[4], (E,), dtype=jnp.float32) * 0.02, 'gate_w': jax.random.normal(ks[5], (E, K), dtype=jnp.float32)}
    _L1_ffn_all = _L1_ffn_setup()
    _L1_ffn_in = {k: v for k, v in _L1_ffn_all.items() if k in ('proj1', 'proj1_bias', 'proj2', 'proj2_bias', 'gate_w')}
    del _L1_ffn_all
    return {'x': x, 'ctx_1024': ctx_1024, 'g_xattn': g_xattn, 'g_ffn': g_ffn, 'L0_xattn_in_proj_w': _L0_xattn_in['in_proj_w'], 'L0_xattn_conv_w': _L0_xattn_in['conv_w'], 'L0_xattn_conv_b': _L0_xattn_in['conv_b'], 'L0_xattn_x_proj_w': _L0_xattn_in['x_proj_w'], 'L0_xattn_dt_proj_w': _L0_xattn_in['dt_proj_w'], 'L0_xattn_dt_proj_b': _L0_xattn_in['dt_proj_b'], 'L0_xattn_A_log': _L0_xattn_in['A_log'], 'L0_xattn_D': _L0_xattn_in['D'], 'L0_ffn_w1': _L0_ffn_in['w1'], 'L0_ffn_w2': _L0_ffn_in['w2'], 'L1_xattn_Wq': _L1_xattn_in['Wq'], 'L1_xattn_bq': _L1_xattn_in['bq'], 'L1_xattn_Wk': _L1_xattn_in['Wk'], 'L1_xattn_bk': _L1_xattn_in['bk'], 'L1_ffn_proj1': _L1_ffn_in['proj1'], 'L1_ffn_proj1_bias': _L1_ffn_in['proj1_bias'], 'L1_ffn_proj2': _L1_ffn_in['proj2'], 'L1_ffn_proj2_bias': _L1_ffn_in['proj2_bias'], 'L1_ffn_gate_w': _L1_ffn_in['gate_w']}

def reference(x, ctx_1024, g_xattn, g_ffn, L0_xattn_in_proj_w, L0_xattn_conv_w, L0_xattn_conv_b, L0_xattn_x_proj_w, L0_xattn_dt_proj_w, L0_xattn_dt_proj_b, L0_xattn_A_log, L0_xattn_D, L0_ffn_w1, L0_ffn_w2, L1_xattn_Wq, L1_xattn_bq, L1_xattn_Wk, L1_xattn_bk, L1_ffn_proj1, L1_ffn_proj1_bias, L1_ffn_proj2, L1_ffn_proj2_bias, L1_ffn_gate_w):
    import jax
    import jax.numpy as jnp

    def _L0_xattn_ref(hidden_states, z, in_proj_w, conv_w, conv_b, x_proj_w, dt_proj_w, dt_proj_b, A_log, D):
        import jax, jax.numpy as jnp
        import numpy as np
        B_, L_, D_MODEL = (4, 512, 256)
        D_STATE, D_CONV, EXPAND = (16, 4, 2)
        D_INNER = EXPAND * D_MODEL
        DT_RANK = (D_MODEL + 15) // 16

        def silu(x):
            return x * jax.nn.sigmoid(x)
        Bsz, L, _ = hidden_states.shape
        d_inner, _, d_conv = conv_w.shape
        dt_rank = dt_proj_w.shape[1]
        d_state = A_log.shape[1]
        x = jnp.einsum('bld,ed->bel', hidden_states, in_proj_w)
        xc = jax.lax.conv_general_dilated(x, conv_w, window_strides=(1,), padding=[(d_conv - 1, 0)], feature_group_count=d_inner, dimension_numbers=('NCH', 'OIH', 'NCH'))
        x = silu(xc + conv_b[None, :, None])
        x_dbl = jnp.einsum('bdl,ed->bel', x, x_proj_w)
        dt_low, Bm, Cm = jnp.split(x_dbl, [dt_rank, dt_rank + d_state], axis=1)
        dt = jnp.einsum('brl,dr->bdl', dt_low, dt_proj_w)
        dt = jax.nn.softplus(dt + dt_proj_b[None, :, None])
        A = -jnp.exp(A_log)
        dt_t = jnp.moveaxis(dt, -1, 0)
        B_t = jnp.moveaxis(Bm, -1, 0)
        C_t = jnp.moveaxis(Cm, -1, 0)
        u_t = jnp.moveaxis(x, -1, 0)

        def step(state, inp):
            d, b, c, u = inp
            dA = jnp.exp(d[..., None] * A)
            state = state * dA + (d * u)[..., None] * b[:, None, :]
            y = jnp.einsum('bdn,bn->bd', state, c)
            return (state, y)
        state0 = jnp.zeros((Bsz, d_inner, d_state), x.dtype)
        _, ys = jax.lax.scan(step, state0, (dt_t, B_t, C_t, u_t))
        y = jnp.moveaxis(ys, 0, 2)
        y = y + D[None, :, None] * x
        y = y * silu(z)
        return jnp.swapaxes(y, 1, 2)

    def _L0_ffn_ref(x, w1, w2):
        import jax, jax.numpy as jnp
        import numpy as np
        EPS = 1e-05

        def _bitlinear(x, w):
            rms = jax.lax.rsqrt(jnp.maximum(jnp.mean(w * w), EPS))
            w_quant = jnp.clip(jnp.round(w * rms), -1.0, 1.0) / rms
            w_quant = jax.lax.stop_gradient(w_quant - w) + w
            scale = 127.0 / jnp.maximum(jnp.max(jnp.abs(x), axis=-1, keepdims=True), EPS)
            x_quant = jnp.clip(jnp.round(x * scale), -128.0, 127.0) / scale
            x_quant = jax.lax.stop_gradient(x_quant - x) + x
            return jnp.einsum('bsd,fd->bsf', x_quant, w_quant)
        h = _bitlinear(x, w1)
        h = jax.nn.gelu(h, approximate=False)
        out = _bitlinear(h, w2)
        return out

    def _L1_xattn_ref(teacher_logits, teacher_features, Wq, bq, Wk, bk):
        import jax, jax.numpy as jnp
        import numpy as np
        query = jnp.einsum('bnc,dc->bnd', teacher_features, Wq) + bq
        key = jnp.einsum('bnc,dc->bnd', teacher_features, Wk) + bk
        energy = jnp.einsum('bnd,bmd->bnm', query, key)
        attention = jax.nn.softmax(energy, axis=-1)
        x_m = jnp.einsum('bln,bmn->blm', teacher_logits, attention)
        return x_m

    def _L1_ffn_ref(x, proj1, proj1_bias, proj2, proj2_bias, gate_w):
        import jax, jax.numpy as jnp
        import numpy as np
        L, N, E, H, K = (512, 8, 512, 2048, 8)
        dst = jnp.argmax(jnp.einsum('lne,ek->lnk', x, gate_w), axis=-1)
        h = jax.nn.gelu(jnp.einsum('lne,he->lnh', x, proj1) + proj1_bias, approximate=False)
        out = jnp.einsum('lnh,eh->lne', h, proj2) + proj2_bias
        del dst
        return out
    x = x + jnp.tanh(g_xattn[0]) * _L0_xattn_ref(ctx_1024, _layernorm(x, axis=-1), L0_xattn_in_proj_w, L0_xattn_conv_w, L0_xattn_conv_b, L0_xattn_x_proj_w, L0_xattn_dt_proj_w, L0_xattn_dt_proj_b, L0_xattn_A_log, L0_xattn_D)
    x = x + jnp.tanh(g_ffn[0]) * _L0_ffn_ref(_layernorm(x, axis=-1), L0_ffn_w1, L0_ffn_w2)
    x = x + jnp.tanh(g_xattn[1]) * _L1_xattn_ref(_layernorm(x, axis=-1), ctx_1024, L1_xattn_Wq, L1_xattn_bq, L1_xattn_Wk, L1_xattn_bk)
    x = x + jnp.tanh(g_ffn[1]) * _L1_ffn_ref(_layernorm(x, axis=-1), L1_ffn_proj1, L1_ffn_proj1_bias, L1_ffn_proj2, L1_ffn_proj2_bias, L1_ffn_gate_w)
    return x

_drawn_inputs = setup_inputs


def setup_inputs(seed=0):
    import zlib

    import numpy as np

    out = dict(_drawn_inputs(seed))
    spreads = {'g_ffn': (-1.0, 0.6),
     'L0_xattn_D': (1.0, 0.6),
     'L1_xattn_bq': (0.0, 0.1),
     'L1_xattn_bk': (0.0, 0.8)}
    factors = {'L0_xattn_in_proj_w': 3.761,
     'L0_xattn_conv_w': 3.779,
     'L0_xattn_conv_b': 8.0,
     'L0_xattn_x_proj_w': 8.0,
     'L0_xattn_dt_proj_w': 8.0,
     'L0_xattn_dt_proj_b': 8.0,
     'L0_xattn_A_log': 8.0,
     'L1_ffn_proj1_bias': 7.964,
     'L1_ffn_proj2_bias': 4.48}
    for name, (base, spread) in spreads.items():
        noise = np.random.default_rng([zlib.crc32(name.encode()), seed]).standard_normal(out[name].shape)
        drawn = base * np.exp(spread * noise) if base else spread * noise
        out[name] = jnp.asarray(drawn.astype(out[name].dtype))
    for name, factor in factors.items():
        out[name] = (out[name] * factor).astype(out[name].dtype)
    return out
```

```python
from contextlib import ExitStack

import numpy as np

import concourse.bass as bass
from concourse import mybir

F32 = mybir.dt.float32
BF16 = mybir.dt.bfloat16
ALU = mybir.AluOpType
ACT = mybir.ActivationFunctionType
AX = mybir.AxisListType

P = 128
B = 4
L = 512
D = 512
C = 256
FF = 2048
NS = 16
R = 16
TAPS = 4
T = L // P
J = D // P
KC = C // P
FT = FF // P
FC = FF // 512
HALF = 2
W = HALF * L
HN = NS * (J // HALF)
SCANBUFS = 3
RING = 4
PAD = TAPS - 1
LN_EPS = 1e-5
Q_EPS = 1e-5
MAGIC = 1.5 * 2.0 ** 23
SLOTS = 15

PC_CONVW, PC_CONVB, PC_DTB, PC_D, PC_ALOG = 0, TAPS, TAPS + 1, TAPS + 2, TAPS + 3
PC_N = TAPS + 3 + NS

SCAN_SLOTS = {4: (0,), 5: (1,), 6: (2, 3), 7: (4, 5), 8: (6, 7), 9: (8, 9), 10: (10, 11), 11: (12, 13), 12: (14, 15)}
ATT_SLOTS = {7: 0, 8: 1, 9: 2, 10: 3}
FFN_SLOTS = {6 + i: (2 * i, 2 * i + 1) for i in range(FT // 2)}


class Tally:

    def __init__(self, sem, per):
        self.sem, self.per, self.n = sem, per, 0

    def start(self):
        assert self.n in (0, self.per), (self.n, self.per)
        self.n = 0

    def link(self, eng, b, ins):
        self.n += 1
        ins.then_inc(self.sem, 1)
        eng.wait_ge(self.sem, b * self.per + self.n)


def program(nc, x_d, ctxT_d, ipw_d, xpw_d, dtw_d, pch_d, w1_d, w2_d, wqk_d, bqk_d, ffn_d, b1_d, b2_d, gate_d,
            ident_d, identb_d, pick_d, out_d):
    with ExitStack() as ctx:
        def sb(name, shape, dt=F32):
            return ctx.enter_context(nc.sbuf_tensor(name, shape, dt))

        def sem(name):
            return ctx.enter_context(nc.semaphore(name))

        banks = [ctx.enter_context(nc.psum_tensor(f"bank{i}", [P, 512], F32)) for i in range(8)]

        ident = sb("ident", [P, P])
        identb = sb("identb", [P, P], BF16)
        pick = sb("pick", [P, 2 * NS], BF16)
        ones = sb("ones", [P, P])
        expo = sb("expo", [P, 2])
        ipw = sb("ipw", [P, KC, D])
        xpw = sb("xpw", [P, J, P])
        dtw = sb("dtw", [R, D])
        pch = sb("pch", [P, J, PC_N])
        a_neg = sb("a_neg", [P, J, NS])
        wqk = sb("wqk", [P, KC, 2, P])
        bqk = sb("bqk", [P, 2])
        b1 = sb("b1", [P, FT])
        b2 = sb("b2", [P, D])
        gates = sb("gates", [P, 4])
        w1q = sb("w1q", [P, J, FF], BF16)
        w2q = sb("w2q", [P, FT, D], BF16)
        wsum = sb("wsum", [P, 2])
        wstat = sb("wstat", [P, 2, 4])
        ring = sb("ring", [P, RING, 2 * D])

        ctxT = sb("ctxT", [P, KC, L])
        xres = sb("xres", [P, T, D])
        xpad = sb("xpad", [P, 2, PAD + L])
        u = sb("u", [P, J, L])
        dt = sb("dt", [P, J, L])
        du = sb("du", [P, J, L])
        decay = sb("decay", [P, 2, HALF, L])
        work = sb("work", [P, SCANBUFS, HALF, L])
        bcast = sb("bcast", [P, 2, L])
        ccast = sb("ccast", [P, 2, L])
        xd = sb("xd", [P, L])
        xd3 = sb("xd3", [P, L], BF16)
        zs = sb("zs", [P, 2, L])
        attT = sb("attT", [P, J, D])
        qk = sb("qk", [P, 2, D])
        ex = sb("ex", [P, D])
        qT = sb("qT", [P, J, L], BF16)
        zst = sb("zst", [P, J, 12])
        x1n = sb("x1n", [P, D])
        q1 = sb("q1", [P, D], BF16)
        mst = sb("mst", [P, T, 16])
        ast = sb("ast", [P, J, 4])

        stage = sb("stage", [P, 4 * FF])
        h = [stage[:, i * FF:(i + 1) * FF] for i in range(2)]
        xb = stage[:, 2 * FF:3 * FF].rearrange("p (t d) -> p t d", t=T)
        xnT = stage[:, 3 * FF:4 * FF].rearrange("p (k l) -> p k l", k=J)
        hq = sb("hq", [P, FF], BF16)
        hqT = sb("hqT", [P, FT, P], BF16)
        xn = sb("xn", [P, 2, D])
        hT = sb("hT", [P, 2, L])
        fst = sb("fst", [P, T, 24])

        bf_bank = [banks[i][:, :].bitcast(BF16) for i in range(8)]

        s_const = sem("s_const")
        s_stage = sem("s_stage")
        s_ctx = sem("s_ctx")
        s_x = sem("s_x")
        s_ring = [sem(f"s_ring{i}") for i in range(RING)]
        s_out = sem("s_out")
        s_stored = sem("s_stored")
        s_ones = sem("s_ones")
        s_aneg = sem("s_aneg")
        s_gates = sem("s_gates")
        s_b2 = sem("s_b2")
        s_wsq = sem("s_wsq")
        s_wmean = sem("s_wmean")
        s_wms = sem("s_wms")
        s_wstat = sem("s_wstat")
        s_wscaled = sem("s_wscaled")
        s_wq = sem("s_wq")
        s_pad = sem("s_pad")
        s_inproj = sem("s_inproj")
        s_inprojc = sem("s_inprojc")
        s_conv = sem("s_conv")
        s_u = sem("s_u")
        s_xdbl = sem("s_xdbl")
        s_xd = sem("s_xd")
        s_split = sem("s_split")
        s_dtmm = sem("s_dtmm")
        s_spabs = sem("s_spabs")
        s_spmax = sem("s_spmax")
        s_spexp = sem("s_spexp")
        s_spln = sem("s_spln")
        s_dt = sem("s_dt")
        s_du = sem("s_du")
        s_accin = sem("s_accin")
        s_bc = sem("s_bc")
        s_bcc = sem("s_bcc")
        s_decay = sem("s_decay")
        s_dbu = sem("s_dbu")
        s_scan = sem("s_scan")
        s_hc = sem("s_hc")
        s_acc = sem("s_acc")
        s_qkmm = sem("s_qkmm")
        s_qk = sem("s_qk")
        s_emm = sem("s_emm")
        s_emax = sem("s_emax")
        s_eexp = sem("s_eexp")
        s_eprob = sem("s_eprob")
        s_eT = sem("s_eT")
        s_att = sem("s_att")
        s_zst = sem("s_zst")
        s_zrs = sem("s_zrs")
        s_zs = sem("s_zs")
        s_y = sem("s_y")
        s_yT = sem("s_yT")
        s_x1 = sem("s_x1")
        s_x1st = sem("s_x1st")
        s_x1rs = sem("s_x1rs")
        s_q1 = sem("s_q1")
        s_q1T = sem("s_q1T")
        s_qT = sem("s_qT")
        s_mm1 = sem("s_mm1")
        s_gelu = sem("s_gelu")
        s_hsc = sem("s_hsc")
        s_hr = sem("s_hr")
        s_hq = sem("s_hq")
        s_hqT = sem("s_hqT")
        s_ev0 = sem("s_ev0")
        s_ev1 = sem("s_ev1")
        s_mm2 = sem("s_mm2")
        s_x2 = sem("s_x2")
        s_lnst = sem("s_lnst")
        s_lnrs = sem("s_lnrs")
        s_xn = sem("s_xn")
        s_xnT = sem("s_xnT")
        s_xnTc = sem("s_xnTc")
        s_xm = sem("s_xm")
        s_x3 = sem("s_x3")
        s_x3b = sem("s_x3b")
        s_fmm1 = sem("s_fmm1")
        s_fgelu = sem("s_fgelu")
        s_fmm2 = sem("s_fmm2")
        s_x4 = sem("s_x4")
        dve_m = Tally(sem("dve_m"), 3 * J + 4 + J + J + 8 * T)
        dve_f = Tally(sem("dve_f"), 6 * T)
        pool_s = Tally(sem("pool_s"), 0)
        pool_m = Tally(sem("pool_m"), 5 * J + T)
        pool_f = Tally(sem("pool_f"), 2 * T)
        dve_w = Tally(sem("dve_w"), 0)

        consts = (
            (ipw[:], ipw_d.rearrange("(k p) e -> p k e", p=P)),
            (pch[:], pch_d.rearrange("(j p) c -> p j c", p=P)),
            (xpw[:], xpw_d.rearrange("(k p) e -> p k e", p=P)),
            (gates[:], gate_d), (dtw[:], dtw_d), (pick[:], pick_d), (ident[:], ident_d), (identb[:], identb_d),
            (bqk[:], bqk_d), (b1[:], b1_d), (b2[:], b2_d),
            (wqk[:, :, 0, :], wqk_d[0].rearrange("(k p) e -> p k e", p=P)),
            (wqk[:, :, 1, :], wqk_d[1].rearrange("(k p) e -> p k e", p=P)),
        )
        const_wait = len(consts) * 16

        carried = {e: sem(f"s_carried_{e}") for e in ("dve", "pool")}

        def carry_wait(eng, name):
            eng.sem_inc(carried[name], 1)

        block = ctx.enter_context(nc.Block())

        @block.sync
        def _(sp):
            def load_ring(slot, f):
                sp.dma_start(ring[:, slot, :], ffn_d[f]).then_inc(s_ring[slot], 16)

            sp.dma_start(ctxT[:], ctxT_d[0].rearrange("(k p) l -> p k l", p=P)).then_inc(s_ctx, 16)
            for dst, src in consts:
                sp.dma_start(dst, src).then_inc(s_const, 16)
            sp.dma_start(xres[:], x_d[0].rearrange("(t p) d -> p t d", p=P)).then_inc(s_x, 16)
            sp.dma_start(stage[:].rearrange("p (k f) -> p k f", k=J),
                         w1_d.rearrange("(k p) f -> p k f", p=P)).then_inc(s_stage, 16)
            for f in range(RING):
                load_ring(f, f)
            sp.wait_ge(s_wq, 4)
            sp.dma_start(stage[:].rearrange("p (k f) -> p k f", k=FT),
                         w2_d.rearrange("(k p) f -> p k f", p=P)).then_inc(s_stage, 16)

            def batch(b, more):
                if more:
                    sp.wait_ge(s_qkmm, b * 2 + 2)
                    sp.wait_ge(s_inproj, b * J + J)
                    sp.dma_start(ctxT[:], ctxT_d[b + 1].rearrange("(k p) l -> p k l", p=P)).then_inc(s_ctx, 16)
                    sp.wait_ge(s_x2, b * T + T)
                    sp.dma_start(xres[:], x_d[b + 1].rearrange("(t p) d -> p t d", p=P)).then_inc(s_x, 16)
                for f in range(FT):
                    if more or f + RING < FT:
                        sp.wait_ge(s_fmm2, b * FT + f + 1)
                        load_ring(f % RING, (f + RING) % FT)
                for t in range(T):
                    sp.wait_ge(s_x4, b * T + t + 2)
                    sp.dma_start(out_d[b, t * P:(t + 1) * P, :], xb[:, t, :]).then_inc(s_out, 16)
                sp.wait_ge(s_out, (b + 1) * T * 16)
                sp.sem_inc(s_stored, 1)

            sp.sem_inc(s_stored, 1)
            with sp.Fori(0, B - 1) as i:
                batch(i, True)
            batch(B - 1, False)
            sp.wait_ge(s_out, B * T * 16)

        @block.tensor
        def _(pe):
            def scan_bcast(b, n):
                if n == 0:
                    pe.wait_ge(s_split, b + 1)
                    pe.wait_ge(s_spabs, b * J + J)
                    pe.wait_ge(s_spmax, b * J + J)
                else:
                    pe.wait_ge(s_bcc, b * 2 * NS + 2 * n)
                for i in range(2):
                    pe.matmul(banks[i][:], pick[:, i * NS + n:i * NS + n + 1].broadcast_to([P, P]), xd3[:],
                              start=True, stop=True).then_inc(s_bc, 1)

            def att_transpose(b, j):
                pe.wait_ge(s_eprob, b * J + j + 1)
                for k in range(J):
                    last = pe.transpose(banks[2][:, k * P:(k + 1) * P], ex[:, k * P:(k + 1) * P], ident[:])
                last.then_inc(s_eT, 1)

            def mixer(b, prev, slot):
                if slot in (0, 1):
                    if slot == 0:
                        pe.wait_ge(s_ctx, b * 16 + 16)
                        if prev is not None:
                            pe.wait_ge(s_x1, prev * T + T)
                    for j in (2 * slot, 2 * slot + 1):
                        if j >= 2:
                            pe.wait_ge(s_inprojc, b * J + j - 1)
                        for k in range(KC):
                            last = pe.matmul(banks[j % 2][:], ipw[:, k, j * P:(j + 1) * P], ctxT[:, k, :],
                                             start=k == 0, stop=k == KC - 1)
                        last.then_inc(s_inproj, 1)
                if slot == 2:
                    pe.wait_ge(s_u, b + 1)
                    for j in range(J):
                        last = pe.matmul(banks[0][:], xpw[:, j, :], u[:, j, :], start=j == 0, stop=j == J - 1)
                    last.then_inc(s_xdbl, 1)
                if slot == 3:
                    pe.wait_ge(s_xd, b + 1)
                    for j in range(J):
                        if j >= 2:
                            pe.wait_ge(s_spabs, b * J + j - 1)
                            pe.wait_ge(s_spmax, b * J + j - 1)
                        pe.matmul(banks[j % 2][:], dtw[:, j * P:(j + 1) * P], xd[0:R, :],
                                  start=True, stop=True).then_inc(s_dtmm, 1)
                    scan_bcast(b, 0)
                if slot in SCAN_SLOTS:
                    for n in SCAN_SLOTS[slot][:1]:
                        if n + 1 < NS:
                            scan_bcast(b, n + 1)
                if slot == 6:
                    if prev is not None:
                        pe.wait_ge(s_xnTc, prev * 2 * T + 2 * T)
                    for i in range(2):
                        if i:
                            pe.wait_ge(s_qk, b * 2 + 1)
                        for k in range(KC):
                            last = pe.matmul(banks[2][:], wqk[:, k, i, :], ctxT[:, k, :],
                                             start=k == 0, stop=k == KC - 1)
                        last.then_inc(s_qkmm, 1)
                if slot in ATT_SLOTS:
                    j = ATT_SLOTS[slot]
                    if j == 0:
                        pe.wait_ge(s_qk, b * 2 + 2)
                    else:
                        att_transpose(b, j - 1)

            def mixer_late(b, prev, slot):
                if slot in SCAN_SLOTS:
                    for n in SCAN_SLOTS[slot][1:]:
                        if n + 1 < NS:
                            scan_bcast(b, n + 1)
                if slot in ATT_SLOTS:
                    j = ATT_SLOTS[slot]
                    if j:
                        pe.wait_ge(s_att, b * J + j)
                    pe.matmul(banks[2][:], qk[:, 0, j * P:(j + 1) * P], qk[:, 1, :],
                              start=True, stop=True).then_inc(s_emm, 1)
                if slot == 11:
                    att_transpose(b, J - 1)
                if slot == 13:
                    for t in range(T):
                        if t == 0:
                            pe.wait_ge(s_y, b * J + J)
                        if t >= 2:
                            pe.wait_ge(s_x1, b * T + t - 1)
                        for j in range(J):
                            last = pe.transpose(banks[t % 2][:, j * P:(j + 1) * P], u[:, j, t * P:(t + 1) * P],
                                                ident[:])
                        last.then_inc(s_yT, 1)
                if slot == 14:
                    for t in range(T):
                        pe.wait_ge(s_q1, b * T + t + 1)
                        if t:
                            pe.wait_ge(s_qT, b * T + t)
                        else:
                            pe.wait_ge(s_att, b * J + J)
                        for k in range(J):
                            last = pe.transpose(bf_bank[2][:, k * P:(k + 1) * P], q1[:, k * P:(k + 1) * P],
                                                identb[:])
                        last.then_inc(s_q1T, 1)

            def up1(b, t):
                pe.wait_ge(s_qT, b * T + t + 1)
                for c in range(FC):
                    if t:
                        pe.wait_ge(s_gelu, b * T * FC + (t - 1) * FC + c + 1)
                    else:
                        pe.wait_ge(s_x4, b * T + 1)
                    for k in range(J):
                        last = pe.matmul(banks[4 + c][:], qT[:, k, t * P:(t + 1) * P],
                                         w1q[:, k, c * 512:(c + 1) * 512], start=k == 0, stop=k == J - 1)
                    last.then_inc(s_mm1, 1)

            def norm_transpose(b, i, bank):
                pe.wait_ge(s_xn, b * 2 * T + i + 1)
                for k in range(J):
                    last = pe.transpose(banks[bank][:, k * P:(k + 1) * P], xn[:, i % 2, k * P:(k + 1) * P], ident[:])
                last.then_inc(s_xnT, 1)

            def attend(b, t):
                pe.wait_ge(s_xnTc, b * 2 * T + t + 1)
                for k in range(J):
                    last = pe.matmul(banks[4 + t][:], xnT[:, k, t * P:(t + 1) * P], attT[:, k, :],
                                     start=k == 0, stop=k == J - 1)
                last.then_inc(s_xm, 1)

            def f_up(b, f):
                if f:
                    pe.wait_ge(s_fgelu, b * FT + f)
                else:
                    pe.wait_ge(s_xnTc, b * 2 * T + 2 * T)
                pe.wait_ge(s_ring[f % RING], (b * (FT // RING) + f // RING + 1) * 16)
                for k in range(J):
                    last = pe.matmul(banks[3][:], ring[:, f % RING, k * P:(k + 1) * P], xnT[:, k, :],
                                     start=k == 0, stop=k == J - 1)
                last.then_inc(s_fmm1, 1)

            def f_down(b, f):
                pe.wait_ge(s_fgelu, b * FT + f + 1)
                if f == 0:
                    pe.wait_ge(s_x3, b * T + T)
                for t in range(T):
                    last = pe.matmul(banks[4 + t][:], hT[:, f % 2, t * P:(t + 1) * P], ring[:, f % RING, D:2 * D],
                                     start=f == 0, stop=f == FT - 1)
                last.then_inc(s_fmm2, 1)

            def rest_a(b, slot):
                if slot < T:
                    if slot == 0:
                        up1(b, 0)
                    if slot + 1 < T:
                        up1(b, slot + 1)

            def rest_b(b, slot):
                if slot < T:
                    t = slot
                    pe.wait_ge(s_hq, b * T + t + 1)
                    if t == 0:
                        pe.wait_ge(s_qT, b * T + T)
                    for r in range(2):
                        if r == 0:
                            if t:
                                pe.wait_ge(s_x2, b * T + t)
                        elif t >= 2:
                            pe.wait_ge(s_xnTc, b * 2 * T + t - 1)
                        elif t:
                            pe.wait_ge(s_ev1, b * T + t)
                        for i in range(FT // 2):
                            f = r * (FT // 2) + i
                            last = pe.transpose(bf_bank[2 + r][:, i * P:(i + 1) * P], hq[:, f * P:(f + 1) * P],
                                                identb[:])
                        last.then_inc(s_hqT, 1)
                    pe.wait_ge(s_ev0, b * T + t + 1)
                    pe.wait_ge(s_ev1, b * T + t + 1)
                    for f in range(FT):
                        last = pe.matmul(banks[2][:], hqT[:, f, :], w2q[:, f, :], start=f == 0, stop=f == FT - 1)
                    last.then_inc(s_mm2, 1)
                    if t:
                        norm_transpose(b, t - 1, 3)
                if slot == 4:
                    pe.wait_ge(s_att, b * J + J)
                    pe.wait_ge(s_gelu, b * T * FC + T * FC)
                    attend(b, 0)
                    attend(b, 1)
                    pe.wait_ge(s_xnTc, b * 2 * T + T - 1)
                    norm_transpose(b, T - 1, 3)
                if slot == 5:
                    attend(b, 2)
                    attend(b, 3)
                    for i in range(T, 2 * T):
                        if i >= T + 2:
                            pe.wait_ge(s_xnTc, b * 2 * T + i - 1)
                        elif i == T:
                            pe.wait_ge(s_x2, b * T + T)
                        norm_transpose(b, i, 2 + i % 2)

            def rest_ffn(b, slot, which):
                if slot in FFN_SLOTS:
                    f = FFN_SLOTS[slot][which]
                    f_up(b, f)
                    if f:
                        f_down(b, f - 1)
                if slot == 14 and which == 0:
                    f_down(b, FT - 1)

            def weight_mean(i):
                pe.wait_ge(s_wsq, i + 1)
                pe.matmul(banks[3][:, i:i + 1], ones[:], wsum[:, i:i + 1], start=True, stop=True).then_inc(s_wmean, 1)

            pe.wait_ge(s_const, const_wait)
            pe.wait_ge(s_ones, 2)
            for slot in range(SLOTS):
                mixer(0, None, slot)
                if slot == 2:
                    weight_mean(0)
                if slot == 7:
                    weight_mean(1)
                mixer_late(0, None, slot)
            pe.wait_ge(s_wq, 8)
            with pe.Fori(0, B - 1) as i:
                for slot in range(SLOTS):
                    rest_a(i, slot)
                    mixer(i + 1, i, slot)
                    rest_b(i, slot)
                    rest_ffn(i, slot, 0)
                    mixer_late(i + 1, i, slot)
                    rest_ffn(i, slot, 1)
            for slot in range(SLOTS):
                rest_a(B - 1, slot)
                rest_b(B - 1, slot)
                rest_ffn(B - 1, slot, 0)
                rest_ffn(B - 1, slot, 1)

        @block.scalar
        def _(act):
            def copy_bc(b, n):
                for i, (dst, used) in enumerate(((bcast, s_dbu), (ccast, s_hc))):
                    act.wait_ge(s_bc, b * 2 * NS + 2 * n + i + 1)
                    if n >= 2:
                        act.wait_ge(used, b * HN + 2 * (n - 1))
                    act.activation(dst[:, n % 2, :], banks[i][:], ACT.Copy).then_inc(s_bcc, 1)

            def decays(b, n):
                for p in range(2):
                    s = 2 * n + p
                    if s >= 2:
                        act.wait_ge(s_scan, b * HN + s - 1)
                    for q in range(HALF):
                        j = p * HALF + q
                        last = act.activation(decay[:, s % 2, q, 1:], dt[:, j, 1:], ACT.Exp,
                                              scale=a_neg[:, j, n:n + 1])
                    last.then_inc(s_decay, 1)

            def mixer(b, prev, slot):
                if slot in (0, 1):
                    for j in (2 * slot, 2 * slot + 1):
                        act.wait_ge(s_inproj, b * J + j + 1)
                        if j >= 2:
                            act.wait_ge(s_conv, b * J + j - 1)
                        elif prev is not None:
                            act.wait_ge(s_conv, prev * J + J)
                        act.activation(xpad[:, j % 2, PAD:], banks[j % 2][:], ACT.Copy).then_inc(s_inprojc, 1)
                if slot == 2:
                    act.wait_ge(s_conv, b * J + J)
                    act.activation(u[:], u[:], ACT.Silu).then_inc(s_u, 1)
                    act.wait_ge(s_xdbl, b + 1)
                    if prev is not None:
                        act.wait_ge(s_bc, prev * 2 * NS + 2 * NS)
                    act.activation(xd[:], banks[0][:], ACT.Copy).then_inc(s_xd, 1)
                if slot == 3:
                    for j in range(J):
                        tmp = work[:, j % 2, :, :]
                        act.wait_ge(s_dtmm, b * J + j + 1)
                        if j >= 2:
                            act.wait_ge(s_dt, b * J + j - 1)
                        act.activation(tmp[:, 0, :], banks[j % 2][:], ACT.Abs,
                                       bias=pch[:, j, PC_DTB:PC_DTB + 1]).then_inc(s_spabs, 1)
                        act.wait_ge(s_spabs, b * J + j + 1)
                        act.activation(tmp[:, 0, :], tmp[:, 0, :], ACT.Exp, scale=-1.0).then_inc(s_spexp, 1)
                        act.wait_ge(s_spexp, b * J + j + 1)
                        act.activation(tmp[:, 1, :], tmp[:, 0, :], ACT.Ln, bias=1.0).then_inc(s_spln, 1)
                    copy_bc(b, 0)
                if slot in SCAN_SLOTS:
                    n = SCAN_SLOTS[slot][0]
                    if n == 0:
                        act.wait_ge(s_dt, b * J + J)
                    decays(b, n)
                    if n + 1 < NS:
                        copy_bc(b, n + 1)
                if slot == 6:
                    for i in range(2):
                        act.wait_ge(s_qkmm, b * 2 + i + 1)
                        if prev is not None:
                            act.wait_ge(s_emm, prev * J + J)
                        act.activation(qk[:, i, :], banks[2][:], ACT.Identity, bias=bqk[:, i:i + 1]).then_inc(s_qk, 1)
                if slot in ATT_SLOTS and ATT_SLOTS[slot]:
                    att_copy(b, prev, ATT_SLOTS[slot] - 1)

            def att_copy(b, prev, j):
                act.wait_ge(s_eT, b * J + j + 1)
                if prev is not None:
                    act.wait_ge(s_xm, prev * T + T)
                act.activation(attT[:, :, j * P:(j + 1) * P], banks[2][:].rearrange("p (k m) -> p k m", k=J),
                               ACT.Copy).then_inc(s_att, 1)

            def mixer_late(b, prev, slot):
                if slot in SCAN_SLOTS:
                    for n in SCAN_SLOTS[slot][1:]:
                        decays(b, n)
                        if n + 1 < NS:
                            copy_bc(b, n + 1)
                if slot in ATT_SLOTS:
                    j = ATT_SLOTS[slot]
                    act.wait_ge(s_emax, b * J + j + 1)
                    if j:
                        act.wait_ge(s_eT, b * J + j)
                    act.activation(ex[:], banks[2][:], ACT.Exp, bias=ast[:, j, 0:1],
                                   accum_out=ast[:, j, 1:2]).then_inc(s_eexp, 1)
                if slot == 11:
                    att_copy(b, prev, J - 1)
                if slot == 13:
                    for j in range(J):
                        act.wait_ge(s_zrs, b * J + j + 1)
                        if j >= 2:
                            act.wait_ge(s_y, b * J + j - 1)
                        elif prev is not None:
                            act.wait_ge(s_y, prev * J + J)
                        act.activation(zs[:, j % 2, :], xres[:, j, :], ACT.Silu, scale=zst[:, j, 9:10],
                                       bias=zst[:, j, 10:11]).then_inc(s_zs, 1)
                if slot == 14:
                    for t in range(T):
                        act.wait_ge(s_q1T, b * T + t + 1)
                        if prev is not None and t == 0:
                            act.wait_ge(s_mm1, prev * T * FC + T * FC)
                        act.activation(qT[:, :, t * P:(t + 1) * P],
                                       bf_bank[2][:, 0:J * P].rearrange("p (k l) -> p k l", k=J),
                                       ACT.Copy).then_inc(s_qT, 1)

            def gelu1(b, t):
                for c in range(FC):
                    act.wait_ge(s_mm1, b * T * FC + t * FC + c + 1)
                    if c == 0:
                        if t >= 2:
                            act.wait_ge(s_hq, b * T + t - 1)
                    act.activation(h[t % 2][:, c * 512:(c + 1) * 512], banks[4 + c][:], ACT.Gelu,
                                   scale=mst[:, t, 13:14]).then_inc(s_gelu, 1)

            def norm_copy(b, i):
                act.wait_ge(s_xnT, b * 2 * T + i + 1)
                t = i % T
                if i >= T:
                    act.wait_ge(s_xm, b * T + t + 1)
                bank = 3 if i < T else 2 + i % 2
                act.activation(xnT[:, :, t * P:(t + 1) * P], banks[bank][:].rearrange("p (k l) -> p k l", k=J),
                               ACT.Copy).then_inc(s_xnTc, 1)

            def rest_a(b, slot):
                if slot < T:
                    if slot == 0:
                        gelu1(b, 0)
                    if slot + 1 < T:
                        gelu1(b, slot + 1)

            def rest_b(b, slot):
                if slot < T:
                    t = slot
                    act.wait_ge(s_hqT, b * 2 * T + 2 * t + 1)
                    if t:
                        act.wait_ge(s_mm2, b * T + t)
                    act.activation(hqT[:, 0:FT // 2, :], bf_bank[2].rearrange("p (f l) -> p f l", l=P),
                                   ACT.Copy).then_inc(s_ev0, 1)
                    if t:
                        norm_copy(b, t - 1)
                if slot == 4:
                    norm_copy(b, T - 1)
                if slot == 5:
                    for i in range(T, 2 * T):
                        norm_copy(b, i)

            def rest_ffn(b, slot, which):
                if slot in FFN_SLOTS:
                    f = FFN_SLOTS[slot][which]
                    act.wait_ge(s_fmm1, b * FT + f + 1)
                    if f >= 2:
                        act.wait_ge(s_fmm2, b * FT + f - 1)
                    act.activation(hT[:, f % 2, :], banks[3][:], ACT.Gelu, bias=b1[:, f:f + 1]).then_inc(s_fgelu, 1)

            act.wait_ge(s_const, const_wait)
            act.activation(gates[:], gates[:], ACT.Tanh).then_inc(s_gates, 1)
            act.activation(a_neg[:], pch[:, :, PC_ALOG:], ACT.Exp).then_inc(s_aneg, 1)
            act.wait_ge(s_aneg, 1)
            act.activation(a_neg[:], a_neg[:], ACT.Copy, scale=-1.0).then_inc(s_aneg, 1)
            act.wait_ge(s_aneg, 2)
            act.wait_ge(s_gates, 1)

            def square(i, junk):
                act.wait_ge(s_stage, 16 * (i + 1))
                act.activation(junk, stage[:], ACT.Square, accum_out=wsum[:, i:i + 1]).then_inc(s_wsq, 1)
                act.wait_ge(s_wsq, i + 1)

            def quantise(i, c):
                dst = (w1q if i == 0 else w2q)[:].rearrange("p a b -> p (a b)")
                act.wait_ge(s_wscaled, 4 * i + c + 1)
                act.activation(dst[:, c * FF:(c + 1) * FF], stage[:, c * FF:(c + 1) * FF], ACT.Copy,
                               bias=-MAGIC).then_inc(s_wq, 1)

            for slot in range(SLOTS):
                mixer(0, None, slot)
                if slot == 2:
                    square(0, w1q[:].rearrange("p a b -> p (a b)"))
                if 4 <= slot < 6:
                    quantise(0, 2 * (slot - 4))
                    quantise(0, 2 * (slot - 4) + 1)
                if slot == 7:
                    square(1, w2q[:].rearrange("p a b -> p (a b)"))
                if 8 <= slot < 12:
                    quantise(1, slot - 8)
                mixer_late(0, None, slot)
            with act.Fori(0, B - 1) as i:
                for slot in range(SLOTS):
                    rest_a(i, slot)
                    mixer(i + 1, i, slot)
                    rest_b(i, slot)
                    rest_ffn(i, slot, 0)
                    mixer_late(i + 1, i, slot)
                    rest_ffn(i, slot, 1)
            for slot in range(SLOTS):
                rest_a(B - 1, slot)
                rest_b(B - 1, slot)
                rest_ffn(B - 1, slot, 0)
                rest_ffn(B - 1, slot, 1)

        @block.vector
        def _(dve):
            def half_step(b, n, p):
                s = 2 * n + p
                js = slice(p * HALF, (p + 1) * HALF)
                w3 = work[:, s % SCANBUFS, :, :]
                flat = w3.rearrange("p a l -> p (a l)")
                dve.wait_ge(s_bcc, b * 2 * NS + 2 * n + 1)
                if s == 0:
                    dve.wait_ge(s_du, b * J + J)
                if s >= SCANBUFS:
                    dve.wait_ge(s_acc, b * HN + s - SCANBUFS + 1)
                dve.tensor_tensor(w3, du[:, js, :], bcast[:, n % 2, :].unsqueeze(1).broadcast_to([P, HALF, L]),
                                  ALU.mult).then_inc(s_dbu, 1)
                dve.wait_ge(s_dbu, b * HN + s + 1)
                dve.wait_ge(s_decay, b * HN + s + 1)
                dve.tensor_tensor_scan(flat, decay[:, s % 2, :, :].rearrange("p a l -> p (a l)"), flat, 0.0,
                                       ALU.mult, ALU.add).then_inc(s_scan, 1)
                dve.wait_ge(s_scan, b * HN + s + 1)
                dve.wait_ge(s_bcc, b * 2 * NS + 2 * n + 2)
                dve.tensor_tensor(w3, w3, ccast[:, n % 2, :].unsqueeze(1).broadcast_to([P, HALF, L]),
                                  ALU.mult).then_inc(s_hc, 1)

            def mixer(b, prev, slot):
                if slot == 0:
                    dve_m.start()
                if slot in (0, 1):
                    for j in (2 * slot, 2 * slot + 1):
                        dve.wait_ge(s_inprojc, b * J + j + 1)
                        if prev is not None and j == 0:
                            dve.wait_ge(s_yT, prev * T + T)
                        xp = xpad[:, j % 2, :]
                        dve_m.link(dve, b, dve.tensor_scalar(u[:, j, :], xp[:, 0:L], pch[:, j, 0:1],
                                                             pch[:, j, PC_CONVB:PC_CONVB + 1], ALU.mult, ALU.add))
                        for k in range(1, TAPS):
                            ins = dve.scalar_tensor_tensor(u[:, j, :], xp[:, k:k + L], pch[:, j, k:k + 1], u[:, j, :],
                                                           ALU.mult, ALU.add)
                            if k < TAPS - 1:
                                dve_m.link(dve, b, ins)
                            else:
                                ins.then_inc(s_conv, 1)
                if slot == 2:
                    dve.wait_ge(s_xd, b + 1)
                    if prev is not None:
                        dve.wait_ge(s_bc, prev * 2 * NS + 2 * NS)
                        dve.wait_ge(s_q1, prev * T + T)
                    dve_m.link(dve, b, dve.tensor_copy(xd3[:], xd[:]))
                    tmp = x1n[:]
                    dve_m.link(dve, b, dve.tensor_tensor(tmp, xd[:], xd3[:], ALU.subtract))
                    dve_m.link(dve, b, dve.tensor_copy(xd3[64:128, :], tmp[64:128, :]))
                    dve_m.link(dve, b, dve.tensor_tensor(tmp[96:128, :], tmp[96:128, :], xd3[96:128, :], ALU.subtract))
                    dve.tensor_copy(xd3[96:128, :], tmp[96:128, :]).then_inc(s_split, 1)
                if slot == 3:
                    for j in range(J):
                        dve.wait_ge(s_spabs, b * J + j + 1)
                        dve.tensor_scalar(dt[:, j, :], banks[j % 2][:], pch[:, j, PC_DTB:PC_DTB + 1], 0.0,
                                          ALU.add, ALU.max).then_inc(s_spmax, 1)
                if slot == 7:
                    dve.wait_ge(s_x, b * 16 + 16)
                    for j in range(J):
                        dve_m.link(dve, b, dve.bn_stats(zst[:, j, 0:6], xres[:, j, :]))
                        carry_wait(dve, "dve")
                        dve.bn_aggr(zst[:, j, 6:8], zst[:, j, 0:6]).then_inc(s_zst, 1)

            def scans(b, slot, which):
                if slot in SCAN_SLOTS and which < len(SCAN_SLOTS[slot]):
                    for p in range(2):
                        half_step(b, SCAN_SLOTS[slot][which], p)

            def mixer_late(b, prev, slot):
                if slot in ATT_SLOTS:
                    j = ATT_SLOTS[slot]
                    dve.wait_ge(s_emm, b * J + j + 1)
                    dve.tensor_reduce(ast[:, j, 0:1], banks[2][:], AX.X, ALU.max, negate=True).then_inc(s_emax, 1)
                if slot == 13:
                    for j in range(J):
                        dve.wait_ge(s_zs, b * J + j + 1)
                        if j == 0:
                            dve.wait_ge(s_acc, b * HN + HN)
                        dve.tensor_tensor(u[:, j, :], u[:, j, :], zs[:, j % 2, :], ALU.mult).then_inc(s_y, 1)
                    for t in range(T):
                        dve.wait_ge(s_yT, b * T + t + 1)
                        dve.scalar_tensor_tensor(xres[:, t, :], banks[t % 2][:], gates[:, 0:1], xres[:, t, :],
                                                 ALU.mult, ALU.add).then_inc(s_x1, 1)
                        dve.wait_ge(s_x1, b * T + t + 1)
                        dve_m.link(dve, b, dve.bn_stats(mst[:, t, 0:6], xres[:, t, :]))
                        carry_wait(dve, "dve")
                        dve.bn_aggr(mst[:, t, 6:8], mst[:, t, 0:6]).then_inc(s_x1st, 1)
                if slot == 14:
                    for t in range(T):
                        st = mst[:, t, :]
                        dve.wait_ge(s_x1rs, b * T + t + 1)
                        if t:
                            dve.wait_ge(s_q1, b * T + t)
                        dve_m.link(dve, b, dve.tensor_scalar(x1n[:], xres[:, t, :], st[:, 6:7], st[:, 9:10],
                                                             ALU.subtract, ALU.mult))
                        dve_m.link(dve, b, dve.tensor_reduce(st[:, 10:11], x1n[:], AX.X, ALU.max,
                                                             apply_absolute_value=True))
                        dve_m.link(dve, b, dve.tensor_scalar(st[:, 11:12], st[:, 10:11], Q_EPS, None, ALU.max))
                        dve_m.link(dve, b, dve.reciprocal(st[:, 12:13], st[:, 11:12]))
                        dve_m.link(dve, b, dve.tensor_scalar(st[:, 12:13], st[:, 12:13], 127.0, None, ALU.mult))
                        dve_m.link(dve, b, dve.tensor_scalar(st[:, 13:14], st[:, 11:12], wstat[:, 0, 3:4], None,
                                                             ALU.mult))
                        dve_m.link(dve, b, dve.tensor_scalar(x1n[:], x1n[:], st[:, 12:13], MAGIC, ALU.mult, ALU.add))
                        if t:
                            dve.wait_ge(s_q1T, b * T + t)
                        dve.tensor_scalar(q1[:], x1n[:], MAGIC, 127.0, ALU.subtract, ALU.min).then_inc(s_q1, 1)

            def att_probs(b, slot):
                j = ATT_SLOTS[slot]
                dve.wait_ge(s_eexp, b * J + j + 1)
                dve_m.link(dve, b, dve.reciprocal(ast[:, j, 2:3], ast[:, j, 1:2]))
                dve.tensor_scalar(ex[:], ex[:], ast[:, j, 2:3], None, ALU.mult).then_inc(s_eprob, 1)

            def norm(b, i):
                t = i % T
                st = fst[:, t, 8:18]
                dve_f.link(dve, b, dve.bn_stats(st[:, 0:6], xb[:, t, :]))
                carry_wait(dve, "dve")
                dve.bn_aggr(st[:, 6:8], st[:, 0:6]).then_inc(s_lnst, 1)

            def norm_apply(b, i):
                t = i % T
                st = fst[:, t, 8:18]
                dve.wait_ge(s_lnrs, b * 2 * T + i + 1)
                if i >= 2:
                    dve.wait_ge(s_xnT, b * 2 * T + i - 1)
                dve.tensor_scalar(xn[:, i % 2, :], xb[:, t, :], st[:, 6:7], st[:, 9:10],
                                  ALU.subtract, ALU.mult).then_inc(s_xn, 1)

            def rest(b, slot):
                if slot < T:
                    t = slot
                    st = fst[:, t, :]
                    dve.wait_ge(s_gelu, b * T * FC + (t + 1) * FC)
                    dve_f.link(dve, b, dve.tensor_reduce(st[:, 0:1], h[t % 2], AX.X, ALU.max,
                                                         apply_absolute_value=True))
                    dve_f.link(dve, b, dve.tensor_scalar(st[:, 1:2], st[:, 0:1], Q_EPS, None, ALU.max))
                    dve_f.link(dve, b, dve.reciprocal(st[:, 2:3], st[:, 1:2]))
                    dve.tensor_scalar(st[:, 3:4], st[:, 2:3], 127.0, None, ALU.mult).then_inc(s_hsc, 1)
                    dve.wait_ge(s_hr, b * T + t + 1)
                    if t:
                        dve.wait_ge(s_hqT, b * 2 * T + 2 * t)
                    dve.tensor_scalar(hq[:], h[t % 2], MAGIC, 127.0, ALU.subtract, ALU.min).then_inc(s_hq, 1)

            def rest_late(b, slot):
                if slot < T:
                    t = slot
                    st = fst[:, t, :]
                    dve.wait_ge(s_hqT, b * 2 * T + 2 * t + 2)
                    if t:
                        dve.wait_ge(s_mm2, b * T + t)
                    dve.tensor_copy(hqT[:, FT // 2:, :], bf_bank[3].rearrange("p (f l) -> p f l", l=P)).then_inc(s_ev1, 1)
                    dve_f.link(dve, b, dve.tensor_scalar(st[:, 4:5], st[:, 1:2], wstat[:, 1, 3:4], None, ALU.mult))
                    dve.wait_ge(s_mm2, b * T + t + 1)
                    dve.wait_ge(s_stored, b + 1)
                    dve.scalar_tensor_tensor(xb[:, t, :], banks[2][:], st[:, 4:5], xres[:, t, :],
                                             ALU.mult, ALU.add).then_inc(s_x2, 1)
                    dve.wait_ge(s_x2, b * T + t + 1)
                    norm(b, t)
                    norm_apply(b, t)

            def third(b, t):
                dve.wait_ge(s_xm, b * T + t + 1)
                dve.scalar_tensor_tensor(xb[:, t, :], banks[4 + t][:], gates[:, 1:2], xb[:, t, :],
                                         ALU.mult, ALU.add).then_inc(s_x3, 1)
                dve.wait_ge(s_x3, b * T + t + 1)
                norm(b, T + t)
                norm_apply(b, T + t)

            def fourth(b):
                dve.wait_ge(s_fmm2, b * FT + FT)
                dve.wait_ge(s_x3b, b * T + T)
                for t in range(T):
                    dve.scalar_tensor_tensor(xb[:, t, :], banks[4 + t][:], gates[:, 3:4], xb[:, t, :],
                                             ALU.mult, ALU.add).then_inc(s_x4, 1)

            dve.memset(ones[:], 1.0).then_inc(s_ones, 1)
            dve.memset(xpad[:, :, 0:PAD], 0.0).then_inc(s_pad, 1)
            dve.sem_inc(s_x4, 1)
            dve.memset(decay[:, :, :, 0:1], 0.0).then_inc(s_pad, 1)
            dve.wait_ge(s_pad, 2)
            dve.wait_ge(s_const, const_wait)
            dve.wait_ge(s_gates, 1)
            dve.tensor_scalar(b2[:], b2[:], gates[:, 3:4], None, ALU.mult).then_inc(s_b2, 1)

            def weight_scale(i, c):
                w = stage[:, c * FF:(c + 1) * FF]
                dve.wait_ge(s_wstat, i + 1)
                dve_w.link(dve, 0, dve.tensor_scalar(w, w, wstat[:, i, 1:2], 1.0, ALU.mult, ALU.min))
                dve.tensor_scalar(w, w, -1.0, MAGIC, ALU.max, ALU.add).then_inc(s_wscaled, 1)

            def weight_mean(i):
                dve.wait_ge(s_wmean, i + 1)
                dve.tensor_scalar(wstat[:, i, 0:1], banks[3][:, i:i + 1], 1.0 / (FF * D), Q_EPS,
                                  ALU.mult, ALU.max).then_inc(s_wms, 1)

            for slot in range(SLOTS):
                mixer(0, None, slot)
                if slot == 2:
                    weight_mean(0)
                if slot == 3:
                    for c in range(4):
                        weight_scale(0, c)
                scans(0, slot, 0)
                if slot == 7:
                    weight_mean(1)
                if slot == 8:
                    for c in range(4):
                        weight_scale(1, c)
                mixer_late(0, None, slot)
                scans(0, slot, 1)
                if slot in ATT_SLOTS:
                    att_probs(0, slot)
            with dve.Fori(0, B - 1) as i:
                dve_f.start()
                for slot in range(SLOTS):
                    rest(i, slot)
                    mixer(i + 1, i, slot)
                    rest_late(i, slot)
                    if slot in (4, 5):
                        third(i, 2 * (slot - 4))
                        half_step(i + 1, slot - 4, 0)
                        third(i, 2 * (slot - 4) + 1)
                        half_step(i + 1, slot - 4, 1)
                    else:
                        scans(i + 1, slot, 0)
                    mixer_late(i + 1, i, slot)
                    if slot == 14:
                        fourth(i)
                    scans(i + 1, slot, 1)
                    if slot in ATT_SLOTS:
                        att_probs(i + 1, slot)
            dve_f.start()
            for slot in range(SLOTS):
                rest(B - 1, slot)
                rest_late(B - 1, slot)
                if slot in (4, 5):
                    third(B - 1, 2 * (slot - 4))
                    third(B - 1, 2 * (slot - 4) + 1)
                if slot == 14:
                    fourth(B - 1)

        @block.gpsimd
        def _(pool):
            def mixer(b, prev, slot):
                if slot == 0:
                    pool_m.start()
                if slot == 3:
                    for j in range(J):
                        e, ln = work[:, j % 2, 0, :], work[:, j % 2, 1, :]
                        tmp = work[:, 2, j % 2, :]
                        pool.wait_ge(s_spexp, b * J + j + 1)
                        carry_wait(pool, "pool")
                        pool_m.link(pool, b, pool.tensor_scalar(tmp, e, 1.0, -1.0, ALU.add, ALU.add))
                        pool.wait_ge(s_spln, b * J + j + 1)
                        pool_m.link(pool, b, pool.tensor_tensor(tmp, e, tmp, ALU.subtract))
                        pool_m.link(pool, b, pool.tensor_tensor(tmp, tmp, ln, ALU.add))
                        pool.wait_ge(s_spmax, b * J + j + 1)
                        pool.tensor_tensor(dt[:, j, :], dt[:, j, :], tmp, ALU.add).then_inc(s_dt, 1)
                        pool.wait_ge(s_dt, b * J + j + 1)
                        if j == 0:
                            pool.wait_ge(s_xdbl, b + 1)
                        pool.tensor_tensor(du[:, j, :], dt[:, j, :], u[:, j, :], ALU.mult).then_inc(s_du, 1)
                        pool.wait_ge(s_du, b * J + j + 1)
                        carry_wait(pool, "pool")
                        pool.tensor_scalar(u[:, j, :], u[:, j, :], pch[:, j, PC_D:PC_D + 1], 1.0,
                                           ALU.mult, ALU.mult).then_inc(s_accin, 1)
                    pool.wait_ge(s_accin, b * J + J)
                if slot == 7:
                    for j in range(J):
                        st = zst[:, j, :]
                        pool.wait_ge(s_zst, b * J + j + 1)
                        rsqrt(pool_m, b, st[:, 8:9], st[:, 7:8], LN_EPS, st[:, 9:10])
                        carry_wait(pool, "pool")
                        pool.tensor_scalar(st[:, 10:11], st[:, 6:7], st[:, 9:10], -1.0, ALU.mult,
                                           ALU.mult).then_inc(s_zrs, 1)

            def rsqrt(tally, b, tmp, var, eps, out, last=None):
                carry_wait(pool, "pool")
                tally.link(pool, b, pool.tensor_scalar(tmp, var, eps, 1.0, ALU.add, ALU.mult))
                ins = pool.tensor_tensor(out, tmp, expo[:, 0:1], ALU.pow)
                if last is None:
                    tally.link(pool, b, ins)
                else:
                    ins.then_inc(last, 1)

            def accumulate(b, n, p):
                s = 2 * n + p
                js = slice(p * HALF, (p + 1) * HALF)
                pool.wait_ge(s_hc, b * HN + s + 1)
                if s >= 2:
                    pool.wait_ge(s_acc, b * HN + s - 1)
                pool.tensor_tensor(u[:, js, :], u[:, js, :], work[:, s % SCANBUFS, :, :], ALU.add).then_inc(s_acc, 1)

            def scans(b, slot, which):
                if slot in SCAN_SLOTS and which < len(SCAN_SLOTS[slot]):
                    for p in range(2):
                        accumulate(b, SCAN_SLOTS[slot][which], p)

            def mixer_late(b, prev, slot):
                if slot == 13:
                    for t in range(T):
                        st = mst[:, t, :]
                        pool.wait_ge(s_x1st, b * T + t + 1)
                        rsqrt(pool_m, b, st[:, 8:9], st[:, 7:8], LN_EPS, st[:, 9:10], s_x1rs)

            def norm(b, i):
                st = fst[:, i % T, 8:18]
                pool.wait_ge(s_lnst, b * 2 * T + i + 1)
                rsqrt(pool_f, b, st[:, 8:9], st[:, 7:8], LN_EPS, st[:, 9:10], s_lnrs)

            def rest(b, slot):
                if slot < T:
                    t = slot
                    pool.wait_ge(s_hsc, b * T + t + 1)
                    carry_wait(pool, "pool")
                    pool.tensor_scalar(h[t % 2], h[t % 2], fst[:, t, 3:4], MAGIC, ALU.mult, ALU.add).then_inc(s_hr, 1)

            def third(b, t):
                norm(b, T + t)

            def bias(b, t):
                pool.wait_ge(s_xn, b * 2 * T + T + t + 1)
                pool.tensor_tensor(xb[:, t, :], xb[:, t, :], b2[:], ALU.add).then_inc(s_x3b, 1)

            pool.memset(expo[:, 0:1], -0.5).then_inc(pool_s.sem, 1)
            pool.memset(expo[:, 1:2], 0.5).then_inc(s_ones, 1)
            pool.wait_ge(pool_s.sem, 1)
            pool.wait_ge(s_ones, 2)
            pool_s.n = 1
            pool.wait_ge(s_const, const_wait)

            def weight_rms(i):
                st = wstat[:, i, :]
                pool.wait_ge(s_wms, i + 1)
                pool_s.link(pool, 0, pool.tensor_tensor(st[:, 1:2], st[:, 0:1], expo[:, 0:1], ALU.pow))
                pool_s.link(pool, 0, pool.tensor_tensor(st[:, 2:3], st[:, 0:1], expo[:, 1:2], ALU.pow))
                if i == 0:
                    carry_wait(pool, "pool")
                    pool.tensor_scalar(st[:, 3:4], st[:, 2:3], 1.0 / 127.0, 1.0, ALU.mult, ALU.mult)\
                        .then_inc(s_wstat, 1)
                else:
                    pool.wait_ge(s_gates, 1)
                    carry_wait(pool, "pool")
                    pool.tensor_scalar(st[:, 3:4], st[:, 2:3], 1.0 / 127.0, gates[:, 2:3], ALU.mult, ALU.mult)\
                        .then_inc(s_wstat, 1)

            for slot in range(SLOTS):
                mixer(0, None, slot)
                if slot == 2:
                    weight_rms(0)
                scans(0, slot, 0)
                if slot == 7:
                    weight_rms(1)
                scans(0, slot, 1)
                mixer_late(0, None, slot)
            with pool.Fori(0, B - 1) as i:
                pool_f.start()
                for slot in range(SLOTS):
                    rest(i, slot)
                    mixer(i + 1, i, slot)
                    if slot < T:
                        norm(i, slot)
                    if slot in (4, 5):
                        for q in range(2):
                            third(i, 2 * (slot - 4) + q)
                            bias(i, 2 * (slot - 4) + q)
                            accumulate(i + 1, slot - 4, q)
                    else:
                        scans(i + 1, slot, 0)
                    scans(i + 1, slot, 1)
                    mixer_late(i + 1, i, slot)
            pool_f.start()
            for slot in range(SLOTS):
                rest(B - 1, slot)
                if slot < T:
                    norm(B - 1, slot)
                if slot in (4, 5):
                    for q in range(2):
                        third(B - 1, 2 * (slot - 4) + q)
                        bias(B - 1, 2 * (slot - 4) + q)


def kernel(x, ctx_1024, g_xattn, g_ffn, L0_xattn_in_proj_w, L0_xattn_conv_w, L0_xattn_conv_b, L0_xattn_x_proj_w,
           L0_xattn_dt_proj_w, L0_xattn_dt_proj_b, L0_xattn_A_log, L0_xattn_D, L0_ffn_w1, L0_ffn_w2, L1_xattn_Wq,
           L1_xattn_bq, L1_xattn_Wk, L1_xattn_bk, L1_ffn_proj1, L1_ffn_proj1_bias, L1_ffn_proj2, L1_ffn_proj2_bias,
           L1_ffn_gate_w):
    import ml_dtypes

    import concourse.bacc as bacc
    from concourse.bass_utils import run_bass_kernel_spmd

    g_x, g_f = np.asarray(g_xattn), np.asarray(g_ffn)
    xp = np.asarray(L0_xattn_x_proj_w)
    rank, rest = xp[:R].T, xp[R:].T
    p1, p2 = np.asarray(L1_ffn_proj1), np.asarray(L1_ffn_proj2)
    up = p1.reshape(FT, P, J, P).transpose(0, 3, 2, 1).reshape(FT, P, D)
    down = p2.reshape(D, FT, P).transpose(1, 2, 0)
    identity = np.eye(P, dtype=np.float32)
    part = np.arange(P)[:, None]
    pick = ((part % (2 * NS) == np.arange(2 * NS)[None, :]) & (part >= 2 * NS)).astype(ml_dtypes.bfloat16)
    arrays = {
        "x": x,
        "ctxT": np.asarray(ctx_1024).transpose(0, 2, 1),
        "in_proj": np.asarray(L0_xattn_in_proj_w).T,
        "x_proj": np.concatenate([rank, rank, rest, rest, rest], axis=1),
        "dt_proj": np.asarray(L0_xattn_dt_proj_w).T,
        "channels": np.concatenate([np.asarray(L0_xattn_conv_w)[:, 0, :], np.asarray(L0_xattn_conv_b)[:, None],
                                    np.asarray(L0_xattn_dt_proj_b)[:, None], np.asarray(L0_xattn_D)[:, None],
                                    np.asarray(L0_xattn_A_log)], axis=1),
        "w1": np.asarray(L0_ffn_w1).T,
        "w2": np.asarray(L0_ffn_w2).T,
        "wqk": np.stack([np.asarray(L1_xattn_Wq).T, np.asarray(L1_xattn_Wk).T]),
        "bqk": np.stack([np.asarray(L1_xattn_bq), np.asarray(L1_xattn_bk)], axis=1),
        "ffn": np.concatenate([up, down], axis=2),
        "b1": np.asarray(L1_ffn_proj1_bias).reshape(FT, P).T,
        "b2": np.broadcast_to(np.asarray(L1_ffn_proj2_bias), (P, D)),
        "gates": np.broadcast_to(np.stack([g_x[0], g_x[1], g_f[0], g_f[1]]), (P, 4)),
        "ident": identity,
        "identb": identity.astype(ml_dtypes.bfloat16),
        "pick": pick,
    }
    arrays = {f"{name}_dram": np.ascontiguousarray(a) for name, a in arrays.items()}
    nc = bacc.Bacc("TRN2", target_bir_lowering=False, num_devices=1)
    args = [nc.dram_tensor(name, a.shape, mybir.dt.from_np(a.dtype), kind="ExternalInput").ap()
            for name, a in arrays.items()]
    out = nc.dram_tensor("out_dram", (B, L, D), F32, kind="ExternalOutput").ap()
    program(nc, *args, out)
    got = run_bass_kernel_spmd(nc, [arrays], core_ids=[0])
    return got.results[0]["out_dram"]
```

```python
from contextlib import ExitStack

import numpy as np

import concourse.bass as bass
from concourse import mybir

F32 = mybir.dt.float32
BF16 = mybir.dt.bfloat16
ALU = mybir.AluOpType
ACT = mybir.ActivationFunctionType
AX = mybir.AxisListType

P = 128
B = 4
L = 512
D = 512
C = 256
FF = 2048
NS = 16
R = 16
TAPS = 4
T = L // P
J = D // P
KC = C // P
FT = FF // P
FC = FF // 512
HALF = 2
W = HALF * L
HN = NS * (J // HALF)
SCANBUFS = 3
DECAYBUFS = 3
RING = 4
PAD = TAPS - 1
LN_EPS = 1e-5
Q_EPS = 1e-5
MAGIC = 1.5 * 2.0 ** 23
SLOTS = 15

PC_CONVW, PC_CONVB, PC_DTB, PC_D, PC_ALOG = 0, TAPS, TAPS + 1, TAPS + 2, TAPS + 3
PC_N = TAPS + 3 + NS

SCAN_SLOTS = {4: (0,), 5: (1, 2), 6: (3, 4), 7: (5, 6), 8: (7, 8), 9: (9, 10), 10: (11, 12), 11: (13, 14), 12: (15,)}
QK_SLOT = 6
ATT_SLOTS = {7: 0, 8: 1, 9: 2, 10: 3}
ATT_LAST_SLOT = 11
ZSTAT_SLOT = 11
ZS_SLOT = 12
GATE_SLOT = 13
QUANT_SLOT = 14
DT_BANKS = (0, 1, 5, 6)
FFN_SLOTS = {6 + i: (2 * i, 2 * i + 1) for i in range(FT // 2)}


class Tally:

    def __init__(self, sem, per):
        self.sem, self.per, self.n = sem, per, 0

    def start(self):
        assert self.n in (0, self.per), (self.n, self.per)
        self.n = 0

    def link(self, eng, b, ins):
        self.n += 1
        ins.then_inc(self.sem, 1)
        eng.wait_ge(self.sem, b * self.per + self.n)


def program(nc, x_d, ctxT_d, ipw_d, xpw_d, dtw_d, pch_d, w1_d, w2_d, wqk_d, bqk_d, ffn_d, b1_d, b2_d, gate_d,
            ident_d, identb_d, pick_d, out_d):
    with ExitStack() as ctx:
        def sb(name, shape, dt=F32):
            return ctx.enter_context(nc.sbuf_tensor(name, shape, dt))

        def sem(name):
            return ctx.enter_context(nc.semaphore(name))

        banks = [ctx.enter_context(nc.psum_tensor(f"bank{i}", [P, 512], F32)) for i in range(8)]

        ident = sb("ident", [P, P])
        identb = sb("identb", [P, P], BF16)
        pick = sb("pick", [P, 2 * NS], BF16)
        ones = sb("ones", [P, P])
        expo = sb("expo", [P, 2])
        ipw = sb("ipw", [P, KC, D])
        xpw = sb("xpw", [P, J, P])
        dtw = sb("dtw", [R, D])
        pch = sb("pch", [P, J, PC_N])
        a_neg = sb("a_neg", [P, J, NS])
        wqk = sb("wqk", [P, KC, 2, P])
        bqk = sb("bqk", [P, 2])
        b1 = sb("b1", [P, FT])
        b2 = sb("b2", [P, D])
        gates = sb("gates", [P, 4])
        w1q = sb("w1q", [P, J, FF], BF16)
        w2q = sb("w2q", [P, FT, D], BF16)
        wsum = sb("wsum", [P, 2])
        wstat = sb("wstat", [P, 2, 4])
        ring = sb("ring", [P, RING, 2 * D])

        ctxT = sb("ctxT", [P, KC, L])
        xres = sb("xres", [P, T, D])
        xpad = sb("xpad", [P, 2, PAD + L])
        u = sb("u", [P, J, L])
        dt = sb("dt", [P, J, L])
        du = sb("du", [P, J, L])
        decay = sb("decay", [P, DECAYBUFS, HALF, L])
        work = sb("work", [P, SCANBUFS, HALF, L])
        bcast = sb("bcast", [P, 2, L])
        ccast = sb("ccast", [P, 2, L])
        xd = sb("xd", [P, L])
        xd3 = sb("xd3", [P, L], BF16)
        sptmp = (work[:, 2, :, :], ccast[:])
        attT = sb("attT", [P, J, D])
        qk = xpad[:, :, PAD:]
        ex = xd
        qT = sb("qT", [P, J, L], BF16)
        zst = sb("zst", [P, J, 12])
        x1n = ccast[:, 0, :]
        q1 = sb("q1", [P, 2, D], BF16)
        mst = sb("mst", [P, T, 16])
        ast = sb("ast", [P, J, 4])

        stage = sb("stage", [P, 4 * FF])
        h = [stage[:, i * FF:(i + 1) * FF] for i in range(2)]
        xb = stage[:, 2 * FF:3 * FF].rearrange("p (t d) -> p t d", t=T)
        xnT = stage[:, 3 * FF:4 * FF].rearrange("p (k l) -> p k l", k=J)
        hq = sb("hq", [P, FF], BF16)
        hqT = sb("hqT", [P, FT, P], BF16)
        xn = sb("xn", [P, 2, D])
        hT = sb("hT", [P, 4, L])
        zs = (xn, qk)
        fst = sb("fst", [P, T, 24])

        bf_bank = [banks[i][:, :].bitcast(BF16) for i in range(8)]

        s_const = sem("s_const")
        s_stage = sem("s_stage")
        s_ctx = sem("s_ctx")
        s_x = sem("s_x")
        s_ring = [sem(f"s_ring{i}") for i in range(RING)]
        s_out = sem("s_out")
        s_stored = sem("s_stored")
        s_ones = sem("s_ones")
        s_aneg = sem("s_aneg")
        s_gates = sem("s_gates")
        s_b2 = sem("s_b2")
        s_wsq = sem("s_wsq")
        s_wmean = sem("s_wmean")
        s_wms = sem("s_wms")
        s_wstat = sem("s_wstat")
        s_wscaled = sem("s_wscaled")
        s_wq = sem("s_wq")
        s_pad = sem("s_pad")
        s_inproj = sem("s_inproj")
        s_inprojc = sem("s_inprojc")
        s_conv = sem("s_conv")
        s_u = sem("s_u")
        s_xdbl = sem("s_xdbl")
        s_xd = sem("s_xd")
        s_split = sem("s_split")
        s_dtmm = sem("s_dtmm")
        s_spabs = sem("s_spabs")
        s_spmax = sem("s_spmax")
        s_spexp = sem("s_spexp")
        s_sptmp = sem("s_sptmp")
        s_spln = sem("s_spln")
        s_log = sem("s_log")
        s_dt = sem("s_dt")
        s_du = sem("s_du")
        s_accin = sem("s_accin")
        s_bc = sem("s_bc")
        s_bcc = sem("s_bcc")
        s_decay = sem("s_decay")
        s_dbu = sem("s_dbu")
        s_dbuP = sem("s_dbuP")
        s_scan = sem("s_scan")
        s_hc = sem("s_hc")
        s_acc = sem("s_acc")
        s_qkmm = sem("s_qkmm")
        s_qk = sem("s_qk")
        s_emm = sem("s_emm")
        s_emax = sem("s_emax")
        s_eexp = sem("s_eexp")
        s_eprob = sem("s_eprob")
        s_eT = sem("s_eT")
        s_att = sem("s_att")
        s_zst = sem("s_zst")
        s_zrs = sem("s_zrs")
        s_zs = sem("s_zs")
        s_y = sem("s_y")
        s_yT = sem("s_yT")
        s_x1 = sem("s_x1")
        s_x1st = sem("s_x1st")
        s_x1rs = sem("s_x1rs")
        s_q1 = sem("s_q1")
        s_q1T = sem("s_q1T")
        s_qT = sem("s_qT")
        s_mm1 = sem("s_mm1")
        s_gelu = sem("s_gelu")
        s_hsc = sem("s_hsc")
        s_hr = sem("s_hr")
        s_hq = sem("s_hq")
        s_hqT = sem("s_hqT")
        s_ev0 = sem("s_ev0")
        s_ev1 = sem("s_ev1")
        s_mm2 = sem("s_mm2")
        s_x2 = sem("s_x2")
        s_lnst = sem("s_lnst")
        s_lnrs = sem("s_lnrs")
        s_xn = sem("s_xn")
        s_xnT = sem("s_xnT")
        s_xnTc = sem("s_xnTc")
        s_xm = sem("s_xm")
        s_x3 = sem("s_x3")
        s_x3b = sem("s_x3b")
        s_fmm1 = sem("s_fmm1")
        s_fgelu = sem("s_fgelu")
        s_fmm2 = sem("s_fmm2")
        s_x4 = sem("s_x4")
        dve_p = Tally(sem("dve_p"), 2 * J + 3 + 2)
        dve_m = Tally(sem("dve_m"), J + J + 6 * T)
        dve_f = Tally(sem("dve_f"), 5 * T)
        pool_s = Tally(sem("pool_s"), 0)
        pool_m = Tally(sem("pool_m"), 2 * J + T)
        pool_f = Tally(sem("pool_f"), 2 * T)
        dve_w = Tally(sem("dve_w"), 0)

        consts = (
            (ipw[:], ipw_d.rearrange("(k p) e -> p k e", p=P)),
            (pch[:], pch_d.rearrange("(j p) c -> p j c", p=P)),
            (xpw[:], xpw_d.rearrange("(k p) e -> p k e", p=P)),
            (gates[:], gate_d), (dtw[:], dtw_d), (pick[:], pick_d), (ident[:], ident_d), (identb[:], identb_d),
            (bqk[:], bqk_d), (b1[:], b1_d), (b2[:], b2_d),
            (wqk[:, :, 0, :], wqk_d[0].rearrange("(k p) e -> p k e", p=P)),
            (wqk[:, :, 1, :], wqk_d[1].rearrange("(k p) e -> p k e", p=P)),
        )
        const_wait = len(consts) * 16

        carried = {e: sem(f"s_carried_{e}") for e in ("dve", "pool")}

        def carry_wait(eng, name):
            eng.sem_inc(carried[name], 1)

        block = ctx.enter_context(nc.Block())

        @block.sync
        def _(sp):
            def load_ring(slot, f):
                sp.dma_start(ring[:, slot, :], ffn_d[f]).then_inc(s_ring[slot], 16)

            sp.dma_start(ctxT[:], ctxT_d[0].rearrange("(k p) l -> p k l", p=P)).then_inc(s_ctx, 16)
            for dst, src in consts:
                sp.dma_start(dst, src).then_inc(s_const, 16)
            sp.dma_start(xres[:], x_d[0].rearrange("(t p) d -> p t d", p=P)).then_inc(s_x, 16)
            sp.dma_start(stage[:].rearrange("p (k f) -> p k f", k=J),
                         w1_d.rearrange("(k p) f -> p k f", p=P)).then_inc(s_stage, 16)
            for f in range(RING):
                load_ring(f, f)
            sp.wait_ge(s_wq, 4)
            sp.dma_start(stage[:].rearrange("p (k f) -> p k f", k=FT),
                         w2_d.rearrange("(k p) f -> p k f", p=P)).then_inc(s_stage, 16)

            def run(b, more):
                if more:
                    sp.wait_ge(s_qkmm, b * 2 + 2)
                    sp.dma_start(ctxT[:], ctxT_d[b + 1].rearrange("(k p) l -> p k l", p=P)).then_inc(s_ctx, 16)
                    sp.wait_ge(s_x2, b * T + T)
                    sp.dma_start(xres[:], x_d[b + 1].rearrange("(t p) d -> p t d", p=P)).then_inc(s_x, 16)
                for f in range(FT):
                    if more or f + RING < FT:
                        sp.wait_ge(s_fmm2, b * FT + f + 1)
                        load_ring(f % RING, (f + RING) % FT)
                for t in range(T):
                    sp.wait_ge(s_x4, b * T + t + 2)
                    sp.dma_start(out_d[b, t * P:(t + 1) * P, :], xb[:, t, :]).then_inc(s_out, 16)
                sp.wait_ge(s_out, (b + 1) * T * 16)
                sp.sem_inc(s_stored, 1)

            sp.sem_inc(s_stored, 1)
            with sp.Fori(0, B - 1) as i:
                run(i, True)
            run(B - 1, False)
            sp.wait_ge(s_out, B * T * 16)

        @block.tensor
        def _(pe):
            def scan_bcast(b, n, i):
                if n == 0 and i == 0:
                    pe.wait_ge(s_split, b + 1)
                    pe.wait_ge(s_spmax, b * J + J)
                else:
                    pe.wait_ge(s_bcc, b * 2 * NS + 2 * n + i)
                pe.matmul(banks[0][:], pick[:, i * NS + n:i * NS + n + 1].broadcast_to([P, P]), xd3[:],
                          start=True, stop=True).then_inc(s_bc, 1)

            def bcast_next(b, slot, which, i):
                if slot in SCAN_SLOTS and which < len(SCAN_SLOTS[slot]) and SCAN_SLOTS[slot][which] + 1 < NS:
                    scan_bcast(b, SCAN_SLOTS[slot][which] + 1, i)

            def att_transpose(b, j):
                pe.wait_ge(s_eprob, b * J + j + 1)
                for k in range(J):
                    last = pe.transpose(banks[1][:, k * P:(k + 1) * P], ex[:, k * P:(k + 1) * P], ident[:])
                last.then_inc(s_eT, 1)

            def prep(b, prev, part):
                if part in (0, 1):
                    if part == 0:
                        pe.wait_ge(s_ctx, b * 16 + 16)
                        if prev is not None:
                            pe.wait_ge(s_x1, prev * T + T)
                    for j in (2 * part, 2 * part + 1):
                        if j >= 2:
                            pe.wait_ge(s_inprojc, b * J + j - 1)
                        elif j == 1 and prev is not None:
                            pe.wait_ge(s_qT, prev * T + T)
                        for k in range(KC):
                            last = pe.matmul(banks[j % 2][:], ipw[:, k, j * P:(j + 1) * P], ctxT[:, k, :],
                                             start=k == 0, stop=k == KC - 1)
                        last.then_inc(s_inproj, 1)
                if part == 2:
                    pe.wait_ge(s_u, b + 1)
                    for j in range(J):
                        last = pe.matmul(banks[0][:], xpw[:, j, :], u[:, j, :], start=j == 0, stop=j == J - 1)
                    last.then_inc(s_xdbl, 1)
                if part == 3:
                    pe.wait_ge(s_xd, b + 1)
                    if prev is not None:
                        pe.wait_ge(s_gelu, prev * T * FC + T * FC)
                    for j in range(J):
                        pe.matmul(banks[DT_BANKS[j]][:], dtw[:, j * P:(j + 1) * P], xd[0:R, :],
                                  start=True, stop=True).then_inc(s_dtmm, 1)

            def qk_products(b, prev, i):
                if i:
                    pe.wait_ge(s_qk, b * 2 + 1)
                for k in range(KC):
                    last = pe.matmul(banks[1][:], wqk[:, k, i, :], ctxT[:, k, :], start=k == 0, stop=k == KC - 1)
                last.then_inc(s_qkmm, 1)

            def energies(b, j):
                if j:
                    pe.wait_ge(s_att, b * J + j)
                else:
                    pe.wait_ge(s_qk, b * 2 + 2)
                pe.matmul(banks[1][:], qk[:, 0, j * P:(j + 1) * P], qk[:, 1, :],
                          start=True, stop=True).then_inc(s_emm, 1)

            def gate_transposes(b, ts):
                for t in ts:
                    if t == 0:
                        pe.wait_ge(s_y, b * 2 + 2)
                        pe.wait_ge(s_att, b * J + J)
                    if t >= 2:
                        pe.wait_ge(s_x1, b * T + t - 1)
                    for j in range(J):
                        last = pe.transpose(banks[(t + 1) % 2][:, j * P:(j + 1) * P], u[:, j, t * P:(t + 1) * P], ident[:])
                    last.then_inc(s_yT, 1)

            def q_transposes(b, ts):
                for t in ts:
                    pe.wait_ge(s_q1, b * T + t + 1)
                    if t:
                        pe.wait_ge(s_qT, b * T + t)
                    else:
                        pe.wait_ge(s_x1, b * T + T - 1)
                    for k in range(J):
                        last = pe.transpose(bf_bank[1][:, k * P:(k + 1) * P], q1[:, t % 2, k * P:(k + 1) * P], identb[:])
                    last.then_inc(s_q1T, 1)

            def up1(b, t):
                pe.wait_ge(s_qT, b * T + t + 1)
                for c in range(FC):
                    g = t * FC + c
                    if g >= 3:
                        pe.wait_ge(s_gelu, b * T * FC + g - 2)
                    elif g == 0:
                        pe.wait_ge(s_x4, b * T + 1)
                    for k in range(J):
                        last = pe.matmul(banks[4 + g % 3][:], qT[:, k, t * P:(t + 1) * P],
                                         w1q[:, k, c * 512:(c + 1) * 512], start=k == 0, stop=k == J - 1)
                    last.then_inc(s_mm1, 1)

            def down1(b, t):
                pe.wait_ge(s_ev0, b * T + t + 1)
                pe.wait_ge(s_ev1, b * T + t + 1)
                if t:
                    pe.wait_ge(s_x2, b * T + t)
                for f in range(FT):
                    last = pe.matmul(banks[7][:], hqT[:, f, :], w2q[:, f, :], start=f == 0, stop=f == FT - 1)
                last.then_inc(s_mm2, 1)

            def transpose_h(b, t):
                pe.wait_ge(s_hq, b * T + t + 1)
                for r in range(2):
                    if r == 0:
                        if t:
                            pe.wait_ge(s_ev0, b * T + t)
                    elif t >= 2:
                        pe.wait_ge(s_xnTc, b * 2 * T + t - 1)
                    elif t:
                        pe.wait_ge(s_ev1, b * T + t)
                    for i in range(FT // 2):
                        f = r * (FT // 2) + i
                        last = pe.transpose(bf_bank[2 + r][:, i * P:(i + 1) * P], hq[:, f * P:(f + 1) * P],
                                            identb[:])
                    last.then_inc(s_hqT, 1)

            def norm_transpose(b, i):
                bank = 3 if i < T else 2 + i % 2
                pe.wait_ge(s_xn, b * 2 * T + i + 1)
                if i < T:
                    pe.wait_ge(s_ev1, b * T + min(i + 2, T))
                if i == T - 1:
                    pe.wait_ge(s_xnTc, b * 2 * T + T - 1)
                if i == T:
                    pe.wait_ge(s_ev0, b * T + T)
                if i > T:
                    pe.wait_ge(s_xnTc, b * 2 * T + i - 1)
                for k in range(J):
                    last = pe.transpose(banks[bank][:, k * P:(k + 1) * P], xn[:, i % 2, k * P:(k + 1) * P], ident[:])
                last.then_inc(s_xnT, 1)

            def attend(b, t):
                pe.wait_ge(s_xnTc, b * 2 * T + t + 1)
                if t == 0:
                    pe.wait_ge(s_gelu, b * T * FC + T * FC)
                    pe.wait_ge(s_att, b * J + J)
                if t == T - 1:
                    pe.wait_ge(s_x2, b * T + T)
                for k in range(J):
                    last = pe.matmul(banks[4 + t][:], xnT[:, k, t * P:(t + 1) * P], attT[:, k, :],
                                     start=k == 0, stop=k == J - 1)
                last.then_inc(s_xm, 1)

            def f_up(b, f):
                if f >= 2:
                    pe.wait_ge(s_fgelu, b * FT + f - 1)
                else:
                    pe.wait_ge(s_xnTc, b * 2 * T + 2 * T)
                pe.wait_ge(s_ring[f % RING], (b * (FT // RING) + f // RING + 1) * 16)
                for k in range(J):
                    last = pe.matmul(banks[2 + f % 2][:], ring[:, f % RING, k * P:(k + 1) * P], xnT[:, k, :],
                                     start=k == 0, stop=k == J - 1)
                last.then_inc(s_fmm1, 1)

            def f_down(b, f):
                if f < 0:
                    return
                pe.wait_ge(s_fgelu, b * FT + f + 1)
                if f == 0:
                    pe.wait_ge(s_x3, b * T + T)
                for t in range(T):
                    last = pe.matmul(banks[4 + t][:], hT[:, f % 4, t * P:(t + 1) * P], ring[:, f % RING, D:2 * D],
                                     start=f == 0, stop=f == FT - 1)
                last.then_inc(s_fmm2, 1)

            def pass_(b, scans, rest=True):
                m, prev = (b + 1, b) if rest else (0, None)
                for slot in range(SLOTS):
                    f0, f1 = FFN_SLOTS.get(slot, (FT, FT + 1))
                    if rest:
                        if slot == 0:
                            up1(b, 0)
                            q_transposes(b, (3,))
                        if 2 <= slot <= 4:
                            norm_transpose(b, slot - 2)
                        if slot == 5:
                            norm_transpose(b, 5)
                        if slot + 1 < T:
                            up1(b, slot + 1)
                        if 2 <= slot <= T:
                            down1(b, slot - 1)
                    if scans:
                        if slot in (0, 1, 3):
                            prep(m, prev, slot)
                        if slot == 4:
                            scan_bcast(m, 0, 1)
                        bcast_next(m, slot, 0, 0)
                        if slot in ATT_SLOTS and ATT_SLOTS[slot]:
                            att_transpose(m, ATT_SLOTS[slot] - 1)
                        if slot == ATT_LAST_SLOT:
                            att_transpose(m, J - 1)
                        if slot == QK_SLOT:
                            qk_products(m, prev, 0)
                    if rest:
                        if slot == 1:
                            down1(b, 0)
                        if slot < T:
                            transpose_h(b, slot)
                        if slot == 3:
                            attend(b, 0)
                        if slot == 4:
                            attend(b, 1)
                            attend(b, 2)
                            norm_transpose(b, 3)
                            attend(b, 3)
                        if slot in FFN_SLOTS:
                            f_up(b, f0)
                    else:
                        weights(slot)
                    if scans:
                        if slot == 2:
                            prep(m, prev, 2)
                        if slot == 3:
                            scan_bcast(m, 0, 0)
                        bcast_next(m, slot, 0, 1)
                        if slot in ATT_SLOTS:
                            energies(m, ATT_SLOTS[slot])
                        if slot == QK_SLOT:
                            qk_products(m, prev, 1)
                        if slot == GATE_SLOT:
                            gate_transposes(m, (0, 1))
                    if rest:
                        if slot == 4:
                            norm_transpose(b, 4)
                        if slot == 5:
                            norm_transpose(b, 6)
                        if slot in FFN_SLOTS:
                            f_up(b, f1)
                    if scans:
                        bcast_next(m, slot, 1, 0)
                        if slot == GATE_SLOT:
                            gate_transposes(m, (2, 3))
                    if rest and slot >= 6:
                        f_down(b, f0 - 2)
                    if scans:
                        bcast_next(m, slot, 1, 1)
                        if slot == QUANT_SLOT:
                            q_transposes(m, (0, 1))
                    if rest:
                        if slot == 5:
                            norm_transpose(b, 7)
                        if slot >= 6:
                            f_down(b, f1 - 2)
                    if scans and slot == QUANT_SLOT:
                        q_transposes(m, (2,))

            def weights(slot):
                if slot == 4:
                    weight_mean(0)
                if slot == 9:
                    weight_mean(1)

            def weight_mean(i):
                pe.wait_ge(s_wsq, i + 1)
                pe.matmul(banks[3][:, i:i + 1], ones[:], wsum[:, i:i + 1], start=True, stop=True).then_inc(s_wmean, 1)

            pe.wait_ge(s_const, const_wait)
            pe.wait_ge(s_ones, 2)
            pass_(None, True, rest=False)
            pe.wait_ge(s_wq, 8)
            with pe.Fori(0, B - 1) as i:
                pass_(i, True)
            pass_(B - 1, False)

        @block.scalar
        def _(act):
            def copy_bc(b, n, i):
                dst = (bcast, ccast)[i]
                act.wait_ge(s_bc, b * 2 * NS + 2 * n + i + 1)
                if n >= 2:
                    if i:
                        act.wait_ge(s_hc, b * HN + 2 * (n - 1))
                    else:
                        act.wait_ge(s_dbu, b * NS + n - 1)
                        act.wait_ge(s_dbuP, b * NS + n - 1)
                act.activation(dst[:, n % 2, :], banks[0][:], ACT.Copy).then_inc(s_bcc, 1)

            def copy_next(b, slot, which, i):
                if slot in SCAN_SLOTS and which < len(SCAN_SLOTS[slot]) and SCAN_SLOTS[slot][which] + 1 < NS:
                    copy_bc(b, SCAN_SLOTS[slot][which] + 1, i)

            def decay_half(b, s):
                if s >= DECAYBUFS:
                    act.wait_ge(s_scan, b * HN + s - DECAYBUFS + 1)
                n, p = divmod(s, 2)
                if n == 0:
                    act.wait_ge(s_dt, b * 2 + p + 1)
                for q in range(HALF):
                    last = act.activation(decay[:, s % DECAYBUFS, q, 1:], dt[:, p * HALF + q, 1:], ACT.Exp,
                                          scale=a_neg[:, p * HALF + q, n:n + 1])
                last.then_inc(s_decay, 1)

            def decays(b, slot, which):
                if slot in SCAN_SLOTS and which < len(SCAN_SLOTS[slot]):
                    n = SCAN_SLOTS[slot][which]
                    if n == 0:
                        decay_half(b, 0)
                    for s in (2 * n + 1, 2 * n + 2):
                        if s < HN:
                            decay_half(b, s)

            def prep(b, prev, part):
                if part in (0, 1):
                    for j in (2 * part, 2 * part + 1):
                        act.wait_ge(s_inproj, b * J + j + 1)
                        if j >= 2:
                            act.wait_ge(s_conv, b * J + j - 1)
                        elif prev is not None and j == 0:
                            act.wait_ge(s_y, prev * 2 + 2)
                            act.wait_ge(s_yT, prev * T + T)
                        act.activation(xpad[:, j % 2, PAD:], banks[j % 2][:], ACT.Copy)
                        act.activation(u[:, j, :], banks[j % 2][:], ACT.Identity, scale=pch[:, j, TAPS - 1:TAPS],
                                       bias=pch[:, j, PC_CONVB:PC_CONVB + 1]).then_inc(s_inprojc, 1)
                if part == 2:
                    act.wait_ge(s_conv, b * J + J)
                    act.activation(u[:], u[:], ACT.Silu).then_inc(s_u, 1)
                if part == 5:
                    act.wait_ge(s_xdbl, b + 1)
                    if prev is not None:
                        act.wait_ge(s_bc, prev * 2 * NS + 2 * NS)
                    act.activation(xd[:], banks[0][:], ACT.Copy)
                    act.activation(xd3[:], banks[0][:], ACT.Copy).then_inc(s_xd, 1)
                if part == 3:
                    if prev is not None:
                        act.wait_ge(s_acc, prev * HN + HN)
                    for j in range(J):
                        act.wait_ge(s_dtmm, b * J + j + 1)
                        act.activation(du[:, j, :], banks[DT_BANKS[j]][:], ACT.Abs,
                                       bias=pch[:, j, PC_DTB:PC_DTB + 1]).then_inc(s_spabs, 1)
                if part == 4:
                    for p in range(2):
                        js = slice(p * HALF, (p + 1) * HALF)
                        act.wait_ge(s_spabs, b * J + (p + 1) * HALF)
                        act.activation(work[:, p, :, :], du[:, js, :], ACT.Exp, scale=-1.0).then_inc(s_spexp, 1)
                    for p in range(2):
                        js = slice(p * HALF, (p + 1) * HALF)
                        act.wait_ge(s_spexp, b * 2 + p + 1)
                        act.activation(du[:, js, :], work[:, p, :, :], ACT.Ln, bias=1.0).then_inc(s_spln, 1)
                if part == 6:
                    if prev is not None:
                        act.wait_ge(s_dbu, prev * NS + NS)
                        act.wait_ge(s_dbuP, prev * NS + NS)
                    copy_bc(b, 0, 0)
                if part == 7:
                    act.wait_ge(s_dt, b * 2 + 2)
                    copy_bc(b, 0, 1)

            def att_copy(b, prev, j):
                act.wait_ge(s_eT, b * J + j + 1)
                if prev is not None:
                    act.wait_ge(s_xm, prev * T + T)
                act.activation(attT[:, :, j * P:(j + 1) * P], banks[1][:].rearrange("p (k m) -> p k m", k=J),
                               ACT.Copy).then_inc(s_att, 1)

            def qk_copy(b, prev, i):
                act.wait_ge(s_qkmm, b * 2 + i + 1)
                act.activation(qk[:, i, :], banks[1][:], ACT.Identity, bias=bqk[:, i:i + 1]).then_inc(s_qk, 1)

            def energy_exp(b, j):
                act.wait_ge(s_emax, b * J + j + 1)
                if j:
                    act.wait_ge(s_eT, b * J + j)
                act.activation(ex[:], banks[1][:], ACT.Exp, bias=ast[:, j, 0:1],
                               accum_out=ast[:, j, 1:2]).then_inc(s_eexp, 1)

            def gates_silu(b):
                act.wait_ge(s_emm, b * J + J)
                for j in range(J):
                    act.wait_ge(s_zrs, b * J + j + 1)
                    act.activation(zs[j // HALF][:, j % HALF, :], xres[:, j, :], ACT.Silu, scale=zst[:, j, 9:10],
                                   bias=zst[:, j, 10:11]).then_inc(s_zs, 1)

            def q_copy(b, ts):
                for t in ts:
                    act.wait_ge(s_q1T, b * T + t + 1)
                    act.activation(qT[:, :, t * P:(t + 1) * P],
                                   bf_bank[1][:, 0:J * P].rearrange("p (k l) -> p k l", k=J),
                                   ACT.Copy).then_inc(s_qT, 1)

            def gelu1(b, t):
                for c in range(FC):
                    g = t * FC + c
                    act.wait_ge(s_mm1, b * T * FC + g + 1)
                    if c == 0 and t >= 2:
                        act.wait_ge(s_hq, b * T + t - 1)
                    act.activation(h[t % 2][:, c * 512:(c + 1) * 512], banks[4 + g % 3][:], ACT.Gelu,
                                   scale=mst[:, t, 13:14]).then_inc(s_gelu, 1)

            def norm_copy(b, i):
                act.wait_ge(s_xnT, b * 2 * T + i + 1)
                t = i % T
                if i >= T:
                    act.wait_ge(s_xm, b * T + t + 1)
                bank = 3 if i < T else 2 + i % 2
                act.activation(xnT[:, :, t * P:(t + 1) * P], banks[bank][:].rearrange("p (k l) -> p k l", k=J),
                               ACT.Copy).then_inc(s_xnTc, 1)

            def h_copy(b, t):
                act.wait_ge(s_hqT, b * 2 * T + 2 * t + 1)
                if t:
                    act.wait_ge(s_mm2, b * T + t)
                act.activation(hqT[:, 0:FT // 2, :], bf_bank[2].rearrange("p (f l) -> p f l", l=P),
                               ACT.Copy).then_inc(s_ev0, 1)
                act.wait_ge(s_hqT, b * 2 * T + 2 * t + 2)
                act.activation(hqT[:, FT // 2:, :], bf_bank[3].rearrange("p (f l) -> p f l", l=P),
                               ACT.Copy).then_inc(s_ev1, 1)

            def f_gelu(b, f):
                act.wait_ge(s_fmm1, b * FT + f + 1)
                if f >= 4:
                    act.wait_ge(s_fmm2, b * FT + f - 3)
                act.activation(hT[:, f % 4, :], banks[2 + f % 2][:], ACT.Gelu, bias=b1[:, f:f + 1]).then_inc(s_fgelu, 1)

            def pass_(b, scans, rest=True):
                m, prev = (b + 1, b) if rest else (0, None)
                for slot in range(SLOTS):
                    if rest:
                        if slot == 0:
                            gelu1(b, 0)
                            q_copy(b, (3,))
                        if 2 <= slot <= 4:
                            norm_copy(b, slot - 2)
                        if slot == 5:
                            norm_copy(b, 5)
                        if slot + 1 < T:
                            gelu1(b, slot + 1)
                    if scans:
                        if slot < T:
                            prep(m, prev, slot)
                        if slot == 4:
                            prep(m, prev, 7)
                        copy_next(m, slot, 0, 0)
                        if slot in ATT_SLOTS and ATT_SLOTS[slot]:
                            att_copy(m, prev, ATT_SLOTS[slot] - 1)
                        if slot == ATT_LAST_SLOT:
                            att_copy(m, prev, J - 1)
                        decays(m, slot, 0)
                        if slot == QK_SLOT:
                            qk_copy(m, prev, 0)
                    if rest:
                        if slot < T:
                            h_copy(b, slot)
                        if slot == 4:
                            norm_copy(b, 3)
                    else:
                        weights(slot)
                    if scans:
                        if slot == 2:
                            prep(m, prev, 5)
                        if slot == 3:
                            prep(m, prev, 4)
                            prep(m, prev, 6)
                        copy_next(m, slot, 0, 1)
                        if slot in ATT_SLOTS:
                            energy_exp(m, ATT_SLOTS[slot])
                        if slot == QK_SLOT:
                            qk_copy(m, prev, 1)
                    if rest:
                        if slot == 4:
                            norm_copy(b, 4)
                        if slot == 5:
                            norm_copy(b, 6)
                        if slot in FFN_SLOTS:
                            for f in FFN_SLOTS[slot]:
                                f_gelu(b, f)
                    if scans:
                        copy_next(m, slot, 1, 0)
                        decays(m, slot, 1)
                        if slot == ZS_SLOT:
                            gates_silu(m)
                        copy_next(m, slot, 1, 1)
                        if slot == QUANT_SLOT:
                            q_copy(m, (0, 1, 2))
                    if rest and slot == 5:
                        norm_copy(b, 7)

            def weights(slot):
                if slot == 4:
                    square(0, w1q[:].rearrange("p a b -> p (a b)"))
                if 5 <= slot < 7:
                    quantise(0, 2 * (slot - 5))
                    quantise(0, 2 * (slot - 5) + 1)
                if slot == 9:
                    square(1, w2q[:].rearrange("p a b -> p (a b)"))
                if 10 <= slot < 14:
                    quantise(1, slot - 10)

            act.wait_ge(s_const, const_wait)
            act.activation(gates[:], gates[:], ACT.Tanh).then_inc(s_gates, 1)
            act.activation(a_neg[:], pch[:, :, PC_ALOG:], ACT.Exp).then_inc(s_aneg, 1)
            act.wait_ge(s_aneg, 1)
            act.activation(a_neg[:], a_neg[:], ACT.Copy, scale=-1.0).then_inc(s_aneg, 1)
            act.wait_ge(s_aneg, 2)
            act.wait_ge(s_gates, 1)

            def square(i, junk):
                act.wait_ge(s_stage, 16 * (i + 1))
                act.activation(junk, stage[:], ACT.Square, accum_out=wsum[:, i:i + 1]).then_inc(s_wsq, 1)
                act.wait_ge(s_wsq, i + 1)

            def quantise(i, c):
                dst = (w1q if i == 0 else w2q)[:].rearrange("p a b -> p (a b)")
                act.wait_ge(s_wscaled, 4 * i + c + 1)
                act.activation(dst[:, c * FF:(c + 1) * FF], stage[:, c * FF:(c + 1) * FF], ACT.Copy,
                               bias=-MAGIC).then_inc(s_wq, 1)

            pass_(None, True, rest=False)
            with act.Fori(0, B - 1) as i:
                pass_(i, True)
            pass_(B - 1, False)

        @block.vector
        def _(dve):
            def half_step(b, n, p):
                s = 2 * n + p
                js = slice(p * HALF, (p + 1) * HALF)
                w3 = work[:, s % SCANBUFS, :, :]
                flat = w3.rearrange("p a l -> p (a l)")
                if p == 0:
                    dve.wait_ge(s_bcc, b * 2 * NS + 2 * n + 1)
                    if s >= SCANBUFS:
                        dve.wait_ge(s_acc, b * HN + s - SCANBUFS + 1)
                    dve.tensor_tensor(w3, du[:, js, :], bcast[:, n % 2, :].unsqueeze(1).broadcast_to([P, HALF, L]),
                                      ALU.mult).then_inc(s_dbu, 1)
                    dve.wait_ge(s_dbu, b * NS + n + 1)
                else:
                    dve.wait_ge(s_dbuP, b * NS + n + 1)
                dve.wait_ge(s_decay, b * HN + s + 1)
                dve.tensor_tensor_scan(flat, decay[:, s % DECAYBUFS, :, :].rearrange("p a l -> p (a l)"), flat, 0.0,
                                       ALU.mult, ALU.add).then_inc(s_scan, 1)
                dve.wait_ge(s_scan, b * HN + s + 1)
                dve.wait_ge(s_bcc, b * 2 * NS + 2 * n + 2)
                dve.tensor_tensor(w3, w3, ccast[:, n % 2, :].unsqueeze(1).broadcast_to([P, HALF, L]),
                                  ALU.mult).then_inc(s_hc, 1)

            def prep(b, prev, part):
                if part == 0:
                    dve_p.start()
                if part in (0, 1):
                    for j in (2 * part, 2 * part + 1):
                        dve.wait_ge(s_inprojc, b * J + j + 1)
                        for k in range(TAPS - 1):
                            ins = dve.scalar_tensor_tensor(u[:, j, :], xpad[:, j % 2, k:k + L], pch[:, j, k:k + 1],
                                                           u[:, j, :], ALU.mult, ALU.add)
                            if k < TAPS - 2:
                                dve_p.link(dve, b, ins)
                            else:
                                ins.then_inc(s_conv, 1)
                if part == 2:
                    dve.wait_ge(s_xd, b + 1)
                    tmp = x1n
                    dve_p.link(dve, b, dve.tensor_tensor(tmp, xd[:], xd3[:], ALU.subtract))
                    dve_p.link(dve, b, dve.tensor_copy(xd3[64:128, :], tmp[64:128, :]))
                    dve_p.link(dve, b, dve.tensor_tensor(tmp[96:128, :], tmp[96:128, :], xd3[96:128, :], ALU.subtract))
                    dve.tensor_copy(xd3[96:128, :], tmp[96:128, :]).then_inc(s_split, 1)
                if part == 3:
                    for j in range(J):
                        dve.wait_ge(s_spabs, b * J + j + 1)
                        dve.tensor_scalar(dt[:, j, :], banks[DT_BANKS[j]][:], pch[:, j, PC_DTB:PC_DTB + 1], 0.0,
                                          ALU.add, ALU.max).then_inc(s_spmax, 1)
                if part == 4:
                    for p in range(2):
                        dve.wait_ge(s_spexp, b * 2 + p + 1)
                        if p:
                            dve.wait_ge(s_split, b + 1)
                        dve.tensor_scalar(sptmp[p], work[:, p, :, :], 1.0, -1.0, ALU.add, ALU.add).then_inc(s_sptmp, 1)
                if part == 5:
                    for p in range(2):
                        js = slice(p * HALF, (p + 1) * HALF)
                        dve.wait_ge(s_log, b * 2 + p + 1)
                        dve.wait_ge(s_spln, b * 2 + p + 1)
                        dve_p.link(dve, b, dve.tensor_tensor(sptmp[p], sptmp[p], du[:, js, :], ALU.add))
                        dve.tensor_tensor(dt[:, js, :], dt[:, js, :], sptmp[p], ALU.add).then_inc(s_dt, 1)
                        dve.wait_ge(s_dt, b * 2 + p + 1)
                        dve.tensor_tensor(du[:, js, :], dt[:, js, :], u[:, js, :], ALU.mult).then_inc(s_du, 1)

            def half(b, slot, which, p):
                if slot in SCAN_SLOTS and which < len(SCAN_SLOTS[slot]):
                    half_step(b, SCAN_SLOTS[slot][which], p)

            def energy_max(b, slot):
                if slot in ATT_SLOTS:
                    j = ATT_SLOTS[slot]
                    dve.wait_ge(s_emm, b * J + j + 1)
                    dve.tensor_reduce(ast[:, j, 0:1], banks[1][:], AX.X, ALU.max, negate=True).then_inc(s_emax, 1)

            def mixer_last(b, prev, slot):
                if slot == ZSTAT_SLOT:
                    dve.wait_ge(s_x, b * 16 + 16)
                    for j in range(J):
                        dve_m.link(dve, b, dve.bn_stats(zst[:, j, 0:6], xres[:, j, :]))
                        carry_wait(dve, "dve")
                        dve.bn_aggr(zst[:, j, 6:8], zst[:, j, 0:6]).then_inc(s_zst, 1)
                if slot in ATT_SLOTS:
                    att_probs(b, slot)
                if slot == GATE_SLOT:
                    for p in range(2):
                        js = slice(p * HALF, (p + 1) * HALF)
                        dve.wait_ge(s_zs, b * J + (p + 1) * HALF)
                        dve.wait_ge(s_acc, b * HN + HN - 1 + p)
                        dve.tensor_tensor(u[:, js, :], u[:, js, :], zs[p][:, :, :], ALU.mult).then_inc(s_y, 1)
                    for t in range(T):
                        first_sum(b, t)
                        if t == T - 2:
                            quantise(b, 0)
                if slot == QUANT_SLOT:
                    quantise(b, 1)

            def first_sum(b, t):
                dve.wait_ge(s_yT, b * T + t + 1)
                dve.scalar_tensor_tensor(xres[:, t, :], banks[(t + 1) % 2][:], gates[:, 0:1], xres[:, t, :],
                                         ALU.mult, ALU.add).then_inc(s_x1, 1)
                dve.wait_ge(s_x1, b * T + t + 1)
                dve_m.link(dve, b, dve.bn_stats(mst[:, t, 0:6], xres[:, t, :]))
                carry_wait(dve, "dve")
                dve.bn_aggr(mst[:, t, 6:8], mst[:, t, 0:6]).then_inc(s_x1st, 1)

            def quantise(b, t):
                st = mst[:, t, :]
                dve.wait_ge(s_x1rs, b * T + t + 1)
                if t:
                    dve.wait_ge(s_q1, b * T + t)
                dve_m.link(dve, b, dve.tensor_scalar(x1n, xres[:, t, :], st[:, 6:7], st[:, 9:10],
                                                     ALU.subtract, ALU.mult))
                dve_m.link(dve, b, dve.tensor_reduce(st[:, 10:11], x1n, AX.X, ALU.max, apply_absolute_value=True))
                dve_m.link(dve, b, dve.tensor_scalar(st[:, 11:12], st[:, 10:11], Q_EPS, 1.0 / 127.0,
                                                     ALU.max, ALU.mult))
                dve_m.link(dve, b, dve.reciprocal(st[:, 12:13], st[:, 11:12]))
                dve.tensor_scalar(st[:, 13:14], st[:, 11:12], wstat[:, 0, 2:3], None, ALU.mult)
                dve_m.link(dve, b, dve.tensor_scalar(x1n, x1n, st[:, 12:13], MAGIC, ALU.mult, ALU.add))
                if t >= 2:
                    dve.wait_ge(s_q1T, b * T + t - 1)
                dve.tensor_scalar(q1[:, t % 2, :], x1n, MAGIC, 127.0, ALU.subtract, ALU.min).then_inc(s_q1, 1)

            def att_probs(b, slot):
                j = ATT_SLOTS[slot]
                dve.wait_ge(s_eexp, b * J + j + 1)
                dve_m.link(dve, b, dve.reciprocal(ast[:, j, 2:3], ast[:, j, 1:2]))
                dve.tensor_scalar(ex[:], ex[:], ast[:, j, 2:3], None, ALU.mult).then_inc(s_eprob, 1)

            def norm(b, i):
                t = i % T
                st = fst[:, t, 8:18]
                dve_f.link(dve, b, dve.bn_stats(st[:, 0:6], xb[:, t, :]))
                carry_wait(dve, "dve")
                dve.bn_aggr(st[:, 6:8], st[:, 0:6]).then_inc(s_lnst, 1)

            def norm_apply(b, i):
                t = i % T
                st = fst[:, t, 8:18]
                dve.wait_ge(s_lnrs, b * 2 * T + i + 1)
                if i >= 2:
                    dve.wait_ge(s_xnT, b * 2 * T + i - 1)
                dve.tensor_scalar(xn[:, i % 2, :], xb[:, t, :], st[:, 6:7], st[:, 9:10],
                                  ALU.subtract, ALU.mult).then_inc(s_xn, 1)

            def h_scale(b, t):
                st = fst[:, t, :]
                dve.wait_ge(s_gelu, b * T * FC + (t + 1) * FC)
                dve_f.link(dve, b, dve.tensor_reduce(st[:, 0:1], h[t % 2], AX.X, ALU.max, apply_absolute_value=True))
                dve_f.link(dve, b, dve.tensor_scalar(st[:, 1:2], st[:, 0:1], Q_EPS, 1.0 / 127.0, ALU.max, ALU.mult))
                dve.reciprocal(st[:, 2:3], st[:, 1:2]).then_inc(s_hsc, 1)

            def h_quant(b, t):
                dve.wait_ge(s_hr, b * T + t + 1)
                if t:
                    dve.wait_ge(s_hqT, b * 2 * T + 2 * t)
                dve.tensor_scalar(hq[:], h[t % 2], MAGIC, 127.0, ALU.subtract, ALU.min).then_inc(s_hq, 1)

            def second(b, t):
                st = fst[:, t, :]
                dve_f.link(dve, b, dve.tensor_scalar(st[:, 4:5], st[:, 1:2], wstat[:, 1, 3:4], None, ALU.mult))
                dve.wait_ge(s_mm2, b * T + t + 1)
                if t == 0:
                    dve.wait_ge(s_stored, b + 1)
                dve.scalar_tensor_tensor(xb[:, t, :], banks[7][:], st[:, 4:5], xres[:, t, :],
                                         ALU.mult, ALU.add).then_inc(s_x2, 1)
                dve.wait_ge(s_x2, b * T + t + 1)
                norm(b, t)

            def third(b, t):
                dve.wait_ge(s_xm, b * T + t + 1)
                dve.scalar_tensor_tensor(xb[:, t, :], banks[4 + t][:], gates[:, 1:2], xb[:, t, :],
                                         ALU.mult, ALU.add).then_inc(s_x3, 1)
                dve.wait_ge(s_x3, b * T + t + 1)
                norm(b, T + t)

            def fourth(b):
                dve.wait_ge(s_fmm2, b * FT + FT)
                dve.wait_ge(s_x3b, b * T + T)
                for t in range(T):
                    dve.scalar_tensor_tensor(xb[:, t, :], banks[4 + t][:], gates[:, 3:4], xb[:, t, :],
                                             ALU.mult, ALU.add).then_inc(s_x4, 1)

            dve.memset(ones[:], 1.0).then_inc(s_ones, 1)
            dve.memset(xpad[:, :, 0:PAD], 0.0).then_inc(s_pad, 1)
            dve.sem_inc(s_x4, 1)
            dve.memset(decay[:, :, :, 0:1], 0.0).then_inc(s_pad, 1)
            dve.wait_ge(s_pad, 2)
            dve.wait_ge(s_const, const_wait)
            dve.wait_ge(s_gates, 1)
            dve.tensor_scalar(b2[:], b2[:], gates[:, 3:4], None, ALU.mult).then_inc(s_b2, 1)

            def weight_scale(i, c):
                w = stage[:, c * FF:(c + 1) * FF]
                dve.wait_ge(s_wstat, i + 1)
                dve_w.link(dve, 0, dve.tensor_scalar(w, w, wstat[:, i, 1:2], 1.0, ALU.mult, ALU.min))
                dve.tensor_scalar(w, w, -1.0, MAGIC, ALU.max, ALU.add).then_inc(s_wscaled, 1)

            def weight_mean(i):
                dve.wait_ge(s_wmean, i + 1)
                dve.tensor_scalar(wstat[:, i, 0:1], banks[3][:, i:i + 1], 1.0 / (FF * D), Q_EPS,
                                  ALU.mult, ALU.max).then_inc(s_wms, 1)

            def weights(slot):
                if slot == 4:
                    weight_mean(0)
                if 5 <= slot < 7:
                    weight_scale(0, 2 * (slot - 5))
                    weight_scale(0, 2 * (slot - 5) + 1)
                if slot == 9:
                    weight_mean(1)
                if 10 <= slot < 14:
                    weight_scale(1, slot - 10)

            def pass_(b, scans, rest=True):
                m, prev = (b + 1, b) if rest else (0, None)
                if rest:
                    dve_f.start()
                if scans:
                    dve_m.start()
                for slot in range(SLOTS):
                    if rest:
                        if slot < T:
                            h_scale(b, slot)
                        if slot == 4:
                            second(b, 3)
                            third(b, 0)
                        if slot == 5:
                            norm_apply(b, 5)
                            third(b, 3)
                    if scans:
                        if slot == 3:
                            prep(m, prev, 3)
                        half(m, slot, 0, 0)
                    if rest:
                        if slot < T:
                            h_quant(b, slot)
                            if slot:
                                second(b, slot - 1)
                        if slot == 4:
                            norm_apply(b, 3)
                            third(b, 1)
                        if slot == 5:
                            norm_apply(b, 6)
                    else:
                        weights(slot)
                    if scans:
                        if slot < 3:
                            prep(m, prev, slot)
                        if slot == 3:
                            prep(m, prev, 4)
                        half(m, slot, 0, 1)
                        energy_max(m, slot)
                    if rest:
                        if 1 <= slot < T:
                            norm_apply(b, slot - 1)
                        if slot == 4:
                            norm_apply(b, 4)
                            third(b, 2)
                        if slot == 5:
                            norm_apply(b, 7)
                    if scans:
                        if slot == 3:
                            prep(m, prev, 5)
                        half(m, slot, 1, 0)
                        half(m, slot, 1, 1)
                        mixer_last(m, prev, slot)
                    if rest and slot == SLOTS - 1:
                        fourth(b)
                    if scans and slot == QUANT_SLOT:
                        quantise(m, 2)
                        quantise(m, 3)

            pass_(None, True, rest=False)
            with dve.Fori(0, B - 1) as i:
                pass_(i, True)
            pass_(B - 1, False)

        @block.gpsimd
        def _(pool):
            def prep(b, part):
                if part == 4:
                    for p in range(2):
                        pool.wait_ge(s_sptmp, b * 2 + p + 1)
                        pool.tensor_tensor(sptmp[p], work[:, p, :, :], sptmp[p], ALU.subtract).then_inc(s_log, 1)
                if part == 5:
                    for j in range(J):
                        if j % HALF == 0:
                            pool.wait_ge(s_du, b * 2 + j // HALF + 1)
                        carry_wait(pool, "pool")
                        pool.tensor_scalar(u[:, j, :], u[:, j, :], pch[:, j, PC_D:PC_D + 1], 1.0,
                                           ALU.mult, ALU.mult).then_inc(s_accin, 1)
                    pool.wait_ge(s_accin, b * J + J)
                    state_input(b, 0)

            def rsqrt(tally, b, tmp, var, eps, out, last=None):
                carry_wait(pool, "pool")
                tally.link(pool, b, pool.tensor_scalar(tmp, var, eps, 1.0, ALU.add, ALU.mult))
                ins = pool.tensor_tensor(out, tmp, expo[:, 0:1], ALU.pow)
                if last is None:
                    tally.link(pool, b, ins)
                else:
                    ins.then_inc(last, 1)

            def state_input(b, n):
                s = 2 * n + 1
                pool.wait_ge(s_bcc, b * 2 * NS + 2 * n + 1)
                if s >= SCANBUFS:
                    pool.wait_ge(s_acc, b * HN + s - SCANBUFS + 1)
                pool.tensor_tensor(work[:, s % SCANBUFS, :, :], du[:, HALF:, :],
                                   bcast[:, n % 2, :].unsqueeze(1).broadcast_to([P, HALF, L]), ALU.mult)\
                    .then_inc(s_dbuP, 1)

            def accumulate(b, n, p):
                s = 2 * n + p
                js = slice(p * HALF, (p + 1) * HALF)
                pool.wait_ge(s_hc, b * HN + s + 1)
                if s >= 2:
                    pool.wait_ge(s_acc, b * HN + s - 1)
                pool.tensor_tensor(u[:, js, :], u[:, js, :], work[:, s % SCANBUFS, :, :], ALU.add).then_inc(s_acc, 1)

            def half(b, slot, which, p):
                if slot in SCAN_SLOTS and which < len(SCAN_SLOTS[slot]):
                    n = SCAN_SLOTS[slot][which]
                    accumulate(b, n, p)
                    if p == 0 and n + 1 < NS:
                        state_input(b, n + 1)

            def mixer_last(b, slot):
                if slot == ZSTAT_SLOT:
                    for j in range(J):
                        st = zst[:, j, :]
                        pool.wait_ge(s_zst, b * J + j + 1)
                        rsqrt(pool_m, b, st[:, 8:9], st[:, 7:8], LN_EPS, st[:, 9:10])
                        carry_wait(pool, "pool")
                        pool.tensor_scalar(st[:, 10:11], st[:, 6:7], st[:, 9:10], -1.0, ALU.mult,
                                           ALU.mult).then_inc(s_zrs, 1)
                if slot == GATE_SLOT:
                    for t in range(T):
                        st = mst[:, t, :]
                        pool.wait_ge(s_x1st, b * T + t + 1)
                        rsqrt(pool_m, b, st[:, 8:9], st[:, 7:8], LN_EPS, st[:, 9:10], s_x1rs)

            def norm(b, i):
                st = fst[:, i % T, 8:18]
                pool.wait_ge(s_lnst, b * 2 * T + i + 1)
                rsqrt(pool_f, b, st[:, 8:9], st[:, 7:8], LN_EPS, st[:, 9:10], s_lnrs)

            def h_round(b, t):
                pool.wait_ge(s_hsc, b * T + t + 1)
                carry_wait(pool, "pool")
                pool.tensor_scalar(h[t % 2], h[t % 2], fst[:, t, 2:3], MAGIC, ALU.mult, ALU.add).then_inc(s_hr, 1)

            def bias(b, t):
                pool.wait_ge(s_xn, b * 2 * T + T + t + 1)
                if t == 0:
                    pool.wait_ge(s_b2, 1)
                pool.tensor_tensor(xb[:, t, :], xb[:, t, :], b2[:], ALU.add).then_inc(s_x3b, 1)

            pool.memset(expo[:, 0:1], -0.5).then_inc(pool_s.sem, 1)
            pool.memset(expo[:, 1:2], 0.5).then_inc(s_ones, 1)
            pool.wait_ge(pool_s.sem, 1)
            pool.wait_ge(s_ones, 2)
            pool_s.n = 1
            pool.wait_ge(s_const, const_wait)

            def weight_rms(i):
                st = wstat[:, i, :]
                pool.wait_ge(s_wms, i + 1)
                pool_s.link(pool, 0, pool.tensor_tensor(st[:, 1:2], st[:, 0:1], expo[:, 0:1], ALU.pow))
                pool_s.link(pool, 0, pool.tensor_tensor(st[:, 2:3], st[:, 0:1], expo[:, 1:2], ALU.pow))
                if i == 0:
                    pool.sem_inc(s_wstat, 1)
                else:
                    pool.wait_ge(s_gates, 1)
                    carry_wait(pool, "pool")
                    pool.tensor_scalar(st[:, 3:4], st[:, 2:3], 1.0, gates[:, 2:3], ALU.mult, ALU.mult)\
                        .then_inc(s_wstat, 1)

            def weights(slot):
                if slot == 4:
                    weight_rms(0)
                if slot == 9:
                    weight_rms(1)

            def pass_(b, scans, rest=True):
                m = b + 1 if rest else 0
                if rest:
                    pool_f.start()
                if scans:
                    pool_m.start()
                for slot in range(SLOTS):
                    if rest:
                        if slot < T:
                            h_round(b, slot)
                        if slot == 4:
                            norm(b, 3)
                            norm(b, 4)
                        if slot == 5:
                            norm(b, 7)
                            bias(b, 1)
                    else:
                        weights(slot)
                    if scans:
                        half(m, slot, 0, 0)
                    if rest:
                        if 1 <= slot < T:
                            norm(b, slot - 1)
                        if slot == 4:
                            norm(b, 5)
                        if slot == 5:
                            bias(b, 2)
                    if scans:
                        if slot == 3:
                            prep(m, 4)
                            prep(m, 5)
                        half(m, slot, 0, 1)
                    if rest:
                        if slot == 4:
                            norm(b, 6)
                            bias(b, 0)
                        if slot == 5:
                            bias(b, 3)
                    if scans:
                        half(m, slot, 1, 0)
                        half(m, slot, 1, 1)
                        mixer_last(m, slot)

            pass_(None, True, rest=False)
            with pool.Fori(0, B - 1) as i:
                pass_(i, True)
            pass_(B - 1, False)


def kernel(x, ctx_1024, g_xattn, g_ffn, L0_xattn_in_proj_w, L0_xattn_conv_w, L0_xattn_conv_b, L0_xattn_x_proj_w,
           L0_xattn_dt_proj_w, L0_xattn_dt_proj_b, L0_xattn_A_log, L0_xattn_D, L0_ffn_w1, L0_ffn_w2, L1_xattn_Wq,
           L1_xattn_bq, L1_xattn_Wk, L1_xattn_bk, L1_ffn_proj1, L1_ffn_proj1_bias, L1_ffn_proj2, L1_ffn_proj2_bias,
           L1_ffn_gate_w):
    import ml_dtypes

    import concourse.bacc as bacc
    from concourse.bass_utils import run_bass_kernel_spmd

    g_x, g_f = np.asarray(g_xattn), np.asarray(g_ffn)
    xp = np.asarray(L0_xattn_x_proj_w)
    rank, rest = xp[:R].T, xp[R:].T
    p1, p2 = np.asarray(L1_ffn_proj1), np.asarray(L1_ffn_proj2)
    up = p1.reshape(FT, P, J, P).transpose(0, 3, 2, 1).reshape(FT, P, D)
    down = p2.reshape(D, FT, P).transpose(1, 2, 0)
    identity = np.eye(P, dtype=np.float32)
    part = np.arange(P)[:, None]
    pick = ((part % (2 * NS) == np.arange(2 * NS)[None, :]) & (part >= 2 * NS)).astype(ml_dtypes.bfloat16)
    arrays = {
        "x": x,
        "ctxT": np.asarray(ctx_1024).transpose(0, 2, 1),
        "in_proj": np.asarray(L0_xattn_in_proj_w).T,
        "x_proj": np.concatenate([rank, rank, rest, rest, rest], axis=1),
        "dt_proj": np.asarray(L0_xattn_dt_proj_w).T,
        "channels": np.concatenate([np.asarray(L0_xattn_conv_w)[:, 0, :], np.asarray(L0_xattn_conv_b)[:, None],
                                    np.asarray(L0_xattn_dt_proj_b)[:, None], np.asarray(L0_xattn_D)[:, None],
                                    np.asarray(L0_xattn_A_log)], axis=1),
        "w1": np.asarray(L0_ffn_w1).T,
        "w2": np.asarray(L0_ffn_w2).T,
        "wqk": np.stack([np.asarray(L1_xattn_Wq).T, np.asarray(L1_xattn_Wk).T]),
        "bqk": np.stack([np.asarray(L1_xattn_bq), np.asarray(L1_xattn_bk)], axis=1),
        "ffn": np.concatenate([up, down], axis=2),
        "b1": np.asarray(L1_ffn_proj1_bias).reshape(FT, P).T,
        "b2": np.broadcast_to(np.asarray(L1_ffn_proj2_bias), (P, D)),
        "gates": np.broadcast_to(np.stack([g_x[0], g_x[1], g_f[0], g_f[1]]), (P, 4)),
        "ident": identity,
        "identb": identity.astype(ml_dtypes.bfloat16),
        "pick": pick,
    }
    arrays = {f"{name}_dram": np.ascontiguousarray(a) for name, a in arrays.items()}
    nc = bacc.Bacc("TRN2", target_bir_lowering=False, num_devices=1)
    args = [nc.dram_tensor(name, a.shape, mybir.dt.from_np(a.dtype), kind="ExternalInput").ap()
            for name, a in arrays.items()]
    out = nc.dram_tensor("out_dram", (B, L, D), F32, kind="ExternalOutput").ap()
    program(nc, *args, out)
    got = run_bass_kernel_spmd(nc, [arrays], core_ids=[0])
    return got.results[0]["out_dram"]
```

```python
from contextlib import ExitStack

import numpy as np

import concourse.bass as bass
from concourse import mybir

F32 = mybir.dt.float32
BF16 = mybir.dt.bfloat16
F32R = mybir.dt.float32r
ALU = mybir.AluOpType
ACT = mybir.ActivationFunctionType
AX = mybir.AxisListType

P = 128
B = 4
L = 512
D = 512
C = 256
FF = 2048
NS = 16
R = 16
TAPS = 4
T = L // P
J = D // P
KC = C // P
FT = FF // P
FC = FF // 512
HALF = 2
HN = NS * (J // HALF)
SCANBUFS = 3
DECAYBUFS = 3
RING = 4
PAD = TAPS - 1
LN_EPS = 1e-5
Q_EPS = 1e-5
MAGIC = 1.5 * 2.0 ** 23
SLOTS = 15

PC_CONVW, PC_CONVB, PC_DTB, PC_D, PC_ALOG = 0, TAPS, TAPS + 1, TAPS + 2, TAPS + 3
PC_N = TAPS + 3 + NS

SCAN_SLOTS = {4: (0, None), 5: (1, 2), 6: (3, 4), 7: (5, 6), 8: (7, 8), 9: (9, 10), 10: (11, 12), 11: (13, 14), 12: (15, None)}
QK_SLOT = 5
ATT_SLOTS = {6: 0, 7: 1, 8: 2, 9: 3}
ATT_LAST_SLOT = 10
ZSTAT_SLOT = 10
ZS_SLOT = 12
GATE_SLOT = 13
QUANT_SLOT = 14
W_SQUARE = {3: (0, (0, 1)), 4: (0, (2, 3)), 9: (1, (0, 1)), 10: (1, (2, 3))}
W_MEAN = {5: 0, 11: 1}
W_SCALE = {6: (0, (0, 1)), 7: (0, (2, 3)), 11: (1, (0, 1)), 12: (1, (2, 3))}
W_ROUND = {slot + 1: what for slot, what in W_SCALE.items()}
SUM_BANKS = (4, 5)
DT_BANKS = (0, 1, 5, 6)
FFN_UP = {5 + i: (2 * i, 2 * i + 1) for i in range(FT // 2)}
FFN_DOWN = {6 + i: (2 * i, 2 * i + 1) for i in range(FT // 2)}


def state_at(slot, which):
    return SCAN_SLOTS[slot][which] if slot in SCAN_SLOTS else None


def in_parts(ap):
    return ap.bitcast(F32R)


class Tally:

    def __init__(self, sem, per):
        self.sem, self.per, self.n = sem, per, 0

    def start(self):
        assert self.n in (0, self.per), (self.n, self.per)
        self.n = 0

    def link(self, eng, b, ins):
        self.n += 1
        ins.then_inc(self.sem, 1)
        eng.wait_ge(self.sem, b * self.per + self.n)


def program(nc, x_d, ctxT_d, ipw_d, xpw_d, dtw_d, pch_d, w1_d, w2_d, wqk_d, bqk_d, ffn_d, b1_d, b2_d, gate_d,
            ident_d, identb_d, pick_d, out_d):
    with ExitStack() as ctx:
        def sb(name, shape, dt=F32):
            return ctx.enter_context(nc.sbuf_tensor(name, shape, dt))

        def sb_mixer(name, shape, dt=F32):
            return mixer_only.enter_context(nc.sbuf_tensor(name, shape, dt))

        def sem(name):
            return ctx.enter_context(nc.semaphore(name))

        banks = [ctx.enter_context(nc.psum_tensor(f"bank{i}", [P, 512], F32)) for i in range(8)]

        ident = sb("ident", [P, P])
        identb = sb("identb", [P, P], BF16)
        pick = sb("pick", [P, 2 * NS], BF16)
        ones = sb("ones", [P, P])
        expo = sb("expo", [P, 3])
        ipw = sb("ipw", [P, KC, D])
        xpw = sb("xpw", [P, J, P])
        dtw = sb("dtw", [R, D])
        pch = sb("pch", [P, J, PC_N])
        a_neg = sb("a_neg", [P, J, NS])
        wqk = sb("wqk", [P, KC, 2, P])
        bqk = sb("bqk", [P, 2])
        b1 = sb("b1", [P, FT])
        b2 = sb("b2", [P, D])
        gates = sb("gates", [P, 4])
        w1q = sb("w1q", [P, J, FF], BF16)
        w2q = sb("w2q", [P, FT, D], BF16)
        wsum = sb("wsum", [P, 2, 4])
        wstat = sb("wstat", [P, 2, 4])
        ring = sb("ring", [P, RING, 2 * D])

        ctxT = sb("ctxT", [P, KC, L])
        xres = sb("xres", [P, T, D])
        xpad = sb("xpad", [P, 2, PAD + L])
        u = sb("u", [P, J, L])
        xd = sb("xd", [P, L])
        xd3 = sb("xd3", [P, L], BF16)
        attT = sb("attT", [P, J, D])
        qk = xpad[:, :, PAD:]
        ex = xd
        qT = sb("qT", [P, J, L], BF16)
        zst = sb("zst", [P, J, 12])
        q1 = sb("q1", [P, 2, D], BF16)
        mst = sb("mst", [P, T, 16])
        ast = sb("ast", [P, J, 4])

        stage = sb("stage", [P, 4 * FF])
        h = [stage[:, i * FF:(i + 1) * FF] for i in range(2)]
        xb = stage[:, 2 * FF:3 * FF].rearrange("p (t d) -> p t d", t=T)
        xnT = stage[:, 3 * FF:4 * FF].rearrange("p (k l) -> p k l", k=J)
        hq = sb("hq", [P, FF], BF16)
        hqT = sb("hqT", [P, FT, P], BF16)
        xn = sb("xn", [P, 2, D])
        fst = sb("fst", [P, T, 24])

        with ExitStack() as mixer_only:
            dt = sb_mixer("dt", [P, J, L])
            du = sb_mixer("du", [P, J, L])
            decay = sb_mixer("decay", [P, DECAYBUFS, HALF, L])
            work = sb_mixer("work", [P, SCANBUFS, HALF, L])
            hT = sb_mixer("hT", [P, 4, L])
            ccast = sb_mixer("ccast", [P, 2, L])
            bcast = sb_mixer("bcast", [P, 2, L])
        x_high = sb("x_high", [P, J, L])
        x_low = sb("x_low", [P, J, L])
        w_high = sb("w_high", [P, 3, 2 * D])
        w_low = sb("w_low", [P, 3, 2 * D])
        h_high = sb("h_high", [P, 2, L])
        h_low = sb("h_low", [P, 2, L])
        h_full = sb("h_full", [P, 2, L])
        x1n = ccast[:, 0, :]
        sptmp = (work[:, 2, :, :], hT[:, 0:HALF, :])
        zs = (xn, qk)

        bf_bank = [banks[i][:, :].bitcast(BF16) for i in range(8)]

        s_first = sem("s_first")
        s_const = sem("s_const")
        s_stage = sem("s_stage")
        s_stage2 = [sem(f"s_stage2_{c}") for c in range(4)]
        s_ctx = sem("s_ctx")
        s_x = sem("s_x")
        s_ring = [sem(f"s_ring{i}") for i in range(RING)]
        s_out = sem("s_out")
        s_stored = sem("s_stored")
        s_ones = sem("s_ones")
        s_aneg = sem("s_aneg")
        s_gates = sem("s_gates")
        s_b2 = sem("s_b2")
        s_wsq = sem("s_wsq")
        s_wmean = sem("s_wmean")
        s_wms = sem("s_wms")
        s_wstat = sem("s_wstat")
        s_wscaled = sem("s_wscaled")
        s_wclip = sem("s_wclip")
        s_wq = sem("s_wq")
        s_pad = sem("s_pad")
        s_inproj = sem("s_inproj")
        s_inprojc = sem("s_inprojc")
        s_conv = sem("s_conv")
        s_u = sem("s_u")
        s_xdbl = sem("s_xdbl")
        s_xd = sem("s_xd")
        s_split = sem("s_split")
        s_dtmm = sem("s_dtmm")
        s_spabs = sem("s_spabs")
        s_spmax = sem("s_spmax")
        s_spexp = sem("s_spexp")
        s_sptmp = sem("s_sptmp")
        s_spln = sem("s_spln")
        s_log = sem("s_log")
        s_dt = sem("s_dt")
        s_du = sem("s_du")
        s_accin = sem("s_accin")
        s_bc = sem("s_bc")
        s_bcc = sem("s_bcc")
        s_decay = sem("s_decay")
        s_dbu = sem("s_dbu")
        s_dbuP = sem("s_dbuP")
        s_scan = sem("s_scan")
        s_hc = sem("s_hc")
        s_acc = sem("s_acc")
        s_sum = sem("s_sum")
        s_qkmm = sem("s_qkmm")
        s_qk = sem("s_qk")
        s_emm = sem("s_emm")
        s_emax = sem("s_emax")
        s_eexp = sem("s_eexp")
        s_eprob = sem("s_eprob")
        s_eT = sem("s_eT")
        s_att = sem("s_att")
        s_zst = sem("s_zst")
        s_zrs = sem("s_zrs")
        s_zs = sem("s_zs")
        s_y = sem("s_y")
        s_yT = sem("s_yT")
        s_x1 = sem("s_x1")
        s_x1st = sem("s_x1st")
        s_x1rs = sem("s_x1rs")
        s_q1 = sem("s_q1")
        s_q1T = sem("s_q1T")
        s_qT = sem("s_qT")
        s_mm1 = sem("s_mm1")
        s_gelu = sem("s_gelu")
        s_hsc = sem("s_hsc")
        s_hr = sem("s_hr")
        s_hq = sem("s_hq")
        s_hqT = sem("s_hqT")
        s_ev0 = sem("s_ev0")
        s_ev1 = sem("s_ev1")
        s_mm2 = sem("s_mm2")
        s_x2 = sem("s_x2")
        s_lnst = sem("s_lnst")
        s_lnrs = sem("s_lnrs")
        s_xn = sem("s_xn")
        s_xnT = sem("s_xnT")
        s_xnTc = sem("s_xnTc")
        s_xm = sem("s_xm")
        s_x3 = sem("s_x3")
        s_x3b = sem("s_x3b")
        s_fmm1 = sem("s_fmm1")
        s_fgelu = sem("s_fgelu")
        s_fmm2 = sem("s_fmm2")
        s_x4 = sem("s_x4")
        s_xlow = sem("s_xlow")
        s_whigh = sem("s_whigh")
        s_wlow = sem("s_wlow")
        s_hhigh = sem("s_hhigh")
        s_hlow = sem("s_hlow")
        dve_p = Tally(sem("dve_p"), 2 * J + 3 + 2)
        dve_m = Tally(sem("dve_m"), J + J + 6 * T)
        dve_f = Tally(sem("dve_f"), 5 * T)
        pool_s = Tally(sem("pool_s"), 0)
        pool_m = Tally(sem("pool_m"), 2 * J + T)
        pool_f = Tally(sem("pool_f"), 2 * T)
        dve_w = Tally(sem("dve_w"), 0)

        consts = (
            (xpw[:], xpw_d.rearrange("(k p) e -> p k e", p=P)),
            (gates[:], gate_d), (dtw[:], dtw_d), (pick[:], pick_d), (ident[:], ident_d), (identb[:], identb_d),
            (bqk[:], bqk_d), (b1[:], b1_d), (b2[:], b2_d),
            (wqk[:, :, 0, :], wqk_d[0].rearrange("(k p) e -> p k e", p=P)),
            (wqk[:, :, 1, :], wqk_d[1].rearrange("(k p) e -> p k e", p=P)),
        )
        const_wait = len(consts) * 16
        first_consts = (
            (ipw[:], ipw_d.rearrange("(k p) e -> p k e", p=P)),
            (pch[:], pch_d.rearrange("(j p) c -> p j c", p=P)),
        )
        first_wait = len(first_consts) * 16

        carried = {e: sem(f"s_carried_{e}") for e in ("dve", "pool")}

        def carry_wait(eng, name):
            eng.sem_inc(carried[name], 1)

        block = ctx.enter_context(nc.Block())

        @block.sync
        def _(sp):
            def load_ring(slot, f):
                sp.dma_start(ring[:, slot, :], ffn_d[f]).then_inc(s_ring[slot], 16)

            sp.dma_start(ctxT[:], ctxT_d[0].rearrange("(k p) l -> p k l", p=P)).then_inc(s_ctx, 16)
            for dst, src in first_consts:
                sp.dma_start(dst, src).then_inc(s_first, 16)
            for dst, src in consts:
                sp.dma_start(dst, src).then_inc(s_const, 16)
            sp.dma_start(xres[:], x_d[0].rearrange("(t p) d -> p t d", p=P)).then_inc(s_x, 16)
            sp.dma_start(stage[:].rearrange("p (k f) -> p k f", k=J),
                         w1_d.rearrange("(k p) f -> p k f", p=P)).then_inc(s_stage, 16)
            for f in range(RING):
                load_ring(f, f)
            for c in range(4):
                sp.wait_ge(s_wq, c + 1)
                sp.dma_start(stage[:, c * FF:(c + 1) * FF].rearrange("p (k f) -> p k f", k=FT // 4),
                             w2_d[c * (FF // 4):(c + 1) * (FF // 4)].rearrange("(k p) f -> p k f", p=P))\
                    .then_inc(s_stage2[c], 16)

            def load_context(b):
                sp.wait_ge(s_qkmm, (b - 1) * 2 + 2)
                sp.dma_start(ctxT[:], ctxT_d[b].rearrange("(k p) l -> p k l", p=P)).then_inc(s_ctx, 16)

            def run(b, more, context_after):
                if more:
                    sp.wait_ge(s_x2, b * T + T)
                    sp.dma_start(xres[:], x_d[b + 1].rearrange("(t p) d -> p t d", p=P)).then_inc(s_x, 16)
                for f in range(FT):
                    if more or f + RING < FT:
                        sp.wait_ge(s_fmm2, b * FT + f + 1)
                        load_ring(f % RING, (f + RING) % FT)
                    if f == FT // 2 and context_after:
                        load_context(b + 2)
                for t in range(T):
                    sp.wait_ge(s_x4, b * T + t + 2)
                    sp.dma_start(out_d[b, t * P:(t + 1) * P, :], xb[:, t, :]).then_inc(s_out, 16)
                sp.wait_ge(s_out, (b + 1) * T * 16)
                sp.sem_inc(s_stored, 1)

            sp.sem_inc(s_stored, 1)
            load_context(1)
            with sp.Fori(0, B - 2) as i:
                run(i, True, True)
            run(B - 2, True, False)
            run(B - 1, False, False)
            sp.wait_ge(s_out, B * T * 16)

        @block.tensor
        def _(pe):
            def scan_bcast(b, n, i):
                if n == 0 and i == 0:
                    pe.wait_ge(s_split, b + 1)
                    pe.wait_ge(s_spmax, b * J + J)
                else:
                    pe.wait_ge(s_bcc, b * 2 * NS + 2 * n + i)
                pe.matmul(banks[0][:], pick[:, i * NS + n:i * NS + n + 1].broadcast_to([P, P]), xd3[:],
                          start=True, stop=True).then_inc(s_bc, 1)

            def bcast_next(b, slot, which, i):
                n = state_at(slot, which)
                if n is not None and n + 1 < NS:
                    scan_bcast(b, n + 1, i)

            def sum_half(n):
                pe.wait_ge(s_hc, 2 * n + 2)
                for q in range(HALF):
                    last = pe.matmul(banks[SUM_BANKS[q]][:], ident[:], work[:, (2 * n + 1) % SCANBUFS, q, :],
                                     start=n == 0, stop=n == NS - 1)
                last.then_inc(s_sum, 1)

            def sum_halves(slot, which):
                n = state_at(slot, which)
                if n:
                    sum_half(n - 1)
                if n == NS - 1:
                    sum_half(n)

            def att_transpose(b, j):
                pe.wait_ge(s_eprob, b * J + j + 1)
                for k in range(J):
                    last = pe.transpose(banks[1][:, k * P:(k + 1) * P], ex[:, k * P:(k + 1) * P], ident[:])
                last.then_inc(s_eT, 1)

            def project(b, prev, j):
                if j == 0:
                    pe.wait_ge(s_ctx, b * 16 + 16)
                    if prev is not None:
                        pe.wait_ge(s_x1, prev * T + T)
                elif j == 1 and prev is not None:
                    pe.wait_ge(s_qT, prev * T + T)
                elif j >= 2:
                    pe.wait_ge(s_inprojc, b * J + j - 1)
                for k in range(KC):
                    last = pe.matmul(banks[j % 2][:], ipw[:, k, j * P:(j + 1) * P], ctxT[:, k, :],
                                     start=k == 0, stop=k == KC - 1)
                last.then_inc(s_inproj, 1)

            def low_rank(b):
                pe.wait_ge(s_u, b + 1)
                for j in range(J):
                    last = pe.matmul(banks[0][:], xpw[:, j, :], u[:, j, :], start=j == 0, stop=j == J - 1)
                last.then_inc(s_xdbl, 1)

            def step_sizes(b, prev):
                pe.wait_ge(s_xd, b + 1)
                if prev is not None:
                    pe.wait_ge(s_gelu, prev * T * FC + T * FC)
                for j in range(J):
                    pe.matmul(banks[DT_BANKS[j]][:], dtw[:, j * P:(j + 1) * P], xd[0:R, :],
                              start=True, stop=True).then_inc(s_dtmm, 1)

            def qk_products(b, prev, i):
                if i:
                    pe.wait_ge(s_qk, b * 2 + 1)
                for k in range(KC):
                    last = pe.matmul(banks[1][:], wqk[:, k, i, :], ctxT[:, k, :], start=k == 0, stop=k == KC - 1)
                last.then_inc(s_qkmm, 1)

            def energies(b, j):
                if j:
                    pe.wait_ge(s_att, b * J + j)
                else:
                    pe.wait_ge(s_qk, b * 2 + 2)
                pe.matmul(banks[1][:], qk[:, 0, j * P:(j + 1) * P], qk[:, 1, :],
                          start=True, stop=True).then_inc(s_emm, 1)

            def gate_transposes(b, ts):
                for t in ts:
                    if t == 0:
                        pe.wait_ge(s_y, b * 2 + 2)
                        pe.wait_ge(s_att, b * J + J)
                    if t >= 2:
                        pe.wait_ge(s_x1, b * T + t - 1)
                    for j in range(J):
                        last = pe.transpose(banks[(t + 1) % 2][:, j * P:(j + 1) * P], u[:, j, t * P:(t + 1) * P], ident[:])
                    last.then_inc(s_yT, 1)

            def q_transposes(b, ts):
                for t in ts:
                    pe.wait_ge(s_q1, b * T + t + 1)
                    if t:
                        pe.wait_ge(s_qT, b * T + t)
                    else:
                        pe.wait_ge(s_x1, b * T + T - 1)
                    for k in range(J):
                        last = pe.transpose(bf_bank[1][:, k * P:(k + 1) * P], q1[:, t % 2, k * P:(k + 1) * P], identb[:])
                    last.then_inc(s_q1T, 1)

            def up1(b, t, cs=range(FC)):
                pe.wait_ge(s_qT, b * T + t + 1)
                for c in cs:
                    g = t * FC + c
                    if g >= 3:
                        pe.wait_ge(s_gelu, b * T * FC + g - 2)
                    elif g == 0:
                        pe.wait_ge(s_x4, b * T + 1)
                    for k in range(J):
                        last = pe.matmul(banks[4 + g % 3][:], qT[:, k, t * P:(t + 1) * P],
                                         w1q[:, k, c * 512:(c + 1) * 512], start=k == 0, stop=k == J - 1)
                    last.then_inc(s_mm1, 1)

            def down1(b, t):
                pe.wait_ge(s_ev0, b * T + t + 1)
                pe.wait_ge(s_ev1, b * T + t + 1)
                if t:
                    pe.wait_ge(s_x2, b * T + t)
                else:
                    pe.wait_ge(s_wq, 8)
                for f in range(FT):
                    last = pe.matmul(banks[7][:], hqT[:, f, :], w2q[:, f, :], start=f == 0, stop=f == FT - 1)
                last.then_inc(s_mm2, 1)

            def transpose_h(b, t):
                pe.wait_ge(s_hq, b * T + t + 1)
                for r in range(2):
                    if r == 0:
                        if t:
                            pe.wait_ge(s_ev0, b * T + t)
                    elif t >= 2:
                        pe.wait_ge(s_xnTc, b * 2 * T + t - 1)
                    elif t:
                        pe.wait_ge(s_ev1, b * T + t)
                    for i in range(FT // 2):
                        f = r * (FT // 2) + i
                        last = pe.transpose(bf_bank[2 + r][:, i * P:(i + 1) * P], hq[:, f * P:(f + 1) * P],
                                            identb[:])
                    last.then_inc(s_hqT, 1)

            def norm_transpose(b, i):
                bank = 3 if i < T else 2 + i % 2
                pe.wait_ge(s_xn, b * 2 * T + i + 1)
                if i < T:
                    pe.wait_ge(s_ev1, b * T + min(i + 2, T))
                if i == T - 1:
                    pe.wait_ge(s_xnTc, b * 2 * T + T - 1)
                if i == T:
                    pe.wait_ge(s_ev0, b * T + T)
                if i > T:
                    pe.wait_ge(s_xnTc, b * 2 * T + i - 1)
                for k in range(J):
                    last = pe.transpose(banks[bank][:, k * P:(k + 1) * P], xn[:, i % 2, k * P:(k + 1) * P], ident[:])
                last.then_inc(s_xnT, 1)

            def attend(b, t):
                pe.wait_ge(s_xnTc, b * 2 * T + t + 1)
                if t == 0:
                    pe.wait_ge(s_gelu, b * T * FC + T * FC)
                    pe.wait_ge(s_att, b * J + J)
                if t == T - 1:
                    pe.wait_ge(s_x2, b * T + T)
                for k in range(J):
                    last = pe.matmul(banks[4 + t][:], xnT[:, k, t * P:(t + 1) * P], attT[:, k, :],
                                     start=k == 0, stop=k == J - 1)
                last.then_inc(s_xm, 1)

            def f_up(b, f):
                if f is None:
                    return
                if f >= 2:
                    pe.wait_ge(s_fgelu, b * FT + f - 1)
                else:
                    pe.wait_ge(s_xnTc, b * 2 * T + 2 * T)
                pe.wait_ge(s_ring[f % RING], (b * (FT // RING) + f // RING + 1) * 16)
                for k in range(J):
                    last = pe.matmul(banks[2 + f % 2][:], ring[:, f % RING, k * P:(k + 1) * P], xnT[:, k, :],
                                     start=k == 0, stop=k == J - 1)
                last.then_inc(s_fmm1, 1)

            def f_down(b, f):
                if f is None:
                    return
                pe.wait_ge(s_fgelu, b * FT + f + 1)
                if f == 0:
                    pe.wait_ge(s_x3, b * T + T)
                for t in range(T):
                    last = pe.matmul(banks[4 + t][:], hT[:, f % 4, t * P:(t + 1) * P], ring[:, f % RING, D:2 * D],
                                     start=f == 0, stop=f == FT - 1)
                last.then_inc(s_fmm2, 1)

            def product(bank, parts, first, last):
                for i, (weights, moving) in enumerate(parts):
                    out = pe.matmul(bank[:], in_parts(weights), in_parts(moving),
                                    start=first and i == 0, stop=last and i == len(parts) - 1)
                return out

            def tail_up(b, f):
                pe.wait_ge(s_wlow, f + 1)
                if f >= 2:
                    pe.wait_ge(s_fgelu, b * FT + f - 1)
                high, low = w_high[:, f % 3, :], w_low[:, f % 3, :]
                for k in range(J):
                    ks = slice(k * P, (k + 1) * P)
                    last = product(banks[2 + f % 2], ((high[:, ks], x_high[:, k, :]), (high[:, ks], x_low[:, k, :]),
                                                      (low[:, ks], x_high[:, k, :])), k == 0, k == J - 1)
                last.then_inc(s_fmm1, 1)

            def tail_down(b, f):
                pe.wait_ge(s_hlow, f + 1)
                if f == 0:
                    pe.wait_ge(s_x3, b * T + T)
                high, low = w_high[:, f % 3, D:], w_low[:, f % 3, D:]
                for t in range(T):
                    ts = slice(t * P, (t + 1) * P)
                    last = product(banks[4 + t], ((h_high[:, f % 2, ts], high), (h_high[:, f % 2, ts], low),
                                                  (h_low[:, f % 2, ts], high)), f == 0, f == FT - 1)
                last.then_inc(s_fmm2, 1)

            def tail(b):
                pe.wait_ge(s_xlow, T)
                for f in range(FT):
                    tail_up(b, f)
                    if f:
                        tail_down(b, f - 1)
                tail_down(b, FT - 1)

            def middle(b, m, prev, scans, rest):
                if not rest:
                    pe.wait_ge(s_const, const_wait)
                    pe.wait_ge(s_ones, 2)
                if rest:
                    up1(b, 3, range(FC - 1))
                    down1(b, 1)
                    up1(b, 3, (FC - 1,))
                    norm_transpose(b, 0)
                    transpose_h(b, 2)
                if scans:
                    low_rank(m)
                if rest:
                    down1(b, 2)
                    norm_transpose(b, 1)
                    transpose_h(b, 3)
                if scans:
                    step_sizes(m, prev)
                if rest:
                    down1(b, 3)
                    attend(b, 0)
                if scans:
                    scan_bcast(m, 0, 0)
                if rest:
                    norm_transpose(b, 2)
                    attend(b, 1)
                if scans:
                    scan_bcast(m, 0, 1)
                if rest:
                    norm_transpose(b, 3)
                    attend(b, 2)

            def pass_(b, scans, rest=True):
                m, prev = (b + 1, b) if rest else (0, None)
                for slot in range(SLOTS if scans else 5):
                    ups, downs = FFN_UP.get(slot, (None, None)), FFN_DOWN.get(slot, (None, None))
                    if slot == 3:
                        middle(b, m, prev, scans, rest)
                    if rest and slot == 0:
                        up1(b, 0)
                    if scans and slot == 0:
                        project(m, prev, 0)
                    if rest:
                        if slot < 2:
                            up1(b, slot + 1)
                        if slot == 4:
                            norm_transpose(b, 4)
                            attend(b, 3)
                            norm_transpose(b, 5)
                    if scans:
                        if slot == 0:
                            project(m, prev, 1)
                            project(m, prev, 2)
                        if slot == 1:
                            project(m, prev, 3)
                        bcast_next(m, slot, 0, 0)
                        if slot in ATT_SLOTS and ATT_SLOTS[slot]:
                            att_transpose(m, ATT_SLOTS[slot] - 1)
                        if slot == ATT_LAST_SLOT:
                            att_transpose(m, J - 1)
                        if slot == QK_SLOT:
                            qk_products(m, prev, 0)
                        if slot == GATE_SLOT:
                            gate_transposes(m, (0, 1))
                    if rest:
                        if slot == 1:
                            down1(b, 0)
                        if slot < 2:
                            transpose_h(b, slot)
                        if slot == 4:
                            norm_transpose(b, 6)
                            norm_transpose(b, 7)
                        f_up(b, ups[0])
                    else:
                        weights(slot)
                    if scans:
                        bcast_next(m, slot, 0, 1)
                        if slot in ATT_SLOTS:
                            energies(m, ATT_SLOTS[slot])
                        if slot == QK_SLOT:
                            qk_products(m, prev, 1)
                    if rest:
                        f_up(b, ups[1])
                    else:
                        sum_halves(slot, 0)
                    if scans:
                        bcast_next(m, slot, 1, 0)
                        if slot == GATE_SLOT:
                            gate_transposes(m, (2, 3))
                    if rest:
                        f_down(b, downs[0])
                    if scans:
                        bcast_next(m, slot, 1, 1)
                        if slot == QUANT_SLOT:
                            q_transposes(m, (0, 1))
                    if rest:
                        f_down(b, downs[1])
                    else:
                        sum_halves(slot, 1)
                    if scans and slot == QUANT_SLOT:
                        q_transposes(m, (2, 3))
                if not scans:
                    tail(b)

            def weights(slot):
                if slot in W_MEAN:
                    weight_mean(W_MEAN[slot])

            def weight_mean(i):
                pe.wait_ge(s_wsq, 4 * i + 4)
                for c in range(4):
                    last = pe.matmul(banks[3][:, i:i + 1], ones[:], wsum[:, i, c:c + 1], start=c == 0, stop=c == 3)
                last.then_inc(s_wmean, 1)

            pe.wait_ge(s_first, first_wait)
            pass_(None, True, rest=False)
            pe.wait_ge(s_wq, 4)
            with pe.Fori(0, B - 1) as i:
                pass_(i, True)
            pass_(B - 1, False)

        @block.scalar
        def _(act):
            def copy_bc(b, n, i):
                dst = (bcast, ccast)[i]
                act.wait_ge(s_bc, b * 2 * NS + 2 * n + i + 1)
                if n >= 2:
                    if i:
                        act.wait_ge(s_hc, b * HN + 2 * (n - 1))
                    else:
                        act.wait_ge(s_dbu, b * NS + n - 1)
                        act.wait_ge(s_dbuP, b * NS + n - 1)
                act.activation(dst[:, n % 2, :], banks[0][:], ACT.Copy).then_inc(s_bcc, 1)

            def copy_next(b, slot, which, i):
                n = state_at(slot, which)
                if n is not None and n + 1 < NS:
                    copy_bc(b, n + 1, i)

            def decay_half(b, s):
                if s >= DECAYBUFS:
                    act.wait_ge(s_scan, b * HN + s - DECAYBUFS + 1)
                n, p = divmod(s, 2)
                if n == 0:
                    act.wait_ge(s_dt, b * 2 + p + 1)
                for q in range(HALF):
                    last = act.activation(decay[:, s % DECAYBUFS, q, 1:], dt[:, p * HALF + q, 1:], ACT.Exp,
                                          scale=a_neg[:, p * HALF + q, n:n + 1])
                last.then_inc(s_decay, 1)

            def decays(b, slot, which, part):
                n = state_at(slot, which)
                if n is not None:
                    if n == 0 and part == 0:
                        decay_half(b, 0)
                    if 2 * n + 1 + part < HN:
                        decay_half(b, 2 * n + 1 + part)

            def project_copy(b, prev, j):
                act.wait_ge(s_inproj, b * J + j + 1)
                if j >= 2:
                    act.wait_ge(s_conv, b * J + j - 1)
                elif prev is not None and j == 0:
                    act.wait_ge(s_y, prev * 2 + 2)
                    act.wait_ge(s_yT, prev * T + T)
                act.activation(xpad[:, j % 2, PAD:], banks[j % 2][:], ACT.Copy)
                act.activation(u[:, j, :], banks[j % 2][:], ACT.Identity, scale=pch[:, j, TAPS - 1:TAPS],
                               bias=pch[:, j, PC_CONVB:PC_CONVB + 1]).then_inc(s_inprojc, 1)

            def silu_u(b):
                act.wait_ge(s_conv, b * J + J)
                act.activation(u[:], u[:], ACT.Silu).then_inc(s_u, 1)

            def low_rank_copy(b, prev):
                act.wait_ge(s_xdbl, b + 1)
                if prev is not None:
                    act.wait_ge(s_bc, prev * 2 * NS + 2 * NS)
                act.activation(xd[:], banks[0][:], ACT.Copy)
                act.activation(xd3[:], banks[0][:], ACT.Copy).then_inc(s_xd, 1)

            def softplus(b, prev):
                if prev is not None:
                    act.wait_ge(s_acc, prev * HN + HN)
                for j in range(J):
                    act.wait_ge(s_dtmm, b * J + j + 1)
                    act.activation(du[:, j, :], banks[DT_BANKS[j]][:], ACT.Abs,
                                   bias=pch[:, j, PC_DTB:PC_DTB + 1]).then_inc(s_spabs, 1)
                for p in range(2):
                    js = slice(p * HALF, (p + 1) * HALF)
                    act.wait_ge(s_spabs, b * J + (p + 1) * HALF)
                    act.activation(work[:, p, :, :], du[:, js, :], ACT.Exp, scale=-1.0).then_inc(s_spexp, 1)
                for p in range(2):
                    js = slice(p * HALF, (p + 1) * HALF)
                    act.wait_ge(s_spexp, b * 2 + p + 1)
                    act.activation(du[:, js, :], work[:, p, :, :], ACT.Ln, bias=1.0).then_inc(s_spln, 1)

            def first_copy(b, prev, i):
                if i:
                    act.wait_ge(s_split, b + 1)
                elif prev is not None:
                    act.wait_ge(s_dbu, prev * NS + NS)
                    act.wait_ge(s_dbuP, prev * NS + NS)
                copy_bc(b, 0, i)

            def weight_high(b, f):
                act.wait_ge(s_ring[f % RING], (b * (FT // RING) + f // RING + 1) * 16)
                if f >= 3:
                    act.wait_ge(s_fmm2, b * FT + f - 2)
                act.activation(in_parts(w_high[:, f % 3, :]), ring[:, f % RING, :], ACT.Copy).then_inc(s_whigh, 1)

            def tail_first(b):
                act.wait_ge(s_scan, B * HN)
                act.wait_ge(s_dbu, B * NS)
                act.wait_ge(s_dbuP, B * NS)
                weight_high(b, 0)
                weight_high(b, 1)

            def tail(b):
                for f in range(FT):
                    act.wait_ge(s_fmm1, b * FT + f + 1)
                    if f >= 2:
                        act.wait_ge(s_hlow, f - 1)
                        act.wait_ge(s_fmm2, b * FT + f - 1)
                    act.activation(h_full[:, f % 2, :], banks[2 + f % 2][:], ACT.Gelu,
                                   bias=b1[:, f:f + 1]).then_inc(s_fgelu, 1)
                    act.wait_ge(s_fgelu, b * FT + f + 1)
                    act.activation(in_parts(h_high[:, f % 2, :]), h_full[:, f % 2, :], ACT.Copy).then_inc(s_hhigh, 1)
                    if f + 2 < FT:
                        weight_high(b, f + 2)

            def middle(b, m, prev, scans, rest):
                if not rest:
                    set_up()
                    weights(3)
                if rest:
                    gelu1(b, 3)
                    norm_copy(b, 0)
                    h_copy(b, 2)
                if scans:
                    low_rank_copy(m, prev)
                if rest:
                    norm_copy(b, 1)
                    h_copy(b, 3)
                if scans:
                    softplus(m, prev)
                    first_copy(m, prev, 0)
                if rest:
                    norm_copy(b, 2)
                if scans:
                    first_copy(m, prev, 1)
                if rest:
                    norm_copy(b, 3)

            def att_copy(b, prev, j):
                act.wait_ge(s_eT, b * J + j + 1)
                if prev is not None:
                    act.wait_ge(s_xm, prev * T + T)
                act.activation(attT[:, :, j * P:(j + 1) * P], banks[1][:].rearrange("p (k m) -> p k m", k=J),
                               ACT.Copy).then_inc(s_att, 1)

            def qk_copy(b, prev, i):
                act.wait_ge(s_qkmm, b * 2 + i + 1)
                act.activation(qk[:, i, :], banks[1][:], ACT.Identity, bias=bqk[:, i:i + 1]).then_inc(s_qk, 1)

            def energy_exp(b, j):
                act.wait_ge(s_emax, b * J + j + 1)
                if j:
                    act.wait_ge(s_eT, b * J + j)
                act.activation(ex[:], banks[1][:], ACT.Exp, bias=ast[:, j, 0:1],
                               accum_out=ast[:, j, 1:2]).then_inc(s_eexp, 1)

            def gates_silu(b):
                act.wait_ge(s_emm, b * J + J)
                for j in range(J):
                    act.wait_ge(s_zrs, b * J + j + 1)
                    act.activation(zs[j // HALF][:, j % HALF, :], xres[:, j, :], ACT.Silu, scale=zst[:, j, 9:10],
                                   bias=zst[:, j, 10:11]).then_inc(s_zs, 1)

            def q_copy(b, ts):
                for t in ts:
                    act.wait_ge(s_q1T, b * T + t + 1)
                    act.activation(qT[:, :, t * P:(t + 1) * P],
                                   bf_bank[1][:, 0:J * P].rearrange("p (k l) -> p k l", k=J),
                                   ACT.Copy).then_inc(s_qT, 1)

            def gelu1(b, t):
                for c in range(FC):
                    g = t * FC + c
                    act.wait_ge(s_mm1, b * T * FC + g + 1)
                    if c == 0 and t >= 2:
                        act.wait_ge(s_hq, b * T + t - 1)
                    act.activation(h[t % 2][:, c * 512:(c + 1) * 512], banks[4 + g % 3][:], ACT.Gelu,
                                   scale=mst[:, t, 13:14]).then_inc(s_gelu, 1)

            def norm_copy(b, i, parts=False):
                act.wait_ge(s_xnT, b * 2 * T + i + 1)
                t = i % T
                if i >= T:
                    act.wait_ge(s_xm, b * T + t + 1)
                bank = 3 if i < T else 2 + i % 2
                if parts:
                    act.activation(in_parts(x_high[:, :, t * P:(t + 1) * P]),
                                   banks[bank][:].rearrange("p (k l) -> p k l", k=J), ACT.Copy)
                act.activation(xnT[:, :, t * P:(t + 1) * P], banks[bank][:].rearrange("p (k l) -> p k l", k=J),
                               ACT.Copy).then_inc(s_xnTc, 1)

            def h_copy(b, t):
                act.wait_ge(s_hqT, b * 2 * T + 2 * t + 1)
                if t:
                    act.wait_ge(s_mm2, b * T + t)
                act.activation(hqT[:, 0:FT // 2, :], bf_bank[2].rearrange("p (f l) -> p f l", l=P),
                               ACT.Copy).then_inc(s_ev0, 1)
                act.wait_ge(s_hqT, b * 2 * T + 2 * t + 2)
                act.activation(hqT[:, FT // 2:, :], bf_bank[3].rearrange("p (f l) -> p f l", l=P),
                               ACT.Copy).then_inc(s_ev1, 1)

            def f_gelu(b, f):
                act.wait_ge(s_fmm1, b * FT + f + 1)
                if f >= 4:
                    act.wait_ge(s_fmm2, b * FT + f - 3)
                act.activation(hT[:, f % 4, :], banks[2 + f % 2][:], ACT.Gelu, bias=b1[:, f:f + 1]).then_inc(s_fgelu, 1)

            def pass_(b, scans, rest=True):
                m, prev = (b + 1, b) if rest else (0, None)
                for slot in range(SLOTS if scans else 5):
                    if slot == 3:
                        if not scans:
                            tail_first(b)
                        middle(b, m, prev, scans, rest)
                    if rest and slot == 0:
                        gelu1(b, 0)
                    if scans and slot == 0:
                        project_copy(m, prev, 0)
                    if rest and slot == 4:
                        norm_copy(b, 4, not scans)
                    if scans and slot == 4:
                        decays(m, slot, 0, 0)
                        decays(m, slot, 0, 1)
                    if rest:
                        if slot < 2:
                            gelu1(b, slot + 1)
                        if slot == 4:
                            norm_copy(b, 5, not scans)
                    if scans:
                        if slot == 0:
                            project_copy(m, prev, 1)
                            project_copy(m, prev, 2)
                        if slot == 1:
                            project_copy(m, prev, 3)
                        copy_next(m, slot, 0, 0)
                        if slot in ATT_SLOTS and ATT_SLOTS[slot]:
                            att_copy(m, prev, ATT_SLOTS[slot] - 1)
                        if slot == ATT_LAST_SLOT:
                            att_copy(m, prev, J - 1)
                        if slot != 4:
                            decays(m, slot, 0, 0)
                        if slot == QK_SLOT:
                            qk_copy(m, prev, 0)
                    if rest:
                        if slot < 2:
                            h_copy(b, slot)
                        if slot == 4:
                            norm_copy(b, 6, not scans)
                            norm_copy(b, 7, not scans)
                    elif slot != 3:
                        weights(slot)
                    if scans:
                        if slot == 1:
                            silu_u(m)
                        copy_next(m, slot, 0, 1)
                        if slot != 4:
                            decays(m, slot, 0, 1)
                        if slot in ATT_SLOTS:
                            energy_exp(m, ATT_SLOTS[slot])
                        if slot == QK_SLOT:
                            qk_copy(m, prev, 1)
                    if rest:
                        for f in FFN_UP.get(slot, ()):
                            if f is not None:
                                f_gelu(b, f)
                    if scans:
                        copy_next(m, slot, 1, 0)
                        decays(m, slot, 1, 0)
                        copy_next(m, slot, 1, 1)
                        decays(m, slot, 1, 1)
                        if slot == ZS_SLOT:
                            gates_silu(m)
                        if slot == QUANT_SLOT:
                            q_copy(m, range(T))
                    if not rest:
                        weights_last(slot)
                if not scans:
                    tail(b)

            def weights(slot):
                if slot in W_SQUARE:
                    square(*W_SQUARE[slot])
                if slot in W_MEAN:
                    mean(W_MEAN[slot])

            def weights_last(slot):
                if slot in W_SCALE:
                    scale(*W_SCALE[slot])
                if slot in W_ROUND:
                    quantise(*W_ROUND[slot])

            def set_up():
                act.wait_ge(s_const, const_wait)
                act.activation(gates[:], gates[:], ACT.Tanh).then_inc(s_gates, 1)
                act.activation(a_neg[:], pch[:, :, PC_ALOG:], ACT.Exp).then_inc(s_aneg, 1)
                act.wait_ge(s_aneg, 1)
                act.activation(a_neg[:], a_neg[:], ACT.Copy, scale=-1.0).then_inc(s_aneg, 1)
                act.wait_ge(s_aneg, 2)
                act.wait_ge(s_gates, 1)

            def square(i, cs):
                junk = (w1q if i == 0 else w2q)[:].rearrange("p a b -> p (a b)")
                for c in cs:
                    act.wait_ge(s_stage2[c] if i else s_stage, 16)
                    act.activation(junk[:, c * FF:(c + 1) * FF], stage[:, c * FF:(c + 1) * FF], ACT.Square,
                                   accum_out=wsum[:, i, c:c + 1]).then_inc(s_wsq, 1)

            def mean(i):
                act.wait_ge(s_wmean, i + 1)
                act.activation(wstat[:, i, 0:1], banks[3][:, i:i + 1], ACT.Copy, scale=1.0 / (FF * D)).then_inc(s_wms, 1)

            def scale(i, cs):
                act.wait_ge(s_wstat, i + 1)
                for c in cs:
                    w = stage[:, c * FF:(c + 1) * FF]
                    act.activation(w, w, ACT.Identity, scale=wstat[:, i, 1:2],
                                   bias=expo[:, 2:3]).then_inc(s_wscaled, 1)

            def quantise(i, cs):
                dst = (w1q if i == 0 else w2q)[:].rearrange("p a b -> p (a b)")
                for c in cs:
                    act.wait_ge(s_wclip, 4 * i + c + 1)
                    act.activation(dst[:, c * FF:(c + 1) * FF], stage[:, c * FF:(c + 1) * FF], ACT.Copy,
                                   bias=-MAGIC).then_inc(s_wq, 1)

            act.wait_ge(s_first, first_wait)
            pass_(None, True, rest=False)
            with act.Fori(0, B - 1) as i:
                pass_(i, True)
            pass_(B - 1, False)

        @block.vector
        def _(dve):
            def half_step(b, prev, n, p):
                s = 2 * n + p
                js = slice(p * HALF, (p + 1) * HALF)
                w3 = work[:, s % SCANBUFS, :, :]
                flat = w3.rearrange("p a l -> p (a l)")
                if p == 0:
                    dve.wait_ge(s_bcc, b * 2 * NS + 2 * n + 1)
                    if s >= SCANBUFS and prev is None:
                        dve.wait_ge(s_sum, (s - SCANBUFS + 1) // 2)
                    elif s >= SCANBUFS:
                        dve.wait_ge(s_acc, b * HN + s - SCANBUFS + 1)
                    dve.tensor_tensor(w3, du[:, js, :], bcast[:, n % 2, :].unsqueeze(1).broadcast_to([P, HALF, L]),
                                      ALU.mult).then_inc(s_dbu, 1)
                    dve.wait_ge(s_dbu, b * NS + n + 1)
                else:
                    dve.wait_ge(s_dbuP, b * NS + n + 1)
                dve.wait_ge(s_decay, b * HN + s + 1)
                dve.tensor_tensor_scan(flat, decay[:, s % DECAYBUFS, :, :].rearrange("p a l -> p (a l)"), flat, 0.0,
                                       ALU.mult, ALU.add).then_inc(s_scan, 1)
                dve.wait_ge(s_scan, b * HN + s + 1)
                dve.wait_ge(s_bcc, b * 2 * NS + 2 * n + 2)
                dve.tensor_tensor(w3, w3, ccast[:, n % 2, :].unsqueeze(1).broadcast_to([P, HALF, L]),
                                  ALU.mult).then_inc(s_hc, 1)

            def convolve(b, j):
                if j == 0:
                    dve_p.start()
                dve.wait_ge(s_inprojc, b * J + j + 1)
                for k in range(TAPS - 1):
                    ins = dve.scalar_tensor_tensor(u[:, j, :], xpad[:, j % 2, k:k + L], pch[:, j, k:k + 1],
                                                   u[:, j, :], ALU.mult, ALU.add)
                    if k < TAPS - 2:
                        dve_p.link(dve, b, ins)
                    else:
                        ins.then_inc(s_conv, 1)

            def split(b):
                dve.wait_ge(s_xd, b + 1)
                tmp = x1n
                dve_p.link(dve, b, dve.tensor_tensor(tmp, xd[:], xd3[:], ALU.subtract))
                dve_p.link(dve, b, dve.tensor_copy(xd3[64:128, :], tmp[64:128, :]))
                dve_p.link(dve, b, dve.tensor_tensor(tmp[96:128, :], tmp[96:128, :], xd3[96:128, :], ALU.subtract))
                dve.tensor_copy(xd3[96:128, :], tmp[96:128, :]).then_inc(s_split, 1)

            def softplus_max(b):
                for j in range(J):
                    dve.wait_ge(s_spabs, b * J + j + 1)
                    dve.tensor_scalar(dt[:, j, :], banks[DT_BANKS[j]][:], pch[:, j, PC_DTB:PC_DTB + 1], 0.0,
                                      ALU.add, ALU.max).then_inc(s_spmax, 1)

            def softplus_tmp(b):
                for p in range(2):
                    dve.wait_ge(s_spexp, b * 2 + p + 1)
                    dve.tensor_scalar(sptmp[p], work[:, p, :, :], 1.0, -1.0, ALU.add, ALU.add).then_inc(s_sptmp, 1)

            def softplus_sum(b, p):
                js = slice(p * HALF, (p + 1) * HALF)
                dve.wait_ge(s_log, b * 2 + p + 1)
                dve.wait_ge(s_spln, b * 2 + p + 1)
                dve_p.link(dve, b, dve.tensor_tensor(sptmp[p], sptmp[p], du[:, js, :], ALU.add))
                dve.tensor_tensor(dt[:, js, :], dt[:, js, :], sptmp[p], ALU.add).then_inc(s_dt, 1)
                dve.wait_ge(s_dt, b * 2 + p + 1)
                dve.tensor_tensor(du[:, js, :], dt[:, js, :], u[:, js, :], ALU.mult).then_inc(s_du, 1)

            def weight_low(f):
                dve.wait_ge(s_whigh, f + 1)
                if f == 0:
                    dve.wait_ge(s_acc, B * HN)
                dve.tensor_tensor(in_parts(w_low[:, f % 3, :]), ring[:, f % RING, :], w_high[:, f % 3, :],
                                  ALU.subtract).then_inc(s_wlow, 1)

            def tail(b):
                for t in range(T):
                    ts = slice(t * P, (t + 1) * P)
                    dve.wait_ge(s_xnTc, b * 2 * T + T + t + 1)
                    dve.tensor_tensor(in_parts(x_low[:, :, ts]), xnT[:, :, ts], x_high[:, :, ts],
                                      ALU.subtract).then_inc(s_xlow, 1)
                for f in range(FT):
                    dve.wait_ge(s_hhigh, f + 1)
                    dve.tensor_tensor(in_parts(h_low[:, f % 2, :]), h_full[:, f % 2, :], h_high[:, f % 2, :],
                                      ALU.subtract).then_inc(s_hlow, 1)
                    if f + 2 < FT:
                        weight_low(f + 2)

            def middle(b, m, scans, rest):
                if not rest:
                    gate_bias()
                if rest:
                    h_scale(b, 2)
                    norm_apply(b, 0)
                    h_quant(b, 2)
                    second(b, 1)
                    h_scale(b, 3)
                if scans:
                    split(m)
                if rest:
                    norm_apply(b, 1)
                    h_quant(b, 3)
                    second(b, 2)
                if scans:
                    softplus_max(m)
                if not scans:
                    weight_low(0)
                    weight_low(1)
                if rest:
                    norm_apply(b, 2)
                if scans:
                    softplus_tmp(m)
                if rest:
                    second(b, 3)
                    third(b, 0)
                    norm_apply(b, 3)
                if scans:
                    softplus_sum(m, 0)
                if rest:
                    norm_apply(b, 4)
                    third(b, 1)
                if scans:
                    softplus_sum(m, 1)

            def half(b, prev, slot, which, p):
                if state_at(slot, which) is not None:
                    half_step(b, prev, state_at(slot, which), p)

            def energy_max(b, slot):
                if slot in ATT_SLOTS:
                    j = ATT_SLOTS[slot]
                    dve.wait_ge(s_emm, b * J + j + 1)
                    dve.tensor_reduce(ast[:, j, 0:1], banks[1][:], AX.X, ALU.max, negate=True).then_inc(s_emax, 1)

            def mixer_last(b, prev, slot):
                if slot == ZSTAT_SLOT:
                    dve.wait_ge(s_x, b * 16 + 16)
                    for j in range(J):
                        dve_m.link(dve, b, dve.bn_stats(zst[:, j, 0:6], xres[:, j, :]))
                        carry_wait(dve, "dve")
                        dve.bn_aggr(zst[:, j, 6:8], zst[:, j, 0:6]).then_inc(s_zst, 1)
                if slot in ATT_SLOTS:
                    att_probs(b, slot)
                if slot == GATE_SLOT:
                    for p in range(2):
                        js = slice(p * HALF, (p + 1) * HALF)
                        dve.wait_ge(s_zs, b * J + (p + 1) * HALF)
                        if prev is not None:
                            dve.wait_ge(s_acc, b * HN + HN - 1 + p)
                        elif p:
                            weights(slot)
                            dve.wait_ge(s_sum, NS)
                            dve.wait_ge(s_accin, J)
                        else:
                            dve.wait_ge(s_acc, NS)
                        if prev is None and p:
                            for q in range(HALF):
                                dve_w.link(dve, 0, dve.tensor_tensor(u[:, HALF + q, :], u[:, HALF + q, :],
                                                                     banks[SUM_BANKS[q]][:], ALU.add))
                        dve.tensor_tensor(u[:, js, :], u[:, js, :], zs[p][:, :, :], ALU.mult).then_inc(s_y, 1)
                    for t in range(T):
                        first_sum(b, t)
                        if t == T - 2:
                            quantise(b, 0)
                if slot == QUANT_SLOT:
                    for t in range(1, T):
                        quantise(b, t)

            def first_sum(b, t):
                dve.wait_ge(s_yT, b * T + t + 1)
                dve.scalar_tensor_tensor(xres[:, t, :], banks[(t + 1) % 2][:], gates[:, 0:1], xres[:, t, :],
                                         ALU.mult, ALU.add).then_inc(s_x1, 1)
                dve.wait_ge(s_x1, b * T + t + 1)
                dve_m.link(dve, b, dve.bn_stats(mst[:, t, 0:6], xres[:, t, :]))
                carry_wait(dve, "dve")
                dve.bn_aggr(mst[:, t, 6:8], mst[:, t, 0:6]).then_inc(s_x1st, 1)

            def quantise(b, t):
                st = mst[:, t, :]
                dve.wait_ge(s_x1rs, b * T + t + 1)
                if t:
                    dve.wait_ge(s_q1, b * T + t)
                dve_m.link(dve, b, dve.tensor_scalar(x1n, xres[:, t, :], st[:, 6:7], st[:, 9:10],
                                                     ALU.subtract, ALU.mult))
                dve_m.link(dve, b, dve.tensor_reduce(st[:, 10:11], x1n, AX.X, ALU.max, apply_absolute_value=True))
                dve_m.link(dve, b, dve.tensor_scalar(st[:, 11:12], st[:, 10:11], Q_EPS, 1.0 / 127.0,
                                                     ALU.max, ALU.mult))
                dve_m.link(dve, b, dve.reciprocal(st[:, 12:13], st[:, 11:12]))
                dve.tensor_scalar(st[:, 13:14], st[:, 11:12], wstat[:, 0, 2:3], None, ALU.mult)
                dve_m.link(dve, b, dve.tensor_scalar(x1n, x1n, st[:, 12:13], MAGIC, ALU.mult, ALU.add))
                if t >= 2:
                    dve.wait_ge(s_q1T, b * T + t - 1)
                dve.tensor_scalar(q1[:, t % 2, :], x1n, MAGIC, 127.0, ALU.subtract, ALU.min).then_inc(s_q1, 1)

            def att_probs(b, slot):
                j = ATT_SLOTS[slot]
                dve.wait_ge(s_eexp, b * J + j + 1)
                dve_m.link(dve, b, dve.reciprocal(ast[:, j, 2:3], ast[:, j, 1:2]))
                dve.tensor_scalar(ex[:], ex[:], ast[:, j, 2:3], None, ALU.mult).then_inc(s_eprob, 1)

            def norm(b, i):
                t = i % T
                st = fst[:, t, 8:18]
                dve_f.link(dve, b, dve.bn_stats(st[:, 0:6], xb[:, t, :]))
                carry_wait(dve, "dve")
                dve.bn_aggr(st[:, 6:8], st[:, 0:6]).then_inc(s_lnst, 1)

            def norm_apply(b, i):
                t = i % T
                st = fst[:, t, 8:18]
                dve.wait_ge(s_lnrs, b * 2 * T + i + 1)
                if i >= 2:
                    dve.wait_ge(s_xnT, b * 2 * T + i - 1)
                dve.tensor_scalar(xn[:, i % 2, :], xb[:, t, :], st[:, 6:7], st[:, 9:10],
                                  ALU.subtract, ALU.mult).then_inc(s_xn, 1)

            def h_scale(b, t):
                st = fst[:, t, :]
                dve.wait_ge(s_gelu, b * T * FC + (t + 1) * FC)
                dve_f.link(dve, b, dve.tensor_reduce(st[:, 0:1], h[t % 2], AX.X, ALU.max, apply_absolute_value=True))
                dve_f.link(dve, b, dve.tensor_scalar(st[:, 1:2], st[:, 0:1], Q_EPS, 1.0 / 127.0, ALU.max, ALU.mult))
                dve.reciprocal(st[:, 2:3], st[:, 1:2]).then_inc(s_hsc, 1)

            def h_quant(b, t):
                dve.wait_ge(s_hr, b * T + t + 1)
                if t:
                    dve.wait_ge(s_hqT, b * 2 * T + 2 * t)
                dve.tensor_scalar(hq[:], h[t % 2], MAGIC, 127.0, ALU.subtract, ALU.min).then_inc(s_hq, 1)

            def second(b, t):
                st = fst[:, t, :]
                dve_f.link(dve, b, dve.tensor_scalar(st[:, 4:5], st[:, 1:2], wstat[:, 1, 3:4], None, ALU.mult))
                dve.wait_ge(s_mm2, b * T + t + 1)
                if t == 0:
                    dve.wait_ge(s_stored, b + 1)
                dve.scalar_tensor_tensor(xb[:, t, :], banks[7][:], st[:, 4:5], xres[:, t, :],
                                         ALU.mult, ALU.add).then_inc(s_x2, 1)
                dve.wait_ge(s_x2, b * T + t + 1)
                norm(b, t)

            def third(b, t):
                dve.wait_ge(s_xm, b * T + t + 1)
                dve.scalar_tensor_tensor(xb[:, t, :], banks[4 + t][:], gates[:, 1:2], xb[:, t, :],
                                         ALU.mult, ALU.add).then_inc(s_x3, 1)
                dve.wait_ge(s_x3, b * T + t + 1)
                norm(b, T + t)

            def fourth(b):
                dve.wait_ge(s_fmm2, b * FT + FT)
                dve.wait_ge(s_x3b, b * T + T)
                for t in range(T):
                    dve.scalar_tensor_tensor(xb[:, t, :], banks[4 + t][:], gates[:, 3:4], xb[:, t, :],
                                             ALU.mult, ALU.add).then_inc(s_x4, 1)

            dve.memset(ones[:], 1.0).then_inc(s_ones, 1)
            dve.memset(xpad[:, :, 0:PAD], 0.0).then_inc(s_pad, 1)
            dve.sem_inc(s_x4, 1)
            dve.memset(decay[:, :, :, 0:1], 0.0).then_inc(s_pad, 1)
            dve.wait_ge(s_pad, 2)
            dve.wait_ge(s_first, first_wait)

            def gate_bias():
                dve.wait_ge(s_const, const_wait)
                dve.wait_ge(s_gates, 1)
                dve.tensor_scalar(b2[:], b2[:], gates[:, 3:4], None, ALU.mult).then_inc(s_b2, 1)

            def weight_clip(i, c):
                w = stage[:, c * FF:(c + 1) * FF]
                dve.wait_ge(s_wscaled, 4 * i + c + 1)
                dve.tensor_scalar(w, w, MAGIC - 1.0, MAGIC + 1.0, ALU.max, ALU.min).then_inc(s_wclip, 1)

            def weights(slot):
                if slot in W_ROUND:
                    i, cs = W_ROUND[slot]
                    for c in cs:
                        weight_clip(i, c)

            def pass_(b, scans, rest=True):
                m, prev = (b + 1, b) if rest else (0, None)
                if rest:
                    dve_f.start()
                if scans:
                    dve_m.start()
                for slot in range(SLOTS if scans else 5):
                    if slot == 3:
                        middle(b, m, scans, rest)
                    if rest:
                        if slot < 2:
                            h_scale(b, slot)
                        if slot == 4:
                            norm_apply(b, 5)
                            third(b, 2)
                            third(b, 3)
                    if scans:
                        if slot == 0:
                            convolve(m, 0)
                        if slot == 1:
                            convolve(m, 2)
                        half(m, prev, slot, 0, 0)
                    if rest:
                        if slot < 2:
                            h_quant(b, slot)
                        if slot == 1:
                            second(b, 0)
                        if slot == 4:
                            norm_apply(b, 6)
                            norm_apply(b, 7)
                    elif slot != GATE_SLOT:
                        weights(slot)
                    if scans:
                        if slot == 0:
                            convolve(m, 1)
                        if slot == 1:
                            convolve(m, 3)
                        half(m, prev, slot, 0, 1)
                        energy_max(m, slot)
                    if scans:
                        half(m, prev, slot, 1, 0)
                        half(m, prev, slot, 1, 1)
                        mixer_last(m, prev, slot)
                    if rest and slot == SLOTS - 1:
                        fourth(b)
                if not scans:
                    tail(b)
                    fourth(b)

            pass_(None, True, rest=False)
            with dve.Fori(0, B - 1) as i:
                pass_(i, True)
            pass_(B - 1, False)

        @block.gpsimd
        def _(pool):
            def softplus_log(b):
                for p in range(2):
                    pool.wait_ge(s_sptmp, b * 2 + p + 1)
                    pool.tensor_tensor(sptmp[p], work[:, p, :, :], sptmp[p], ALU.subtract).then_inc(s_log, 1)

            def start_sum(b, prev):
                for j in range(J):
                    if j % HALF == 0:
                        pool.wait_ge(s_du, b * 2 + j // HALF + 1)
                    carry_wait(pool, "pool")
                    pool.tensor_scalar(u[:, j, :], u[:, j, :], pch[:, j, PC_D:PC_D + 1], 1.0,
                                       ALU.mult, ALU.mult).then_inc(s_accin, 1)
                pool.wait_ge(s_accin, b * J + J)
                state_input(b, prev, 0)

            def middle(b, m, prev, scans, rest):
                if rest:
                    h_round(b, 2)
                    norm(b, 1)
                    h_round(b, 3)
                    norm(b, 2)
                if scans:
                    softplus_log(m)
                if rest:
                    norm(b, 3)
                    norm(b, 4)
                    norm(b, 5)
                if scans:
                    start_sum(m, prev)

            def rsqrt(tally, b, tmp, var, eps, out, last=None):
                carry_wait(pool, "pool")
                tally.link(pool, b, pool.tensor_scalar(tmp, var, eps, 1.0, ALU.add, ALU.mult))
                ins = pool.tensor_tensor(out, tmp, expo[:, 0:1], ALU.pow)
                if last is None:
                    tally.link(pool, b, ins)
                else:
                    ins.then_inc(last, 1)

            def state_input(b, prev, n):
                s = 2 * n + 1
                pool.wait_ge(s_bcc, b * 2 * NS + 2 * n + 1)
                if s >= SCANBUFS:
                    pool.wait_ge(s_acc, n if prev is None else b * HN + s - SCANBUFS + 1)
                pool.tensor_tensor(work[:, s % SCANBUFS, :, :], du[:, HALF:, :],
                                   bcast[:, n % 2, :].unsqueeze(1).broadcast_to([P, HALF, L]), ALU.mult)\
                    .then_inc(s_dbuP, 1)

            def accumulate(b, prev, n, p):
                s = 2 * n + p
                js = slice(p * HALF, (p + 1) * HALF)
                if prev is None and p:
                    if n == NS - 1:
                        pool.wait_ge(s_sum, NS)
                        pool.wait_ge(s_y, 1)
                        pool.sem_inc(s_acc, NS)
                    return
                pool.wait_ge(s_hc, b * HN + s + 1)
                if n:
                    pool.wait_ge(s_acc, n if prev is None else b * HN + s - 1)
                pool.tensor_tensor(u[:, js, :], u[:, js, :], work[:, s % SCANBUFS, :, :], ALU.add).then_inc(s_acc, 1)

            def half(b, prev, slot, which, p):
                n = state_at(slot, which)
                if n is not None:
                    accumulate(b, prev, n, p)
                    if p == 0 and n + 1 < NS:
                        state_input(b, prev, n + 1)

            def mixer_last(b, slot):
                if slot == ZSTAT_SLOT:
                    for j in range(J):
                        st = zst[:, j, :]
                        pool.wait_ge(s_zst, b * J + j + 1)
                        rsqrt(pool_m, b, st[:, 8:9], st[:, 7:8], LN_EPS, st[:, 9:10])
                        carry_wait(pool, "pool")
                        pool.tensor_scalar(st[:, 10:11], st[:, 6:7], st[:, 9:10], -1.0, ALU.mult,
                                           ALU.mult).then_inc(s_zrs, 1)
                if slot == GATE_SLOT:
                    for t in range(T):
                        st = mst[:, t, :]
                        pool.wait_ge(s_x1st, b * T + t + 1)
                        rsqrt(pool_m, b, st[:, 8:9], st[:, 7:8], LN_EPS, st[:, 9:10], s_x1rs)

            def norm(b, i):
                st = fst[:, i % T, 8:18]
                pool.wait_ge(s_lnst, b * 2 * T + i + 1)
                rsqrt(pool_f, b, st[:, 8:9], st[:, 7:8], LN_EPS, st[:, 9:10], s_lnrs)

            def h_round(b, t):
                pool.wait_ge(s_hsc, b * T + t + 1)
                carry_wait(pool, "pool")
                pool.tensor_scalar(h[t % 2], h[t % 2], fst[:, t, 2:3], MAGIC, ALU.mult, ALU.add).then_inc(s_hr, 1)

            def bias(b, t):
                pool.wait_ge(s_xn, b * 2 * T + T + t + 1)
                if t == 0:
                    pool.wait_ge(s_b2, 1)
                pool.tensor_tensor(xb[:, t, :], xb[:, t, :], b2[:], ALU.add).then_inc(s_x3b, 1)

            pool.memset(expo[:, 0:1], -0.5).then_inc(pool_s.sem, 1)
            pool.memset(expo[:, 2:3], MAGIC)
            pool.memset(expo[:, 1:2], 0.5).then_inc(s_ones, 1)
            pool.wait_ge(pool_s.sem, 1)
            pool.wait_ge(s_ones, 2)
            pool_s.n = 1
            pool.wait_ge(s_const, const_wait)

            def weight_rms(i):
                st = wstat[:, i, :]
                pool.wait_ge(s_wms, i + 1)
                carry_wait(pool, "pool")
                pool_s.link(pool, 0, pool.tensor_scalar(st[:, 0:1], st[:, 0:1], Q_EPS, 1.0, ALU.max, ALU.mult))
                pool_s.link(pool, 0, pool.tensor_tensor(st[:, 1:2], st[:, 0:1], expo[:, 0:1], ALU.pow))
                pool_s.link(pool, 0, pool.tensor_tensor(st[:, 2:3], st[:, 0:1], expo[:, 1:2], ALU.pow))
                if i == 0:
                    pool.sem_inc(s_wstat, 1)
                else:
                    pool.wait_ge(s_gates, 1)
                    carry_wait(pool, "pool")
                    pool.tensor_scalar(st[:, 3:4], st[:, 2:3], 1.0, gates[:, 2:3], ALU.mult, ALU.mult)\
                        .then_inc(s_wstat, 1)

            def weights(slot):
                if slot in W_MEAN:
                    weight_rms(W_MEAN[slot])

            def pass_(b, scans, rest=True):
                m, prev = (b + 1, b) if rest else (0, None)
                if rest:
                    pool_f.start()
                if scans:
                    pool_m.start()
                for slot in range(SLOTS):
                    if slot == 3:
                        middle(b, m, prev, scans, rest)
                    if rest:
                        if slot < 2:
                            h_round(b, slot)
                        if slot == 4:
                            norm(b, 6)
                            norm(b, 7)
                        if slot == 5:
                            bias(b, 2)
                    else:
                        weights(slot)
                    if scans:
                        half(m, prev, slot, 0, 0)
                    if rest:
                        if slot == 1:
                            norm(b, 0)
                        if slot == 4:
                            bias(b, 0)
                        if slot == 5:
                            bias(b, 3)
                    if scans:
                        half(m, prev, slot, 0, 1)
                    if rest:
                        if slot == 4:
                            bias(b, 1)
                    if scans:
                        half(m, prev, slot, 1, 0)
                        half(m, prev, slot, 1, 1)
                        mixer_last(m, slot)

            pass_(None, True, rest=False)
            with pool.Fori(0, B - 1) as i:
                pass_(i, True)
            pass_(B - 1, False)


def kernel(x, ctx_1024, g_xattn, g_ffn, L0_xattn_in_proj_w, L0_xattn_conv_w, L0_xattn_conv_b, L0_xattn_x_proj_w,
           L0_xattn_dt_proj_w, L0_xattn_dt_proj_b, L0_xattn_A_log, L0_xattn_D, L0_ffn_w1, L0_ffn_w2, L1_xattn_Wq,
           L1_xattn_bq, L1_xattn_Wk, L1_xattn_bk, L1_ffn_proj1, L1_ffn_proj1_bias, L1_ffn_proj2, L1_ffn_proj2_bias,
           L1_ffn_gate_w):
    import ml_dtypes

    import concourse.bacc as bacc
    from concourse.bass_utils import run_bass_kernel_spmd

    g_x, g_f = np.asarray(g_xattn), np.asarray(g_ffn)
    xp = np.asarray(L0_xattn_x_proj_w)
    rank, rest = xp[:R].T, xp[R:].T
    p1, p2 = np.asarray(L1_ffn_proj1), np.asarray(L1_ffn_proj2)
    up = p1.reshape(FT, P, J, P).transpose(0, 3, 2, 1).reshape(FT, P, D)
    down = p2.reshape(D, FT, P).transpose(1, 2, 0)
    identity = np.eye(P, dtype=np.float32)
    part = np.arange(P)[:, None]
    pick = ((part % (2 * NS) == np.arange(2 * NS)[None, :]) & (part >= 2 * NS)).astype(ml_dtypes.bfloat16)
    arrays = {
        "x": x,
        "ctxT": np.asarray(ctx_1024).transpose(0, 2, 1),
        "in_proj": np.asarray(L0_xattn_in_proj_w).T,
        "x_proj": np.concatenate([rank, rank, rest, rest, rest], axis=1),
        "dt_proj": np.asarray(L0_xattn_dt_proj_w).T,
        "channels": np.concatenate([np.asarray(L0_xattn_conv_w)[:, 0, :], np.asarray(L0_xattn_conv_b)[:, None],
                                    np.asarray(L0_xattn_dt_proj_b)[:, None], np.asarray(L0_xattn_D)[:, None],
                                    np.asarray(L0_xattn_A_log)], axis=1),
        "w1": np.asarray(L0_ffn_w1).T,
        "w2": np.asarray(L0_ffn_w2).T,
        "wqk": np.stack([np.asarray(L1_xattn_Wq).T, np.asarray(L1_xattn_Wk).T]),
        "bqk": np.stack([np.asarray(L1_xattn_bq), np.asarray(L1_xattn_bk)], axis=1),
        "ffn": np.concatenate([up, down], axis=2),
        "b1": np.asarray(L1_ffn_proj1_bias).reshape(FT, P).T,
        "b2": np.broadcast_to(np.asarray(L1_ffn_proj2_bias), (P, D)),
        "gates": np.broadcast_to(np.stack([g_x[0], g_x[1], g_f[0], g_f[1]]), (P, 4)),
        "ident": identity,
        "identb": identity.astype(ml_dtypes.bfloat16),
        "pick": pick,
    }
    arrays = {f"{name}_dram": np.ascontiguousarray(a) for name, a in arrays.items()}
    nc = bacc.Bacc("TRN2", target_bir_lowering=False, num_devices=1)
    args = [nc.dram_tensor(name, a.shape, mybir.dt.from_np(a.dtype), kind="ExternalInput").ap()
            for name, a in arrays.items()]
    out = nc.dram_tensor("out_dram", (B, L, D), F32, kind="ExternalOutput").ap()
    program(nc, *args, out)
    got = run_bass_kernel_spmd(nc, [arrays], core_ids=[0])
    return got.results[0]["out_dram"]
```
